# Optimizing a Trainium2 kernel written in Bass

```python
import numpy as np
import jax
import jax.numpy as jnp

def _softmax(x, axis=-1):
    return jax.nn.softmax(x, axis=axis)

def _gelu(x):
    return jax.nn.gelu(x, approximate=True)

def _silu(x):
    return jax.nn.silu(x)

def _sigmoid(x):
    return jax.nn.sigmoid(x)

def _layernorm(x, axis=-1, eps=1e-05):
    m = jnp.mean(x, axis=axis, keepdims=True)
    v = jnp.var(x, axis=axis, keepdims=True)
    return (x - m) / jnp.sqrt(v + eps)

def _scatter_add(tgt, idx, src, axis=0):
    return tgt.at[idx].add(src)

def _segment_sum(src, seg, n):
    return jax.ops.segment_sum(src, seg, n)
kernel_name = 'mk_adaln_attn_ffn_d1_seqx_r4_fd2ace'

def setup_inputs(seed: int=0):
    np.random.seed(seed)
    _w = jnp.asarray

    def _rec_inputs():
        import jax
        import jax.numpy as jnp
        _rk = jax.random.key(seed)
        x = -0.0002928 + 1 * jax.random.normal(jax.random.fold_in(_rk, 1), (2, 1024, 256), jnp.float32)
        _lenS = 1024 - jax.random.randint(jax.random.fold_in(_rk, 7), (2,), 0, max(1, 1024 // 4) + 1, jnp.int32)
        _lenS2 = 1024 - jax.random.randint(jax.random.fold_in(_rk, 8), (2,), 0, max(1, 1024 // 4) + 1, jnp.int32)
        cond_1024 = 0.000887014 + 1.03683 * jax.random.normal(jax.random.fold_in(_rk, 11), (2, 256), jnp.float32)
        return (x, cond_1024)
    x, cond_1024 = _rec_inputs()

    def _L0_cond_setup():
        import jax, jax.numpy as jnp
        import numpy as np
        TOP_K = 2
        N_EXPERTS = 8
        N_SHARED = 1
        EPS = 1e-09
        key = jax.random.key(seed)
        ks = jax.random.split(key, 10)
        B, T, d = (2, 512, 256)
        h_s, h_r, E = (512, 128, N_EXPERTS)
        return {'x': jax.random.normal(ks[0], (B, T, d), jnp.float32), 't_emb': jax.random.normal(ks[1], (B, d), jnp.float32), 'router_w': jax.random.normal(ks[2], (E, d), jnp.float32) * 0.01, 'router_t_w': jax.random.normal(ks[3], (E, d), jnp.float32) * 0.01, 'router_bias': jnp.zeros((E,), jnp.float32), 'sw1': jax.random.normal(ks[4], (h_s, d), jnp.float32) * 0.02, 'sw3': jax.random.normal(ks[5], (h_s, d), jnp.float32) * 0.02, 'sw2': jax.random.normal(ks[6], (d, h_s), jnp.float32) * 0.02, 'rw1': jax.random.normal(ks[7], (E, h_r, d), jnp.float32) * 0.02, 'rw2': jax.random.normal(ks[8], (E, d, h_r), jnp.float32) * 0.02}
    _L0_cond_all = _L0_cond_setup()
    _L0_cond_in = {k: v for k, v in _L0_cond_all.items() if k in ('router_w', 'router_t_w', 'router_bias', 'sw1', 'sw3', 'sw2', 'rw1', 'rw2')}
    del _L0_cond_all

    def _L0_attn_setup():
        import jax, jax.numpy as jnp
        from jax import lax
        import numpy as np
        D_MODEL = 256
        D_STATE = 16
        D_CONV = 4
        EXPAND = 2
        D_INNER = EXPAND * D_MODEL
        DT_RANK = D_MODEL // 16
        BATCH = 4
        SEQ = 256

        def _mamba(x, inproj, conv_w, conv_b, xproj, dt_w, dt_b, Alog, Dp, outproj):
            B, L, _ = x.shape
            xz = x @ inproj
            u, z = jnp.split(xz, 2, axis=-1)
            K = conv_w.shape[1]
            up = jnp.pad(u, ((0, 0), (K - 1, 0), (0, 0)))
            uc = conv_b
            for k in range(K):
                uc = uc + up[:, k:k + L, :] * conv_w[:, k]
            uc = jax.nn.silu(uc)
            dbl = uc @ xproj
            N = Alog.shape[1]
            dt, Bm, Cm = jnp.split(dbl, [DT_RANK, DT_RANK + N], axis=-1)
            delta = jax.nn.softplus(dt @ dt_w + dt_b)
            A = -jnp.exp(Alog)

            def step(h, inp):
                u_t, d_t, B_t, C_t = inp
                dA = jnp.exp(d_t[..., None] * A)
                h = dA * h + (d_t * u_t)[..., None] * B_t[:, None, :]
                y_t = jnp.einsum('bdn,bn->bd', h, C_t)
                return (h, y_t)
            h0 = jnp.zeros((B, uc.shape[-1], N), x.dtype)
            xs = (uc.transpose(1, 0, 2), delta.transpose(1, 0, 2), Bm.transpose(1, 0, 2), Cm.transpose(1, 0, 2))
            _, ys = lax.scan(step, h0, xs)
            y = ys.transpose(1, 0, 2) + uc * Dp
            y = y * jax.nn.silu(z)
            return y @ outproj
        key = jax.random.key(seed)
        ks = iter(jax.random.split(key, 40))

        def w(shape, s=0.02):
            return (s * jax.random.normal(next(ks), shape)).astype(jnp.float32)
        inp = {'x': jax.random.normal(next(ks), (BATCH, SEQ, D_MODEL), dtype=jnp.float32)}
        Alog = jnp.log(jnp.tile(jnp.arange(1, D_STATE + 1, dtype=jnp.float32), (D_INNER, 1)))
        for s in ('f', 'b'):
            inp[f'inproj_{s}'] = w((D_MODEL, 2 * D_INNER))
            inp[f'conv_w_{s}'] = w((D_INNER, D_CONV), 0.2)
            inp[f'conv_b_{s}'] = jnp.zeros((D_INNER,), jnp.float32)
            inp[f'xproj_{s}'] = w((D_INNER, DT_RANK + 2 * D_STATE))
            inp[f'dt_w_{s}'] = w((DT_RANK, D_INNER))
            inp[f'dt_b_{s}'] = jnp.full((D_INNER,), -4.0, jnp.float32)
            inp[f'Alog_{s}'] = Alog
            inp[f'Dp_{s}'] = jnp.ones((D_INNER,), jnp.float32)
            inp[f'outproj_{s}'] = w((D_INNER, D_MODEL))
        inp['gate_w'] = w((2 * D_MODEL, D_MODEL))
        inp['gate_b'] = jnp.zeros((D_MODEL,), jnp.float32)
        inp['proj_w'] = w((D_MODEL, D_MODEL))
        inp['proj_b'] = jnp.zeros((D_MODEL,), jnp.float32)
        return inp
    _L0_attn_all = _L0_attn_setup()
    _L0_attn_in = {k: v for k, v in _L0_attn_all.items() if k in ('inproj_f', 'conv_w_f', 'conv_b_f', 'xproj_f', 'dt_w_f', 'dt_b_f', 'Alog_f', 'Dp_f', 'outproj_f', 'inproj_b', 'conv_w_b', 'conv_b_b', 'xproj_b', 'dt_w_b', 'dt_b_b', 'Alog_b', 'Dp_b', 'outproj_b', 'gate_w', 'gate_b', 'proj_w', 'proj_b')}
    del _L0_attn_all

    def _L0_cond2_setup():
        import jax, jax.numpy as jnp
        import numpy as np
        TEMPERATURE = 2.0
        key = jax.random.key(seed)
        k1, k2 = jax.random.split(key)
        B, N, D = (16, 512, 256)
        x = jax.random.normal(k1, (B, N, D), dtype=jnp.float32)
        random_values = jax.random.uniform(k2, (B, D), dtype=jnp.float32)
        return {'x': x, 'random_values': random_values}
    _L0_cond2_all = _L0_cond2_setup()
    _L0_cond2_in = {k: v for k, v in _L0_cond2_all.items() if k in ()}
    del _L0_cond2_all

    def _L0_ffn_setup():
        import jax, jax.numpy as jnp
        import numpy as np
        B, M, D = (4, 512, 256)
        N, P = (64, 32)
        key = jax.random.key(seed)
        k1, k2, k3, k4 = jax.random.split(key, 4)
        x = jax.random.normal(k1, (B, M, D), dtype=jnp.float32)
        phi = jax.random.normal(k2, (D, N, P), dtype=jnp.float32) * (1.0 / np.sqrt(D))
        W = jax.random.normal(k3, (N, D, D), dtype=jnp.float32) * (1.0 / np.sqrt(D))
        b = jax.random.normal(k4, (N, D), dtype=jnp.float32) * 0.01
        return {'x': x, 'phi': phi, 'W': W, 'b': b}
    _L0_ffn_all = _L0_ffn_setup()
    _L0_ffn_in = {k: v for k, v in _L0_ffn_all.items() if k in ('phi', 'W', 'b')}
    del _L0_ffn_all
    return {'x': x, 'cond_1024': cond_1024, 'L0_cond_router_w': _L0_cond_in['router_w'], 'L0_cond_router_t_w': _L0_cond_in['router_t_w'], 'L0_cond_router_bias': _L0_cond_in['router_bias'], 'L0_cond_sw1': _L0_cond_in['sw1'], 'L0_cond_sw3': _L0_cond_in['sw3'], 'L0_cond_sw2': _L0_cond_in['sw2'], 'L0_cond_rw1': _L0_cond_in['rw1'], 'L0_cond_rw2': _L0_cond_in['rw2'], 'L0_attn_inproj_f': _L0_attn_in['inproj_f'], 'L0_attn_conv_w_f': _L0_attn_in['conv_w_f'], 'L0_attn_conv_b_f': _L0_attn_in['conv_b_f'], 'L0_attn_xproj_f': _L0_attn_in['xproj_f'], 'L0_attn_dt_w_f': _L0_attn_in['dt_w_f'], 'L0_attn_dt_b_f': _L0_attn_in['dt_b_f'], 'L0_attn_Alog_f': _L0_attn_in['Alog_f'], 'L0_attn_Dp_f': _L0_attn_in['Dp_f'], 'L0_attn_outproj_f': _L0_attn_in['outproj_f'], 'L0_attn_inproj_b': _L0_attn_in['inproj_b'], 'L0_attn_conv_w_b': _L0_attn_in['conv_w_b'], 'L0_attn_conv_b_b': _L0_attn_in['conv_b_b'], 'L0_attn_xproj_b': _L0_attn_in['xproj_b'], 'L0_attn_dt_w_b': _L0_attn_in['dt_w_b'], 'L0_attn_dt_b_b': _L0_attn_in['dt_b_b'], 'L0_attn_Alog_b': _L0_attn_in['Alog_b'], 'L0_attn_Dp_b': _L0_attn_in['Dp_b'], 'L0_attn_outproj_b': _L0_attn_in['outproj_b'], 'L0_attn_gate_w': _L0_attn_in['gate_w'], 'L0_attn_gate_b': _L0_attn_in['gate_b'], 'L0_attn_proj_w': _L0_attn_in['proj_w'], 'L0_attn_proj_b': _L0_attn_in['proj_b'], 'L0_ffn_phi': _L0_ffn_in['phi'], 'L0_ffn_W': _L0_ffn_in['W'], 'L0_ffn_b': _L0_ffn_in['b']}

def reference(x, cond_1024, L0_cond_router_w, L0_cond_router_t_w, L0_cond_router_bias, L0_cond_sw1, L0_cond_sw3, L0_cond_sw2, L0_cond_rw1, L0_cond_rw2, L0_attn_inproj_f, L0_attn_conv_w_f, L0_attn_conv_b_f, L0_attn_xproj_f, L0_attn_dt_w_f, L0_attn_dt_b_f, L0_attn_Alog_f, L0_attn_Dp_f, L0_attn_outproj_f, L0_attn_inproj_b, L0_attn_conv_w_b, L0_attn_conv_b_b, L0_attn_xproj_b, L0_attn_dt_w_b, L0_attn_dt_b_b, L0_attn_Alog_b, L0_attn_Dp_b, L0_attn_outproj_b, L0_attn_gate_w, L0_attn_gate_b, L0_attn_proj_w, L0_attn_proj_b, L0_ffn_phi, L0_ffn_W, L0_ffn_b):
    import jax
    import jax.numpy as jnp

    def _L0_cond_ref(x, t_emb, router_w, router_t_w, router_bias, sw1, sw3, sw2, rw1, rw2):
        import jax, jax.numpy as jnp
        import numpy as np
        TOP_K = 2
        N_EXPERTS = 8
        N_SHARED = 1
        EPS = 1e-09
        B, T, C = x.shape
        N = B * T
        x_flat = x.reshape(N, C)
        shared_out = jnp.einsum('nh,dh->nd', jax.nn.silu(x_flat @ sw1.T) * (x_flat @ sw3.T), sw2)
        t_bias = t_emb @ router_t_w.T
        t_bias_flat = jnp.broadcast_to(t_bias[:, None, :], (B, T, N_EXPERTS)).reshape(N, N_EXPERTS)
        s = jax.nn.sigmoid((x_flat @ router_w.T + t_bias_flat).astype(jnp.float32))
        sel_scores = s + router_bias
        _, topk_idx = jax.lax.top_k(sel_scores, TOP_K)
        s_sel = jnp.take_along_axis(s, topk_idx, axis=1)
        denom = jnp.sum(s_sel, axis=1, keepdims=True)
        gates = jnp.where(denom > EPS, s_sel / (denom + EPS), 1.0 / TOP_K).astype(x.dtype)
        combine = jnp.sum(gates[:, :, None] * jax.nn.one_hot(topk_idx, N_EXPERTS, dtype=x.dtype), axis=1)
        H = jax.nn.gelu(jnp.einsum('nd,ehd->enh', x_flat, rw1), approximate=False)
        O = jnp.einsum('enh,edh->end', H, rw2)
        routed_out = jnp.einsum('end,ne->nd', O, combine)
        out = (shared_out + routed_out) / (N_SHARED + TOP_K)
        return out.reshape(B, T, C)

    def _L0_attn_ref(x, inproj_f, conv_w_f, conv_b_f, xproj_f, dt_w_f, dt_b_f, Alog_f, Dp_f, outproj_f, inproj_b, conv_w_b, conv_b_b, xproj_b, dt_w_b, dt_b_b, Alog_b, Dp_b, outproj_b, gate_w, gate_b, proj_w, proj_b):
        import jax, jax.numpy as jnp
        from jax import lax
        import numpy as np
        D_MODEL = 256
        D_STATE = 16
        D_CONV = 4
        EXPAND = 2
        D_INNER = EXPAND * D_MODEL
        DT_RANK = D_MODEL // 16
        BATCH = 4
        SEQ = 256

        def _mamba(x, inproj, conv_w, conv_b, xproj, dt_w, dt_b, Alog, Dp, outproj):
            B, L, _ = x.shape
            xz = x @ inproj
            u, z = jnp.split(xz, 2, axis=-1)
            K = conv_w.shape[1]
            up = jnp.pad(u, ((0, 0), (K - 1, 0), (0, 0)))
            uc = conv_b
            for k in range(K):
                uc = uc + up[:, k:k + L, :] * conv_w[:, k]
            uc = jax.nn.silu(uc)
            dbl = uc @ xproj
            N = Alog.shape[1]
            dt, Bm, Cm = jnp.split(dbl, [DT_RANK, DT_RANK + N], axis=-1)
            delta = jax.nn.softplus(dt @ dt_w + dt_b)
            A = -jnp.exp(Alog)

            def step(h, inp):
                u_t, d_t, B_t, C_t = inp
                dA = jnp.exp(d_t[..., None] * A)
                h = dA * h + (d_t * u_t)[..., None] * B_t[:, None, :]
                y_t = jnp.einsum('bdn,bn->bd', h, C_t)
                return (h, y_t)
            h0 = jnp.zeros((B, uc.shape[-1], N), x.dtype)
            xs = (uc.transpose(1, 0, 2), delta.transpose(1, 0, 2), Bm.transpose(1, 0, 2), Cm.transpose(1, 0, 2))
            _, ys = lax.scan(step, h0, xs)
            y = ys.transpose(1, 0, 2) + uc * Dp
            y = y * jax.nn.silu(z)
            return y @ outproj
        y_f = _mamba(x, inproj_f, conv_w_f, conv_b_f, xproj_f, dt_w_f, dt_b_f, Alog_f, Dp_f, outproj_f)
        xb = jnp.flip(x, axis=1)
        y_b = _mamba(xb, inproj_b, conv_w_b, conv_b_b, xproj_b, dt_w_b, dt_b_b, Alog_b, Dp_b, outproj_b)
        y_b = jnp.flip(y_b, axis=1)
        g = jax.nn.sigmoid(jnp.concatenate([y_f, y_b], axis=-1) @ gate_w + gate_b)
        y = g * y_f + (1.0 - g) * y_b
        return y @ proj_w + proj_b

    def _L0_cond2_ref(x, random_values):
        import jax, jax.numpy as jnp
        import numpy as np
        TEMPERATURE = 2.0
        ax = jnp.abs(x)
        p = ax / jnp.sum(ax, axis=1, keepdims=True)
        pi = jnp.exp(p * TEMPERATURE)
        thresholds = pi / jnp.sum(pi, axis=1, keepdims=True)
        cum = jnp.cumsum(thresholds, axis=1) + 0.001
        rv = random_values[:, None, :]
        chosen_idx = jnp.sum(cum <= rv, axis=1, keepdims=True)
        gathered = jnp.take_along_axis(ax, chosen_idx, axis=1)
        mask = ax >= gathered
        return x * mask

    def _L0_ffn_ref(x, phi, W, b):
        import jax, jax.numpy as jnp
        import numpy as np
        B, M, D = (4, 512, 256)
        N, P = (64, 32)
        logits = jnp.einsum('bmd,dnp->bmnp', x, phi)
        dispatch = jax.nn.softmax(logits, axis=0)
        bsz, m, n, p = logits.shape
        combine = jax.nn.softmax(logits.reshape(bsz, m, n * p), axis=-1).reshape(bsz, m, n, p)
        slots = jnp.einsum('bmd,bmnp->bnpd', x, dispatch)
        y = jnp.einsum('bnpd,nde->bnpe', slots, W) + b[None, :, None, :]
        out = jnp.einsum('bnpd,bmnp->bmd', y, combine)
        return out
    x = x + _L0_attn_ref(_L0_cond_ref(x, cond_1024, L0_cond_router_w, L0_cond_router_t_w, L0_cond_router_bias, L0_cond_sw1, L0_cond_sw3, L0_cond_sw2, L0_cond_rw1, L0_cond_rw2), L0_attn_inproj_f, L0_attn_conv_w_f, L0_attn_conv_b_f, L0_attn_xproj_f, L0_attn_dt_w_f, L0_attn_dt_b_f, L0_attn_Alog_f, L0_attn_Dp_f, L0_attn_outproj_f, L0_attn_inproj_b, L0_attn_conv_w_b, L0_attn_conv_b_b, L0_attn_xproj_b, L0_attn_dt_w_b, L0_attn_dt_b_b, L0_attn_Alog_b, L0_attn_Dp_b, L0_attn_outproj_b, L0_attn_gate_w, L0_attn_gate_b, L0_attn_proj_w, L0_attn_proj_b)
    x = x + _L0_ffn_ref(_L0_cond2_ref(x, cond_1024), L0_ffn_phi, L0_ffn_W, L0_ffn_b)
    return x

_drawn_inputs = setup_inputs


def setup_inputs(seed=0):
    import zlib

    import numpy as np

    out = dict(_drawn_inputs(seed))
    spreads = {'L0_cond_router_bias': (0.0, 0.1),
     'L0_attn_conv_b_f': (0.0, 0.1),
     'L0_attn_dt_b_f': (-4.0, 0.2),
     'L0_attn_Dp_f': (1.0, 0.2),
     'L0_attn_conv_b_b': (0.0, 0.1),
     'L0_attn_dt_b_b': (-4.0, 0.2),
     'L0_attn_Dp_b': (1.0, 0.2),
     'L0_attn_gate_b': (0.0, 0.1),
     'L0_attn_proj_b': (0.0, 0.1)}
    factors = {}
    for name, (base, spread) in spreads.items():
        noise = np.random.default_rng([zlib.crc32(name.encode()), seed]).standard_normal(out[name].shape)
        drawn = base * np.exp(spread * noise) if base else spread * noise
        out[name] = jnp.asarray(drawn.astype(out[name].dtype))
    for name, factor in factors.items():
        out[name] = (out[name] * factor).astype(out[name].dtype)
    return out
```

```python
from contextlib import ExitStack

import numpy as np

import concourse.bass as bass
from concourse import mybir

F32 = mybir.dt.float32
ALU = mybir.AluOpType
ACT = mybir.ActivationFunctionType
AX_X = mybir.AxisListType.X

P = 128
BATCH, SEQ, DM = 2, 1024, 256
TOKENS = BATCH * SEQ
CT = 512
KC = DM // P

SHARED, EXPERTS, EXPERT_H, TOP_K = 512, 8, 128, 2
SU = SHARED // P
UNITS = SU + EXPERTS


def wait(eng, semaphore, value):
    if isinstance(value, int) and value <= 0:
        return
    eng.wait_ge(semaphore, value)


def moe_phase(nc, a, cond):
    with ExitStack() as ctx:
        def sb(name, shape):
            return ctx.enter_context(nc.sbuf_tensor("moe_" + name, shape, F32))

        def ps(name, shape):
            return ctx.enter_context(nc.psum_tensor("moe_" + name, shape, F32))

        def sem(name):
            return ctx.enter_context(nc.semaphore("moe_" + name))

        NT = TOKENS // P
        CB, NC = SEQ // CT, TOKENS // CT
        TPB = SEQ // P
        HB = 4
        xT = sb("xT", [P, KC, TOKENS])
        sw1, sw3 = sb("sw1", [P, KC, SHARED]), sb("sw3", [P, KC, SHARED])
        sw2 = sb("sw2", [P, SU, DM])
        rw1, rw2 = sb("rw1", [P, KC, EXPERTS * P]), sb("rw2", [P, EXPERTS, DM])
        rout = sb("rout", [P, KC, EXPERTS])
        rout_t = sb("rout_t", [P, KC, EXPERTS])
        temb = sb("temb", [P, KC, BATCH])
        temb_wide = sb("temb_wide", [P, KC, BATCH, P])
        bias = sb("bias", [P, EXPERTS])
        ident, tri, sel = sb("ident", [P, P]), sb("tri", [P, EXPERTS, EXPERTS]), sb("sel", [EXPERTS, EXPERTS, P])
        prob, score, mask, comb = (sb(n, [P, NT, EXPERTS]) for n in ("prob", "score", "mask", "comb"))
        gt, eq = (sb(n, [P, NT, EXPERTS, EXPERTS]) for n in ("gt", "eq"))
        rank = sb("rank", [P, NT, EXPERTS])
        den, rden, big, half = (sb(n, [P, NT]) for n in ("den", "rden", "big", "half"))
        comb_t = sb("comb_t", [EXPERTS, TOKENS])
        act_h = sb("act_h", [P, 2, CT])
        hid = sb("hid", [P, HB, CT])
        out_sb, rev_sb = sb("out_sb", [P, KC, CT]), sb("rev_sb", [P, KC, CT])
        scratch = sb("scratch", [P, 8])
        first = ps("first", [P, 3, 2, CT])
        second = ps("second", [P, KC, CT])

        loaded_router, loaded_x = sem("loaded_router"), sem("loaded_x")
        loaded_w1, loaded_w2 = sem("loaded_w1"), sem("loaded_w2")
        wide_made, logits_done, probs_done = sem("wide_made"), sem("logits_done"), sem("probs_done")
        chain = sem("chain")
        comb_ready, comb_turned, comb_t_ready = sem("comb_ready"), sem("comb_turned"), sem("comb_t_ready")
        first_done, act_done = sem("first_done"), sem("act_done")
        hid_done, hid_used = sem("hid_done"), sem("hid_used")
        second_done, second_read = sem("second_done"), sem("second_read")
        turned_back = sem("turned_back")
        stored = [[sem(f"stored{d}_{cc}") for cc in range(KC)] for d in range(2)]

        logits = first[:, 0, 0, 0:NT * EXPERTS].rearrange("p (t e) -> p t e", e=EXPERTS)
        turned = [first[0:EXPERTS, 1 + q // 2, q % 2, :] for q in range(4)]

        block = ctx.enter_context(nc.Block())

        @block.sync
        def _(sp):
            for dst, src in ((rout, a["router_T"]), (rout_t, a["router_t_T"]), (temb, a["temb_T"]), (ident, a["ident"]),
                             (tri, a["tri"]), (sel, a["sel"])):
                sp.dma_start(dst[:], src).then_inc(loaded_router, 16)
            sp.dma_start(bias[:], a["router_bias"].partition_broadcast(P)).then_inc(loaded_router, 16)
            sp.dma_start(xT[:], a["xT"]).then_inc(loaded_x, 16)
            for dst, src in ((sw1, a["sw1T"]), (sw3, a["sw3T"]), (rw1, a["rw1T"])):
                sp.dma_start(dst[:], src).then_inc(loaded_w1, 16)
            for dst, src in ((sw2, a["sw2T"]), (rw2, a["rw2T"])):
                sp.dma_start(dst[:], src).then_inc(loaded_w2, 16)
            for c in range(NC):
                b, h = divmod(c, CB)
                for cc in range(KC):
                    sp.wait_ge(second_read, KC * c + cc + 1)
                    sp.dma_start(cond[2 * b, :, cc, h * CT:(h + 1) * CT], out_sb[:, cc, :]
                                 ).then_inc(stored[0][cc], 16)
                    sp.wait_ge(turned_back, KC * c + cc + 1)
                    sp.dma_start(cond[2 * b + 1, :, cc, (CB - 1 - h) * CT:(CB - h) * CT], rev_sb[:, cc, :]
                                 ).then_inc(stored[1][cc], 16)
            for slot in stored[0] + stored[1]:
                sp.wait_ge(slot, 16 * NC)

        @block.tensor
        def _(pe):
            pe.wait_ge(loaded_router, 7 * 16)
            pe.wait_ge(wide_made, 1)
            pe.wait_ge(loaded_x, 16)
            for t in range(NT):
                for k in range(KC):
                    nc.tensor.matmul(logits[:, t, :], xT[:, k, t * P:(t + 1) * P], rout[:, k, :],
                                     start=(k == 0), stop=False)
                for k in range(KC):
                    mm = nc.tensor.matmul(logits[:, t, :], temb_wide[:, k, t // TPB, :], rout_t[:, k, :],
                                          start=False, stop=(k == KC - 1))
            mm.then_inc(logits_done, 1)
            pe.wait_ge(comb_ready, 1)
            for t in range(NT):
                mm = nc.tensor.transpose(turned[t // 4][:, (t % 4) * P:(t % 4 + 1) * P], comb[:, t, :], ident[:])
            mm.then_inc(comb_turned, 1)
            pe.wait_ge(comb_t_ready, 4)
            pe.wait_ge(loaded_w1, 3 * 16)
            pe.wait_ge(loaded_w2, 2 * 16)
            def chunk(c):
                def hidden(u):
                    pe.wait_ge(hid_done, UNITS * c + u + 1)
                    value, factor = first[:, u % 3, 0, :], first[:, u % 3, 1, :]
                    xs = [xT[:, k, bass.ds(c * CT, CT)] for k in range(KC)]
                    w = sw1[:, :, u * P:(u + 1) * P] if u < SU else rw1[:, :, (u - SU) * P:(u - SU + 1) * P]
                    for k in range(KC):
                        mm = nc.tensor.matmul(value, w[:, k, :], xs[k], start=(k == 0), stop=(k == KC - 1))
                    mm.then_inc(first_done, 1)
                    if u < SU:
                        for k in range(KC):
                            mm = nc.tensor.matmul(factor, sw3[:, k, u * P:(u + 1) * P], xs[k],
                                                  start=(k == 0), stop=(k == KC - 1))
                    else:
                        mm = nc.tensor.matmul(factor, sel[:, u - SU, :], comb_t[:, bass.ds(c * CT, CT)],
                                              start=True, stop=True)
                    mm.then_inc(first_done, 1)

                def project(u):
                    pe.wait_ge(hid_done, UNITS * c + u + 1 + 3)
                    w = sw2[:, u, :] if u < SU else rw2[:, u - SU, :]
                    for cc in range(KC):
                        if u == 0:
                            wait(pe, second_read, KC * c)
                        mm = nc.tensor.matmul(second[:, cc, :], w[:, cc * P:(cc + 1) * P], hid[:, u % HB, :],
                                              start=(u == 0), stop=(u == UNITS - 1))
                        if u == UNITS - 1:
                            mm.then_inc(second_done, 1)
                        elif cc == KC - 1:
                            mm.then_inc(hid_used, 1)

                for u in range(UNITS):
                    hidden(u)
                    if u >= 2:
                        project(u - 2)
                project(UNITS - 2)
                project(UNITS - 1)

            chunk(0)
            with pe.Fori(1, NC) as c:
                chunk(c)

        @block.scalar
        def _(act):
            act.wait_ge(logits_done, 1)
            nc.scalar.activation(prob[:], logits, ACT.Sigmoid).then_inc(probs_done, 1)
            def chunk(c):
                for u in range(UNITS):
                    act.wait_ge(first_done, 2 * (UNITS * c + u) + 1)
                    act.wait_ge(hid_done, UNITS * c + u + 2)
                    nc.scalar.activation(act_h[:, u % 2, :], first[:, u % 3, 0, :],
                                         ACT.Silu if u < SU else ACT.Gelu).then_inc(act_done, 1)
                for cc in range(KC):
                    act.wait_ge(second_done, KC * c + cc + 1)
                    wait(act, stored[0][cc], 16 * c)
                    wait(act, turned_back, KC * (c - 1) + cc + 1)
                    nc.scalar.activation(out_sb[:, cc, :], second[:, cc, :], ACT.Copy,
                                         scale=1.0 / (1 + TOP_K)).then_inc(second_read, 1)

            chunk(0)
            with act.Fori(1, NC) as c:
                chunk(c)

        @block.vector
        def _(dve):
            links = [0]

            def link(ins):
                links[0] += 1
                ins.then_inc(chain, 1)
                dve.wait_ge(chain, links[0])

            dve.wait_ge(loaded_router, 7 * 16)
            nc.vector.tensor_copy(temb_wide[:], temb[:].unsqueeze(3).to_broadcast([P, KC, BATCH, P])
                                  ).then_inc(wide_made, 1)
            nc.vector.memset(scratch[:], 0.0).then_inc(hid_done, 3)
            dve.wait_ge(probs_done, 1)
            link(nc.vector.tensor_tensor(score[:], prob[:], bias[:].unsqueeze(1).to_broadcast([P, NT, EXPERTS]), ALU.add))
            other = score[:].unsqueeze(2).to_broadcast([P, NT, EXPERTS, EXPERTS])
            own = score[:].unsqueeze(3).to_broadcast([P, NT, EXPERTS, EXPERTS])
            link(nc.vector.tensor_tensor(gt[:], other, own, ALU.is_gt))
            link(nc.vector.tensor_tensor(eq[:], other, own, ALU.is_equal))
            link(nc.vector.tensor_tensor(eq[:], eq[:], tri[:].unsqueeze(1).to_broadcast([P, NT, EXPERTS, EXPERTS]), ALU.mult))
            link(nc.vector.tensor_tensor(gt[:], gt[:], eq[:], ALU.add))
            link(nc.vector.tensor_reduce(rank[:], gt[:], AX_X, ALU.add))
            link(nc.vector.tensor_scalar(mask[:], rank[:], float(TOP_K), None, ALU.is_lt))
            link(nc.vector.tensor_tensor(comb[:], prob[:], mask[:], ALU.mult))
            link(nc.vector.tensor_reduce(den[:], comb[:], AX_X, ALU.add))
            link(nc.vector.tensor_scalar(big[:], den[:], 1e-9, None, ALU.is_gt))
            link(nc.vector.tensor_scalar(half[:], big[:], -1.0 / TOP_K, 1.0 / TOP_K, ALU.mult, ALU.add))
            link(nc.vector.tensor_scalar(den[:], den[:], 1e-9, None, ALU.add))
            link(nc.vector.reciprocal(rden[:], den[:]))
            link(nc.vector.tensor_tensor(rden[:], rden[:], big[:], ALU.mult))
            link(nc.vector.tensor_tensor(comb[:], comb[:], rden[:].unsqueeze(2).to_broadcast([P, NT, EXPERTS]), ALU.mult))
            link(nc.vector.tensor_tensor(mask[:], mask[:], half[:].unsqueeze(2).to_broadcast([P, NT, EXPERTS]), ALU.mult))
            nc.vector.tensor_tensor(comb[:], comb[:], mask[:], ALU.add).then_inc(comb_ready, 1)
            dve.wait_ge(comb_turned, 1)
            for q in range(4):
                nc.vector.tensor_copy(comb_t[:, q * CT:(q + 1) * CT], turned[q]).then_inc(comb_t_ready, 1)
            def chunk(c):
                for u in range(UNITS):
                    dve.wait_ge(first_done, 2 * (UNITS * c + u) + 2)
                    dve.wait_ge(act_done, UNITS * c + u + 1)
                    if u >= HB:
                        dve.wait_ge(hid_used, (UNITS - 1) * c + u - HB + 1)
                    else:
                        wait(dve, second_done, KC * c)
                    nc.vector.tensor_tensor(hid[:, u % HB, :], act_h[:, u % 2, :], first[:, u % 3, 1, :],
                                            ALU.mult).then_inc(hid_done, 1)
                for cc in range(KC):
                    dve.wait_ge(second_read, KC * c + cc + 1)
                    wait(dve, stored[1][cc], 16 * c)
                    nc.vector.tensor_copy(rev_sb[:, cc, :], out_sb[:, cc, ::-1]).then_inc(turned_back, 1)

            chunk(0)
            with dve.Fori(1, NC) as c:
                chunk(c)


DIN, NST, DTR, TAPS = 512, 16, 16, 4
DC = DIN // P
GROUPS = 2 * BATCH
HALVES = SEQ // CT
PASSES = 2
Q = DC // PASSES
RG = 4
NR = NST // RG
UB = PASSES * NST * Q
HCR = 8

def bank_uses(last):
    order, uses, count = [], {}, [0, 0]
    for h in range(HALVES):
        if h > 0:
            order += [(0, ("out", h - 1, 0)), (1, ("out", h - 1, 1))]
        order += [(0, ("dt", h, 1, q)) for q in range(Q)] + [(1, ("z", h, 1, q)) for q in range(Q)]
        if h < HALVES - 1 or not last:
            order += [(dc % 2, ("u", h + 1, dc)) for dc in range(DC)] + [(0, ("x", h + 1))]
            order += [(0, ("dt", h + 1, 0, q)) for q in range(Q)] + [(1, ("z", h + 1, 0, q)) for q in range(Q)]
    order += [(0, ("out", HALVES - 1, 0)), (1, ("out", HALVES - 1, 1))]
    for bank, use in order:
        count[bank] += 1
        uses[use] = count[bank]
    return uses, count


def mamba_phase(nc, a, cond, bc_rows, y_all):
    with ExitStack() as ctx:
        def sb(name, shape):
            return ctx.enter_context(nc.sbuf_tensor("scan_" + name, shape, F32))

        def ps(name, shape):
            return ctx.enter_context(nc.psum_tensor("scan_" + name, shape, F32))

        def sem(name):
            return ctx.enter_context(nc.semaphore("scan_" + name))

        inw = sb("inw", [P, KC, 2 * DIN])
        xw = sb("xw", [P, DC, DTR + 2 * NST])
        dtw = sb("dtw", [DTR, DIN])
        outw = sb("outw", [P, DC, DM])
        ident = sb("ident", [P, P])
        neg_a = sb("neg_a", [P, GROUPS, DC, NST])
        cw, cb = sb("cw", [P, GROUPS, DC, TAPS]), sb("cb", [P, GROUPS, DC])
        dtb, dp = sb("dtb", [P, GROUPS, DC]), sb("dp", [P, GROUPS, DC])
        xin = sb("xin", [P, KC, CT])
        u = sb("u", [P, DC, TAPS - 1 + SEQ])
        uc = sb("uc", [P, HALVES, DC, CT])
        th = sb("th", [P, 2, CT])
        thz = sb("thz", [P, Q, CT])
        dbl = sb("dbl", [DTR + 2 * NST, CT])
        delta, du, sz = (sb(n, [P, PASSES, Q, CT]) for n in ("delta", "du", "sz"))
        relu = sb("relu", [P, Q, CT])
        bc = sb("bc", [P, RG, 2, NR, CT])
        dbu = sb("dbu", [P, 2, Q, CT])
        hc = sb("hc", [P, HCR, CT])
        carry = sb("carry", [P, DC, NST])
        yo = sb("yo", [P, KC, CT])

        ysum = ps("ysum", [P, Q, CT])
        da = ps("da", [P, 2, CT])
        hs = ps("hs", [P, 2, CT])
        pb = ps("pb", [P, 2, CT])

        vecs, weights, outw_in, xin_in = sem("vecs"), sem("weights"), sem("outw_in"), sem("xin_in")
        neg_done, zeroed = sem("neg_done"), sem("zeroed")
        bank_ready = [sem(f"bank_ready{i}") for i in range(2)]
        bank_free = [sem(f"bank_free{i}") for i in range(2)]
        conv, uc_done, th_done, thz_done = sem("conv"), sem("uc_done"), sem("th_done"), sem("thz_done")
        bc_out = sem("bc_out")
        bc_in = [sem(f"bc_in{r}") for r in range(RG)]
        soft = sem("soft")
        delta_done, du_done = sem("delta_done"), sem("du_done")
        da_done, scan_done, dbu_done, hc_done = sem("da_done"), sem("scan_done"), sem("dbu_done"), sem("hc_done")
        ysum_done, y_read, yg_done = sem("ysum_done"), sem("y_read"), sem("yg_done")
        yo_stored = sem("yo_stored")
        carried = sem("carried")

        FIRST = {("u", 0, dc): 1 + dc // 2 for dc in range(DC)}
        FIRST.update({("x", 0): 3, **{("dt", 0, 0, q): 4 + q for q in range(Q)}, **{("z", 0, 0, q): 3 + q for q in range(Q)}})
        PRE = [5, 4]
        USES, PER = bank_uses(False)
        USES_LAST, _ = bank_uses(True)

        class At:
            def __init__(self, g, last=False, before=False):
                self.g, self.last, self.before = g, last, before

            def use(self, bank, *key):
                if self.before:
                    return FIRST[key]
                return PRE[bank] + PER[bank] * self.g + (USES_LAST if self.last else USES)[key]

        block = ctx.enter_context(nc.Block())

        def blk(at, h):
            return 0 if at.before else HALVES * at.g + h

        def vec(at, h):
            return 0 if at.before else at.g + h // HALVES

        @block.sync
        def _(sp):
            for dst, name in ((neg_a, "alog"), (cw, "convw"), (cb, "convb"), (dtb, "dtb"), (dp, "dp")):
                for g in range(GROUPS):
                    sp.dma_start(dst[:, g], a[name][g % 2]).then_inc(vecs, 16)
            sp.dma_start(ident[:], a["ident"]).then_inc(vecs, 16)

            def load_weights(g):
                for dst, name in ((inw, "inw"), (xw, "xw"), (dtw, "dtw")):
                    src = a[name][g % 2] if isinstance(g, int) else a[name + "4"][bass.ds(g, 1)].squeeze(0)
                    sp.dma_start(dst[:], src).then_inc(weights, 16)

            def load_x(at, h):
                src = cond[0] if at.before else cond[bass.ds(at.g + h // HALVES, 1)].squeeze(0)
                hh = h % HALVES
                sp.dma_start(xin[:], src[:, :, hh * CT:(hh + 1) * CT]).then_inc(xin_in, 16)

            def rows(at, h):
                k = blk(at, h)
                sp.wait_ge(bank_free[0], at.use(0, "x", h))
                dst = bc_rows[0] if at.before else bc_rows[bass.ds(k, 1)].squeeze(0)
                sp.dma_start(dst, dbl[DTR:DTR + 2 * NST, :]).then_inc(bc_out, 16)
                sp.wait_ge(bc_out, 16 * (k + 1))
                for r in range(RG):
                    wait(sp, dbu_done, 2 * NST * (k - 1) + NST + NR * (r + 1))
                    wait(sp, hc_done, UB * (k - 1) + Q * (NST + NR * (r + 1)))
                    src = dst.rearrange("(k r n) t -> r k (n t)", k=2, r=RG)[r]
                    sp.dma_start(bc[:, r].rearrange("p k n t -> p k (n t)"), src.partition_broadcast(P)
                                 ).then_inc(bc_in[r], 16)

            def store(at, h):
                k = blk(at, h)
                for cc in range(KC):
                    sp.wait_ge(bank_free[cc], at.use(cc, "out", h, cc))
                sp.dma_start(y_all[bass.ds(at.g, 1)].squeeze(0)[:, :, h * CT:(h + 1) * CT], yo[:]
                             ).then_inc(yo_stored, 16)

            def group(at):
                for h in range(HALVES):
                    if h > 0:
                        store(at, h - 1)
                    nxt = h < HALVES - 1 or not at.last
                    if nxt:
                        if h == HALVES - 1:
                            for bank, name in ((0, "dt"), (1, "z")):
                                sp.wait_ge(bank_ready[bank], at.use(bank, name, h, 1, Q - 1))
                            load_weights(at.g + 1)
                        else:
                            sp.wait_ge(bank_ready[1], at.use(1, "z", h, 1, Q - 1))
                        load_x(at, h + 1)
                        rows(at, h + 1)
                    if h == HALVES - 1:
                        store(at, h)
                        if not at.last:
                            sp.dma_start(outw[:], a["outw4"][bass.ds(at.g + 1, 1)].squeeze(0)).then_inc(outw_in, 16)

            before = At(0, before=True)
            load_weights(0)
            load_x(before, 0)
            sp.dma_start(outw[:], a["outw4"][0]).then_inc(outw_in, 16)
            rows(before, 0)
            for g in range(GROUPS):
                group(At(g, last=(g == GROUPS - 1)))
            sp.wait_ge(yo_stored, 16 * GROUPS * HALVES)

        @block.tensor
        def _(pe):
            def claim(at, bank, *key):
                use = at.use(bank, *key)
                wait(pe, bank_free[bank], use - 1)

            def in_proj(at, h, dc):
                k = blk(at, h)
                claim(at, dc % 2, "u", h, dc)
                if dc == 0:
                    pe.wait_ge(weights, 48 * (vec(at, h) + 1))
                    pe.wait_ge(xin_in, 16 * (k + 1))
                for c in range(KC):
                    mm = nc.tensor.matmul(pb[:, dc % 2, :], inw[:, c, dc * P:(dc + 1) * P], xin[:, c, :],
                                          start=(c == 0), stop=(c == KC - 1))
                mm.then_inc(bank_ready[dc % 2], 1)

            def x_proj(at, h):
                k = blk(at, h)
                claim(at, 0, "x", h)
                pe.wait_ge(uc_done, DC * (k + 1))
                for dc in range(DC):
                    mm = nc.tensor.matmul(pb[0:DTR + 2 * NST, 0, :], xw[:, dc, :], uc[:, h % 2, dc, :],
                                          start=(dc == 0), stop=(dc == DC - 1))
                mm.then_inc(bank_ready[0], 1)

            def dt_z(at, h, p, q):
                dc = Q * p + q
                claim(at, 0, "dt", h, p, q)
                nc.tensor.matmul(pb[:, 0, :], dtw[:, dc * P:(dc + 1) * P], dbl[0:DTR, :], start=True, stop=True
                                 ).then_inc(bank_ready[0], 1)
                claim(at, 1, "z", h, p, q)
                for c in range(KC):
                    mm = nc.tensor.matmul(pb[:, 1, :], inw[:, c, DIN + dc * P:DIN + (dc + 1) * P], xin[:, c, :],
                                          start=(c == 0), stop=(c == KC - 1))
                mm.then_inc(bank_ready[1], 1)

            def out_proj(at, h):
                k = blk(at, h)
                pe.wait_ge(yg_done, DC * (k + 1))
                if h == 0:
                    pe.wait_ge(outw_in, 16 * (at.g + 1))
                for cc in range(KC):
                    claim(at, cc, "out", h, cc)
                    for dc in range(DC):
                        mm = nc.tensor.matmul(pb[:, cc, :], outw[:, dc, cc * P:(cc + 1) * P], uc[:, h, dc, :],
                                              start=(dc == 0), stop=(dc == DC - 1))
                    mm.then_inc(bank_ready[cc], 1)

            def add_states(at, h, p, n):
                for q in range(Q):
                    s = UB * blk(at, h) + (p * NST + n) * Q + q
                    pe.wait_ge(hc_done, s + 1)
                    if n == 0 and q == 0:
                        wait(pe, y_read, Q * (PASSES * blk(at, h) + p))
                    nc.tensor.matmul(ysum[:, q, :], ident[:], hc[:, ((p * NST + n) * Q + q) % HCR, :],
                                     start=(n == 0), stop=(n == NST - 1)).then_inc(ysum_done, 1)

            def group(at):
                for h in range(HALVES):
                    nxt = h < HALVES - 1 or not at.last
                    for p in range(PASSES):
                        for n in range(NST):
                            add_states(at, h, p, n)
                            if p == 0 and n == 3 and h > 0:
                                out_proj(at, h - 1)
                            if p == 0 and n in (5, 7):
                                dt_z(at, h, 1, (n - 5) // 2)
                            if p == 1 and nxt and n in (0, 2, 4, 6):
                                in_proj(at, h + 1, n // 2)
                            if p == 1 and nxt and n == 9:
                                x_proj(at, h + 1)
                            if p == 1 and nxt and n in (11, 13):
                                dt_z(at, h + 1, 0, (n - 11) // 2)
                out_proj(at, HALVES - 1)

            pe.wait_ge(vecs, 16 * (5 * GROUPS + 1))
            before = At(0, before=True)
            for dc in range(DC):
                in_proj(before, 0, dc)
            x_proj(before, 0)
            for q in range(Q):
                dt_z(before, 0, 0, q)
            for g in range(GROUPS):
                group(At(g, last=(g == GROUPS - 1)))

        @block.scalar
        def _(act):
            def conv_in(at, h, dc):
                v = vec(at, h)
                bank = dc % 2
                act.wait_ge(bank_ready[bank], at.use(bank, "u", h, dc))
                lo = TAPS - 1 + (h % 2) * CT
                nc.scalar.activation(u[:, dc, lo:lo + CT], pb[:, bank, :], ACT.Copy)
                nc.scalar.activation(uc[:, h % 2, dc, :], pb[:, bank, :], ACT.Identity,
                                     scale=cw[:, bass.ds(v, 1), dc, TAPS - 1], bias=cb[:, bass.ds(v, 1), dc]
                                     ).then_inc(bank_free[bank], 1)

            def conv_tanh(at, h, dc):
                k = blk(at, h)
                act.wait_ge(conv, (TAPS - 1) * (DC * k + dc + 1))
                nc.scalar.activation(th[:, dc % 2, :], uc[:, h % 2, dc, :], ACT.Tanh).then_inc(th_done, 1)

            def copy_rows(at, h):
                k = blk(at, h)
                act.wait_ge(bank_ready[0], at.use(0, "x", h))
                wait(act, bc_out, 16 * k)
                nc.scalar.activation(dbl[:], pb[0:DTR + 2 * NST, 0, :], ACT.Copy).then_inc(bank_free[0], 1)

            def soft_in(at, h, p, q):
                k, v, dc = blk(at, h), vec(at, h), Q * p + q
                w = PASSES * k + p
                act.wait_ge(bank_ready[0], at.use(0, "dt", h, p, q))
                bias = dtb[:, bass.ds(v, 1), dc]
                wait(act, delta_done, Q * (w - 1) + q + 1)
                wait(act, du_done, Q * (w - PASSES) + q + 1)
                nc.scalar.activation(delta[:, p, q, :], pb[:, 0, :], ACT.Abs, bias=bias).then_inc(soft, 1)
                nc.scalar.activation(relu[:, q, :], pb[:, 0, :], ACT.Relu, bias=bias).then_inc(bank_free[0], 1)
                act.wait_ge(bank_ready[1], at.use(1, "z", h, p, q))
                wait(act, bank_free[1], at.use(1, "z", h, p, q) - 1)
                nc.scalar.activation(thz[:, q, :], pb[:, 1, :], ACT.Tanh, scale=0.5).then_inc(thz_done, 1)
                act.wait_ge(soft, 3 * Q * w + 2 * q + 1)
                nc.scalar.activation(delta[:, p, q, :], delta[:, p, q, :], ACT.Exp, scale=-1.0).then_inc(soft, 1)

            def soft_ln(at, h, p):
                w = PASSES * blk(at, h) + p
                for q in range(Q):
                    act.wait_ge(soft, 3 * Q * w + 2 * q + 2)
                    nc.scalar.activation(delta[:, p, q, :], delta[:, p, q, :], ACT.Ln, bias=1.0).then_inc(soft, 1)

            def decay(at, h, p, n):
                k = blk(at, h)
                if n == 0:
                    act.wait_ge(delta_done, Q * (PASSES * k + p + 1))
                for q in range(Q):
                    s = UB * k + (p * NST + n) * Q + q
                    wait(act, scan_done, s - 1)
                    nc.scalar.activation(da[:, q, :], delta[:, p, q, :], ACT.Exp,
                                         scale=neg_a[:, bass.ds(at.g, 1), Q * p + q, n]).then_inc(da_done, 1)

            def scale_out(at, h):
                k = blk(at, h)
                wait(act, yo_stored, 16 * k)
                for cc in range(KC):
                    act.wait_ge(bank_ready[cc], at.use(cc, "out", h, cc))
                    nc.scalar.activation(yo[:, cc, :], pb[:, cc, :], ACT.Copy, scale=0.5).then_inc(bank_free[cc], 1)

            def group(at):
                for h in range(HALVES):
                    nxt = h < HALVES - 1 or not at.last
                    for p in range(PASSES):
                        for n in range(NST):
                            decay(at, h, p, n)
                            if p == 0 and n == 6 and h > 0:
                                scale_out(at, h - 1)
                            if p == 0 and n in (8, 10):
                                soft_in(at, h, 1, (n - 8) // 2)
                            if p == 0 and n == 11:
                                soft_ln(at, h, 1)
                            if p == 1 and nxt and n in (1, 3, 5, 7):
                                conv_in(at, h + 1, n // 2)
                            if p == 1 and nxt and n in (3, 5, 7, 9):
                                conv_tanh(at, h + 1, n // 2 - 1)
                            if p == 1 and nxt and n == 11:
                                copy_rows(at, h + 1)
                            if p == 1 and nxt and n in (13, 14):
                                soft_in(at, h + 1, 0, n - 13)
                            if p == 1 and nxt and n == 15:
                                soft_ln(at, h + 1, 0)
                scale_out(at, HALVES - 1)

            act.wait_ge(vecs, 16 * (5 * GROUPS + 1))
            nc.scalar.activation(neg_a[:], neg_a[:], ACT.Exp).then_inc(neg_done, 1)
            act.wait_ge(zeroed, 3)
            before = At(0, before=True)
            for dc in range(DC):
                conv_in(before, 0, dc)
                if dc >= 1:
                    conv_tanh(before, 0, dc - 1)
            conv_tanh(before, 0, DC - 1)
            copy_rows(before, 0)
            for q in range(Q):
                soft_in(before, 0, 0, q)
            soft_ln(before, 0, 0)
            act.wait_ge(neg_done, 2)
            for g in range(GROUPS):
                group(At(g, last=(g == GROUPS - 1)))

        @block.gpsimd
        def _(pool):
            def steps(at, h, p):
                k = blk(at, h)
                w = PASSES * k + p
                for q in range(Q):
                    pool.wait_ge(soft, 3 * Q * w + 2 * Q + q + 1)
                    nc.gpsimd.tensor_tensor(delta[:, p, q, :], delta[:, p, q, :], relu[:, q, :], ALU.add
                                            ).then_inc(delta_done, 1)
                pool.wait_ge(uc_done, DC * (k + 1))
                for q in range(Q):
                    pool.wait_ge(delta_done, Q * w + q + 1)
                    nc.gpsimd.tensor_tensor(du[:, p, q, :], delta[:, p, q, :], uc[:, h % 2, Q * p + q, :], ALU.mult
                                            ).then_inc(du_done, 1)

            def inputs(at, h, p, n):
                k = blk(at, h)
                m = 2 * NST * k + p * NST + n
                if n == 0:
                    pool.wait_ge(du_done, Q * (PASSES * k + p + 1))
                if n % NR == 0 and p == 0:
                    pool.wait_ge(bc_in[n // NR], 16 * (k + 1))
                wait(pool, scan_done, Q * (m - 1))
                row = bc[:, n // NR, 0, n % NR, :].unsqueeze(1).to_broadcast([P, Q, CT])
                nc.gpsimd.tensor_tensor(dbu[:, n % 2], du[:, p], row, ALU.mult).then_inc(dbu_done, 1)

            def group(at):
                for h in range(HALVES):
                    nxt = h < HALVES - 1 or not at.last
                    for p in range(PASSES):
                        for n in range(NST):
                            inputs(at, h, p, n)
                            if p == 0 and n == 13:
                                steps(at, h, 1)
                    if nxt:
                        steps(at, h + 1, 0)

            steps(At(0, before=True), 0, 0)
            for g in range(GROUPS):
                group(At(g, last=(g == GROUPS - 1)))

        @block.vector
        def _(dve):
            def taps(at, h, dc):
                k, v = blk(at, h), vec(at, h)
                dve.wait_ge(bank_free[dc % 2], at.use(dc % 2, "u", h, dc))
                for t in range(TAPS - 1):
                    if t > 0:
                        dve.wait_ge(conv, (TAPS - 1) * (DC * k + dc) + t)
                    lo = (h % 2) * CT + t
                    nc.vector.scalar_tensor_tensor(uc[:, h % 2, dc, :], u[:, dc, lo:lo + CT], cw[:, bass.ds(v, 1), dc, t],
                                                   uc[:, h % 2, dc, :], ALU.mult, ALU.add).then_inc(conv, 1)

            def silu(at, h, dc):
                k = blk(at, h)
                dve.wait_ge(th_done, DC * k + dc + 1)
                nc.vector.scalar_tensor_tensor(uc[:, h % 2, dc, :], th[:, dc % 2, :], 1.0, uc[:, h % 2, dc, :],
                                               ALU.add, ALU.mult).then_inc(uc_done, 1)

            def gate_in(at, h, p, q):
                dve.wait_ge(thz_done, Q * (PASSES * blk(at, h) + p) + q + 1)
                nc.vector.scalar_tensor_tensor(sz[:, p, q, :], thz[:, q, :], 1.0, pb[:, 1, :], ALU.add, ALU.mult
                                               ).then_inc(bank_free[1], 1)

            def gate_out(at, h, p):
                k = blk(at, h)
                w = PASSES * k + p
                for q in range(Q):
                    dc = Q * p + q
                    dve.wait_ge(ysum_done, UB * k + (p + 1) * NST * Q - Q + q + 1)
                    nc.vector.scalar_tensor_tensor(uc[:, h, dc, :], uc[:, h, dc, :], dp[:, bass.ds(at.g, 1), dc],
                                                   ysum[:, q, :], ALU.mult, ALU.add).then_inc(y_read, 1)
                for q in range(Q):
                    dc = Q * p + q
                    dve.wait_ge(y_read, Q * w + q + 1)
                    nc.vector.tensor_tensor(uc[:, h, dc, :], uc[:, h, dc, :], sz[:, p, q, :], ALU.mult
                                            ).then_inc(yg_done, 1)

            def scan(at, h, p, n):
                k = blk(at, h)
                for q in range(Q):
                    dc = Q * p + q
                    i = (p * NST + n) * Q + q
                    s = UB * k + i
                    dve.wait_ge(da_done, s + 1)
                    if q == 0:
                        dve.wait_ge(dbu_done, 2 * NST * k + p * NST + n + 1)
                    wait(dve, hc_done, s - 1)
                    nc.vector.tensor_tensor_scan(hs[:, q, :], da[:, q, :], dbu[:, n % 2, q, :],
                                                 0.0 if h == 0 else carry[:, dc, n:n + 1], ALU.mult, ALU.add
                                                 ).then_inc(scan_done, 1)

            def weigh(at, h, p, n):
                k = blk(at, h)
                for q in range(Q):
                    dc = Q * p + q
                    i = (p * NST + n) * Q + q
                    s = UB * k + i
                    dve.wait_ge(scan_done, s + 1)
                    if n % NR == 0 and p == 0 and q == 0:
                        dve.wait_ge(bc_in[n // NR], 16 * (k + 1))
                    wait(dve, ysum_done, s - HCR + 1)
                    if h == 0:
                        nc.vector.tensor_copy(carry[:, dc, n:n + 1], hs[:, q, CT - 1:CT]).then_inc(carried, 1)
                    nc.vector.tensor_tensor(hc[:, i % HCR, :], hs[:, q, :], bc[:, n // NR, 1, n % NR, :], ALU.mult
                                            ).then_inc(hc_done, 1)

            def group(at):
                for h in range(HALVES):
                    nxt = h < HALVES - 1 or not at.last
                    for p in range(PASSES):
                        for n in range(NST):
                            scan(at, h, p, n)
                            weigh(at, h, p, n)
                            if n == 1 and (h, p) != (0, 0):
                                gate_out(at, *((h, 0) if p == 1 else (h - 1, 1)))
                            if p == 0 and n in (9, 11):
                                gate_in(at, h, 1, (n - 9) // 2)
                            if p == 1 and nxt and n in (2, 4, 6, 8):
                                taps(at, h + 1, n // 2 - 1)
                            if p == 1 and nxt and n in (4, 6, 8, 9):
                                silu(at, h + 1, {4: 0, 6: 1, 8: 2, 9: 3}[n])
                            if p == 1 and nxt and n in (14, 15):
                                gate_in(at, h + 1, 0, n - 14)
                gate_out(at, HALVES - 1, PASSES - 1)

            nc.vector.memset(u[:, :, 0:TAPS - 1], 0.0).then_inc(zeroed, 1)
            dve.wait_ge(vecs, 16 * (5 * GROUPS + 1))
            nc.vector.tensor_scalar(cw[:], cw[:], 0.5, None, ALU.mult).then_inc(zeroed, 1)
            nc.vector.tensor_scalar(cb[:], cb[:], 0.5, None, ALU.mult).then_inc(zeroed, 1)
            dve.wait_ge(neg_done, 1)
            dve.wait_ge(zeroed, 3)
            nc.vector.tensor_scalar(neg_a[:], neg_a[:], -1.0, None, ALU.mult).then_inc(neg_done, 1)
            before = At(0, before=True)
            for dc in range(DC):
                taps(before, 0, dc)
                silu(before, 0, dc)
            for q in range(Q):
                gate_in(before, 0, 0, q)
            for g in range(GROUPS):
                group(At(g, last=(g == GROUPS - 1)))


def mamba_inputs(i):
    g = {k[8:]: np.asarray(v) for k, v in i.items() if k.startswith("L0_attn_")}

    def both(f):
        return np.stack([f(g, "_f"), f(g, "_b")])

    def cols(v):
        return np.ascontiguousarray(np.moveaxis(v.reshape(DC, P, *v.shape[1:]), 0, 1))

    r = {
        "inw": both(lambda g, d: rows(g["inproj" + d])), "xw": both(lambda g, d: rows(g["xproj" + d])),
        "dtw": both(lambda g, d: g["dt_w" + d]), "outw": both(lambda g, d: rows(g["outproj" + d])),
        "alog": both(lambda g, d: cols(g["Alog" + d])), "convw": both(lambda g, d: cols(g["conv_w" + d])),
        "convb": both(lambda g, d: cols(g["conv_b" + d])), "dtb": both(lambda g, d: cols(g["dt_b" + d])),
        "dp": both(lambda g, d: cols(g["Dp" + d])),
    }
    for name in ("inw", "xw", "dtw", "outw"):
        r[name + "4"] = np.concatenate([r[name]] * BATCH)
    del r["outw"]
    return r


def mix_phase(nc, a, y_all, x1_t):
    with ExitStack() as ctx:
        def sb(name, shape):
            return ctx.enter_context(nc.sbuf_tensor("mix_" + name, shape, F32))

        def ps(name, shape):
            return ctx.enter_context(nc.psum_tensor("mix_" + name, shape, F32))

        def sem(name):
            return ctx.enter_context(nc.semaphore("mix_" + name))

        NC = TOKENS // CT
        gw, pw = sb("gw", [P, 2 * KC, DM]), sb("pw", [P, KC, DM])
        gb, prb = sb("gb", [P, KC]), sb("prb", [P, KC])
        yf, yb, xt = (sb(n, [P, KC, TOKENS]) for n in ("yf", "yb", "xt"))
        gate, dif, y = (sb(n, [P, 2, KC, CT]) for n in ("gate", "dif", "y"))
        res = sb("res", [P, 2, KC, CT])
        pg, pp = ps("pg", [P, 2, KC, CT]), ps("pp", [P, 2, KC, CT])

        loaded_w = sem("loaded_w")
        loaded_y = [sem(f"loaded_y{b}") for b in range(BATCH)]
        gate_mm, gate_done, dif_done, mul_done, y_done = (sem(n) for n in ("gate_mm", "gate_done", "dif_done", "mul_done", "y_done"))
        proj_mm, res_done = sem("proj_mm"), sem("res_done")
        stored = [sem(f"stored{s}") for s in range(2)]

        def backward(t, k, c):
            b, h = divmod(c, SEQ // CT)
            lo = b * SEQ + (SEQ // CT - 1 - h) * CT
            return t[:, k, lo:lo + CT][:, ::-1]

        block = ctx.enter_context(nc.Block())

        @block.sync
        def _(sp):
            for dst, name in ((gw, "gatew"), (pw, "projw"), (gb, "gateb"), (prb, "projb")):
                sp.dma_start(dst[:], a[name]).then_inc(loaded_w, 16)
            for b in range(BATCH):
                for d, t in enumerate((yf, yb)):
                    sp.dma_start(t[:, :, b * SEQ:(b + 1) * SEQ], y_all[2 * b + d]).then_inc(loaded_y[b], 16)
                sp.dma_start(xt[:, :, b * SEQ:(b + 1) * SEQ], a["xT"][:, :, b * SEQ:(b + 1) * SEQ]
                             ).then_inc(loaded_y[b], 16)
            for c in range(NC):
                sp.wait_ge(res_done, KC * (c + 1))
                sp.dma_start(x1_t[:, :, c * CT:(c + 1) * CT], res[:, c % 2]).then_inc(stored[c % 2], 16)
            for slot in stored:
                sp.wait_ge(slot, 16 * NC // 2)

        @block.tensor
        def _(pe):
            def gates(c):
                if c % 2 == 0:
                    pe.wait_ge(loaded_y[c // 2], 3 * 16)
                if c >= 2:
                    pe.wait_ge(gate_done, KC * (c - 1))
                for cc in range(KC):
                    for k in range(2 * KC):
                        rhs = yf[:, k, c * CT:(c + 1) * CT] if k < KC else backward(yb, k - KC, c)
                        mm = nc.tensor.matmul(pg[:, c % 2, cc, :], gw[:, k, cc * P:(cc + 1) * P], rhs,
                                              start=(k == 0), stop=(k == 2 * KC - 1))
                    mm.then_inc(gate_mm, 1)

            def project(c):
                pe.wait_ge(y_done, KC * (c + 1))
                if c >= 2:
                    pe.wait_ge(res_done, KC * (c - 1))
                for cc in range(KC):
                    for k in range(KC):
                        mm = nc.tensor.matmul(pp[:, c % 2, cc, :], pw[:, k, cc * P:(cc + 1) * P], y[:, c % 2, k, :],
                                              start=(k == 0), stop=(k == KC - 1))
                    mm.then_inc(proj_mm, 1)

            pe.wait_ge(loaded_w, 4 * 16)
            for c in range(NC):
                gates(c)
                if c >= 1:
                    project(c - 1)
            project(NC - 1)

        @block.scalar
        def _(act):
            act.wait_ge(loaded_w, 4 * 16)
            for c in range(NC):
                for cc in range(KC):
                    act.wait_ge(gate_mm, KC * c + cc + 1)
                    if c >= 2:
                        act.wait_ge(mul_done, KC * (c - 2) + cc + 1)
                    nc.scalar.activation(gate[:, c % 2, cc, :], pg[:, c % 2, cc, :], ACT.Sigmoid, bias=gb[:, cc:cc + 1]
                                         ).then_inc(gate_done, 1)

        @block.vector
        def _(dve):
            def mix(c):
                for k in range(KC):
                    dve.wait_ge(loaded_y[c // 2], 3 * 16)
                    nc.vector.tensor_tensor(dif[:, c % 2, k, :], yf[:, k, c * CT:(c + 1) * CT], backward(yb, k, c),
                                            ALU.subtract).then_inc(dif_done, 1)
                for k in range(KC):
                    dve.wait_ge(gate_done, KC * c + k + 1)
                    dve.wait_ge(dif_done, KC * c + k + 1)
                    nc.vector.tensor_tensor(dif[:, c % 2, k, :], dif[:, c % 2, k, :], gate[:, c % 2, k, :], ALU.mult
                                            ).then_inc(mul_done, 1)
                for k in range(KC):
                    dve.wait_ge(mul_done, KC * c + k + 1)
                    if c >= 2:
                        dve.wait_ge(proj_mm, KC * (c - 1))
                    nc.vector.tensor_tensor(y[:, c % 2, k, :], dif[:, c % 2, k, :], backward(yb, k, c), ALU.add
                                            ).then_inc(y_done, 1)

            def residual(c):
                for cc in range(KC):
                    dve.wait_ge(proj_mm, KC * c + cc + 1)
                    if c >= 2:
                        dve.wait_ge(stored[c % 2], 16 * (c // 2))
                    nc.vector.scalar_tensor_tensor(res[:, c % 2, cc, :], pp[:, c % 2, cc, :], prb[:, cc:cc + 1],
                                                   xt[:, cc, c * CT:(c + 1) * CT], ALU.add, ALU.add).then_inc(res_done, 1)

            for c in range(NC):
                mix(c)
                if c >= 1:
                    residual(c - 1)
            residual(NC - 1)


def mix_inputs(i):
    g = {k: np.asarray(v) for k, v in i.items()}
    return {"gatew": rows(g["L0_attn_gate_w"]), "projw": rows(g["L0_attn_proj_w"]),
            "gateb": np.ascontiguousarray(g["L0_attn_gate_b"].reshape(KC, P).T),
            "projb": np.ascontiguousarray(g["L0_attn_proj_b"].reshape(KC, P).T)}


NEXP, SLOTS = 64, 32
NP = NEXP * SLOTS
NCH = NP // CT
MT = SEQ // P
JT = CT // P
XPT = P // SLOTS
FAR = 1.0e30


def ffn_phase(nc, a, x1_t, x1_rows, out):
    with ExitStack() as ctx:
        def sb(name, shape):
            return ctx.enter_context(nc.sbuf_tensor("ffn_" + name, shape, F32))

        def ps(name, shape):
            return ctx.enter_context(nc.psum_tensor("ffn_" + name, shape, F32))

        def sem(name):
            return ctx.enter_context(nc.semaphore("ffn_" + name))

        xm_t = sb("xm_t", [P, KC, BATCH, SEQ])
        xm = sb("xm", [P, BATCH, MT, DM])
        et = sb("et", [P, BATCH, JT, SEQ])
        work = et[:].rearrange("p b j s -> p (b j s)")
        x1s = [work[:, u * SEQ:(u + 1) * SEQ] for u in range(4)]
        mag, share, cum, ones = (work[:, (4 + u) * SEQ:(5 + u) * SEQ] for u in range(4))
        below = sb("below", [P, SEQ + 1])
        rv = sb("rv", [P, KC, BATCH])
        stat = sb("stat", [P, 4, 8])
        ident = sb("ident", [P, P])
        phi = sb("phi", [P, KC, NP])
        wt = sb("wt", [P, JT, XPT, KC, DM])
        ebias = sb("ebias", [P, NP // P, DM])
        turn_sb = sb("turn_sb", [P, 2, CT])
        lsb = sb("lsb", [P, 2, BATCH, CT])
        diff, tanh = sb("diff", [P, 2, CT]), sb("tanh", [P, 2, CT])
        disp, ex = sb("disp", [P, 2, BATCH, CT]), sb("ex", [P, 2, BATCH, CT])
        slots = sb("slots", [P, BATCH, KC, CT])
        y = sb("y", [P, JT, BATCH, DM])
        acc = sb("acc", [P, MT, BATCH, DM])
        nmax = sb("nmax", [P, NCH + 1, MT, BATCH])
        lmax = sb("lmax", [P, MT, BATCH])
        drop = sb("drop", [P, NCH, MT, BATCH])
        alpha = sb("alpha", [P, NCH, MT, BATCH])
        part = sb("part", [P, NCH, MT, BATCH])
        den, rden = sb("den", [P, MT, BATCH]), sb("rden", [P, MT, BATCH])
        xres = sb("xres", [P, 2, BATCH, DM])

        lg = ps("lg", [P, BATCH, CT])
        sl = ps("sl", [P, BATCH, KC, CT])
        tb = ps("tb", [P, CT])
        oy = ps("oy", [P, CT])

        loaded_x, loaded_c, loaded_phi, loaded_b = sem("loaded_x"), sem("loaded_c"), sem("loaded_phi"), sem("loaded_b")
        mag_done, exp2_done, xm_done, chain = sem("mag_done"), sem("exp2_done"), sem("xm_done"), sem("chain")
        sum_inv = sem("sum_inv")
        turned = sem("turned")
        turn_read = [sem(f"turn_read{q}") for q in range(2)]
        xrow_stored = [sem(f"xrow_stored{q}") for q in range(2)]
        init_done, alpha_done = sem("init_done"), sem("alpha_done")
        l_done, l_copied, nm_ready, diff_done = sem("l_done"), sem("l_copied"), sem("nm_ready"), sem("diff_done")
        tanh_done, disp_done, exp_done = sem("tanh_done"), sem("disp_done"), sem("exp_done")
        slots_step, sl_act, sl_dve = sem("slots_step"), sem("sl_act"), sem("sl_dve")
        et_turned, et_act, et_dve = sem("et_turned"), sem("et_act"), sem("et_dve")
        y_mm, y_sb = sem("y_mm"), sem("y_sb")
        out_done, acc_done = sem("out_done"), sem("acc_done")
        small = sem("small")
        w_loaded = [sem(f"w_loaded{j}") for j in range(JT)]
        res_loaded = [sem(f"res_loaded{j}") for j in range(2)]
        res_done = sem("res_done")
        stored = [sem(f"stored{s}") for s in range(2)]

        PIECES = [(b, cc) for b in range(BATCH) for cc in range(KC)]

        block = ctx.enter_context(nc.Block())

        @block.sync
        def _(sp):
            for u, (b, cc) in enumerate(PIECES):
                sp.dma_start(x1s[u], x1_t[:, cc, b * SEQ:(b + 1) * SEQ]).then_inc(loaded_x, 16)
            sp.dma_start(rv[:], a["temb_T"]).then_inc(loaded_c, 16)
            sp.dma_start(ident[:], a["ident"]).then_inc(loaded_c, 16)
            sp.dma_start(phi[:], a["phi"]).then_inc(loaded_phi, 16)
            sp.dma_start(ebias[:], a["ebias"]).then_inc(loaded_b, 16)
            for j in range(JT):
                sp.dma_start(wt[:, j], a["ew"][j]).then_inc(w_loaded[j], 16)
            for g in range(MT):
                sp.wait_ge(turn_read[g % 2], g // 2 + 1)
                b, m = divmod(2 * g, MT)
                sp.dma_start(x1_rows[:, b, m:m + 2, :], turn_sb[:, g % 2, :].rearrange("p (m d) -> p m d", m=2)
                             ).then_inc(xrow_stored[g % 2], 16)
            with sp.Fori(1, NCH) as c:
                for j in range(JT):
                    sp.wait_ge(y_mm, JT * (c - 1) + j + 1)
                    sp.dma_start(wt[:, j], a["ew"][bass.ds(c * JT + j, 1)].rearrange("o p n k e -> (o p) n k e")
                                 ).then_inc(w_loaded[j], 16)
            for q in range(2):
                sp.wait_ge(xrow_stored[q], 16 * MT // 2)
            for m in range(MT):
                if m >= 2:
                    sp.wait_ge(stored[m % 2], 16 * (m // 2))
                sp.dma_start(xres[:, m % 2], x1_rows[:, :, m, :]).then_inc(res_loaded[m % 2], 16)
                if m >= 1:
                    sp.wait_ge(res_done, m)
                    sp.dma_start(out[:, (m - 1) * P:m * P, :].rearrange("b p d -> p b d"), xres[:, (m - 1) % 2]
                                 ).then_inc(stored[(m - 1) % 2], 16)
            sp.wait_ge(res_done, MT)
            sp.dma_start(out[:, (MT - 1) * P:MT * P, :].rearrange("b p d -> p b d"), xres[:, (MT - 1) % 2]
                         ).then_inc(stored[(MT - 1) % 2], 16)
            for slot in stored:
                sp.wait_ge(slot, 16 * MT // 2)

        @block.tensor
        def _(pe):
            pe.wait_ge(loaded_c, 32)
            pe.wait_ge(loaded_x, 4 * 16)
            banks = [tb, oy]
            for g in range(2 * MT):
                b, m = divmod(2 * (g % MT), MT)
                if g >= MT:
                    pe.wait_ge(xm_done, KC * b + KC)
                if g >= 2:
                    pe.wait_ge(turn_read[g % 2], g // 2)
                for q in range(4):
                    cc, mm_ = q % 2, m + q // 2
                    src = x1s[KC * b + cc] if g < MT else xm_t[:, cc, b, :]
                    mm = nc.tensor.transpose(banks[g % 2][:, q * P:(q + 1) * P], src[:, mm_ * P:(mm_ + 1) * P], ident[:])
                mm.then_inc(turned, 1)
            for q in range(2):
                pe.wait_ge(turn_read[q], MT)
            pe.wait_ge(loaded_phi, 16)

            def logits(c, m):
                wait(pe, l_copied, BATCH * (MT * c + m))
                for b in range(BATCH):
                    for k in range(KC):
                        mm = nc.tensor.matmul(lg[:, b, :], xm_t[:, k, b, m * P:(m + 1) * P],
                                              phi[:, k, bass.ds(c * CT, CT)], start=(k == 0), stop=(k == KC - 1))
                    mm.then_inc(l_done, 1)

            def combine(c, m):
                if m == 0:
                    pe.wait_ge(y_sb, JT * (c + 1))
                else:
                    wait(pe, acc_done, MT * c + m)
                for b in range(BATCH):
                    for j in range(JT):
                        mm = nc.tensor.matmul(oy[:, b * DM:(b + 1) * DM], et[:, b, j, m * P:(m + 1) * P], y[:, j, b, :],
                                              start=(j == 0), stop=(j == JT - 1))
                mm.then_inc(out_done, 1)

            def gather(c, m, b):
                pe.wait_ge(disp_done, 2 * (MT * c + m) + b + 1)
                if m == 0 and b == 0:
                    wait(pe, sl_act, KC * c)
                    wait(pe, sl_dve, KC * c)
                for cc in range(KC):
                    mm = nc.tensor.matmul(sl[:, b, cc, :], xm[:, b, m, cc * P:(cc + 1) * P], disp[:, m % 2, b, :],
                                          start=(m == 0), stop=(m == MT - 1))
                if b == BATCH - 1:
                    mm.then_inc(slots_step, 1)

            def turn(c, m, b):
                pe.wait_ge(exp_done, 2 * (MT * c + m) + b + 1)
                if b == 0:
                    wait(pe, et_dve, MT * c + m)
                    if m == 0:
                        wait(pe, y_sb, JT * c)
                else:
                    pe.wait_ge(et_act, MT * c + m + 1)
                for j in range(JT):
                    mm = nc.tensor.transpose(tb[:, j * P:(j + 1) * P], ex[:, m % 2, b, j * P:(j + 1) * P], ident[:])
                mm.then_inc(et_turned, 1)

            def tile_rest(c, m):
                gather(c, m, 0)
                turn(c, m, 0)
                gather(c, m, 1)
                turn(c, m, 1)

            def experts(c, j):
                pe.wait_ge(w_loaded[j], 16 * (c + 1))
                if j == 0:
                    pe.wait_ge(sl_act, KC * (c + 1))
                    pe.wait_ge(sl_dve, KC * (c + 1))
                    wait(pe, acc_done, MT * c)
                elif j == 1:
                    pe.wait_ge(et_dve, MT * (c + 1))
                else:
                    pe.wait_ge(y_sb, JT * c + j - 1)
                bank = oy if j % 2 == 0 else tb
                for b in range(BATCH):
                    for k in range(KC):
                        for n in range(XPT):
                            mm = nc.tensor.matmul(bank[n * SLOTS:(n + 1) * SLOTS, b * DM:(b + 1) * DM],
                                                  slots[:, b, k, j * P + n * SLOTS:j * P + (n + 1) * SLOTS],
                                                  wt[:, j, n, k, :], start=(k == 0), stop=(k == KC - 1),
                                                  tile_position=(0, n * SLOTS))
                mm.then_inc(y_mm, 1)

            def chunk(c, first):
                for m in range(MT):
                    logits(c, m)
                    if not first:
                        combine(c - 1, m)
                    if m >= 1:
                        tile_rest(c, m - 1)
                gather(c, MT - 1, 0)
                gather(c, MT - 1, 1)
                turn(c, MT - 1, 0)
                turn(c, MT - 1, 1)
                for j in range(JT):
                    experts(c, j)

            chunk(0, True)
            with pe.Fori(1, NCH) as c:
                chunk(c, False)
            for m in range(MT):
                combine(NCH - 1, m)

        @block.scalar
        def _(act):
            def turned_out(g):
                b, m = divmod(2 * (g % MT), MT)
                act.wait_ge(turned, g + 1)
                bank = (tb, oy)[g % 2]
                if g < MT:
                    if g >= 2:
                        act.wait_ge(xrow_stored[g % 2], 16 * (g // 2))
                    nc.scalar.activation(turn_sb[:, g % 2, :], bank[:], ACT.Copy).then_inc(turn_read[g % 2], 1)
                else:
                    nc.scalar.activation(xm[:, b, m:m + 2, :], bank[:].rearrange("p (m d) -> p m d", m=2), ACT.Copy
                                         ).then_inc(turn_read[g % 2], 1)

            act.wait_ge(loaded_x, 4 * 16)
            for u in range(len(PIECES)):
                if u >= 1:
                    act.wait_ge(xm_done, u)
                nc.scalar.activation(mag, x1s[u], ACT.Abs, accum_out=stat[:, u, 0:1]).then_inc(mag_done, 1)
                act.wait_ge(sum_inv, u + 1)
                nc.scalar.activation(share, mag, ACT.Exp, scale=stat[:, u, 2:3],
                                     accum_out=stat[:, u, 3:4]).then_inc(exp2_done, 1)
                turned_out(2 * u)
                turned_out(2 * u + 1)
            for g in range(MT + 1, 2 * MT, 2):
                turned_out(g)

            def turn_out(c, m):
                act.wait_ge(et_turned, 2 * (MT * c + m) + 1)
                wait(act, out_done, MT * (c - 1) + m + 1)
                nc.scalar.activation(et[:, 0, :, m * P:(m + 1) * P], tb[:].rearrange("p (j s) -> p j s", j=JT),
                                     ACT.Copy).then_inc(et_act, 1)

            def chunk(c):
                for m in range(MT):
                    t = MT * c + m
                    wait(act, diff_done, t - 1)
                    for b in range(BATCH):
                        act.wait_ge(l_done, BATCH * t + b + 1)
                        nc.scalar.activation(lsb[:, m % 2, b, :], lg[:, b, :], ACT.Copy).then_inc(l_copied, 1)
                    act.wait_ge(diff_done, t + 1)
                    wait(act, disp_done, 2 * (t - 1))
                    nc.scalar.activation(tanh[:, m % 2, :], diff[:, m % 2, :], ACT.Tanh, scale=0.5
                                         ).then_inc(tanh_done, 1)
                    act.wait_ge(nm_ready, t + 1)
                    wait(act, et_turned, 2 * (t - 1))
                    for b in range(BATCH):
                        nc.scalar.activation(ex[:, m % 2, b, :], lsb[:, m % 2, b, :], ACT.Exp,
                                             bias=nmax[:, bass.ds(c + 1, 1), m, b],
                                             accum_out=part[:, bass.ds(c, 1), m, b]).then_inc(exp_done, 1)
                    nc.scalar.activation(alpha[:, bass.ds(c, 1), m, :], drop[:, bass.ds(c, 1), m, :], ACT.Exp
                                         ).then_inc(alpha_done, 1)
                    if m >= 1:
                        turn_out(c, m - 1)
                turn_out(c, MT - 1)
                act.wait_ge(slots_step, MT * (c + 1))
                wait(act, y_mm, JT * c)
                for cc in range(KC):
                    nc.scalar.activation(slots[:, 0, cc, :], sl[:, 0, cc, :], ACT.Copy).then_inc(sl_act, 1)

            act.wait_ge(init_done, 2)
            chunk(0)
            with act.Fori(1, NCH) as c:
                chunk(c)

        @block.gpsimd
        def _(pool):
            nc.gpsimd.memset(nmax[:, 0], FAR).then_inc(init_done, 1)
            nc.gpsimd.memset(acc[:], 0.0).then_inc(init_done, 1)

        @block.vector
        def _(dve):
            links = [0]

            def link(ins):
                links[0] += 1
                ins.then_inc(chain, 1)
                dve.wait_ge(chain, links[0])

            link(nc.vector.memset(ones, 1.0))
            link(nc.vector.memset(below[:, 0:1], 1.0))
            dve.wait_ge(loaded_c, 32)
            for u, (b, cc) in enumerate(PIECES):
                s = stat[:, u, :]
                dve.wait_ge(mag_done, u + 1)
                link(nc.vector.reciprocal(s[:, 1:2], s[:, 0:1]))
                nc.vector.tensor_scalar(s[:, 2:3], s[:, 1:2], 2.0, None, ALU.mult).then_inc(sum_inv, 1)
                dve.wait_ge(exp2_done, u + 1)
                link(nc.vector.reciprocal(s[:, 4:5], s[:, 3:4]))
                link(nc.vector.tensor_scalar(share, share, s[:, 4:5], None, ALU.mult))
                link(nc.vector.tensor_tensor_scan(cum, ones, share, 0.0, ALU.mult, ALU.add))
                link(nc.vector.tensor_scalar(below[:, 1:SEQ + 1], cum, 0.001, rv[:, cc, b:b + 1], ALU.add, ALU.is_le))
                link(nc.vector.tensor_tensor(cum, below[:, 0:SEQ], below[:, 1:SEQ + 1], ALU.subtract))
                link(nc.vector.tensor_tensor_reduce(share, mag, cum, 1.0, 0.0, ALU.mult, ALU.add, s[:, 5:6]))
                link(nc.vector.tensor_scalar(s[:, 6:7], below[:, SEQ:SEQ + 1], 3.0e38, s[:, 5:6], ALU.mult, ALU.add))
                nc.vector.scalar_tensor_tensor(xm_t[:, cc, b, :], mag, s[:, 6:7], x1s[u], ALU.is_ge, ALU.mult
                                               ).then_inc(xm_done, 1)
            for g in range(MT, 2 * MT, 2):
                b, m = divmod(2 * (g % MT), MT)
                dve.wait_ge(turned, g + 1)
                nc.vector.tensor_copy(xm[:, b, m:m + 2, :], tb[:].rearrange("p (m d) -> p m d", m=2)
                                      ).then_inc(turn_read[0], 1)

            def turn_out(c, m):
                dve.wait_ge(et_turned, 2 * (MT * c + m) + 2)
                wait(dve, out_done, MT * (c - 1) + m + 1)
                nc.vector.tensor_copy(et[:, 1, :, m * P:(m + 1) * P], tb[:].rearrange("p (j s) -> p j s", j=JT)
                                      ).then_inc(et_dve, 1)

            def add_output(c, m):
                dve.wait_ge(out_done, MT * c + m + 1)
                dve.wait_ge(alpha_done, MT * c + m + 1)
                for b in range(BATCH):
                    last = nc.vector.scalar_tensor_tensor(acc[:, m, b, :], acc[:, m, b, :], alpha[:, bass.ds(c, 1), m, b],
                                                          oy[:, b * DM:(b + 1) * DM], ALU.mult, ALU.add)
                last.then_inc(acc_done, 1)

            def chunk(c, first):
                for m in range(MT):
                    t = MT * c + m
                    dve.wait_ge(l_copied, BATCH * (t + 1))
                    nc.vector.tensor_reduce(lmax[:, m, :], lsb[:, m % 2], AX_X, ALU.max, negate=True).then_inc(small, 1)
                    dve.wait_ge(small, 2 * t + 1)
                    nc.vector.tensor_tensor(nmax[:, bass.ds(c + 1, 1), m, :].rearrange("p o b -> p (o b)"),
                                            nmax[:, bass.ds(c, 1), m, :].rearrange("p o b -> p (o b)"), lmax[:, m, :],
                                            ALU.min).then_inc(small, 1)
                    dve.wait_ge(small, 2 * t + 2)
                    nc.vector.tensor_tensor(drop[:, bass.ds(c, 1), m, :], nmax[:, bass.ds(c + 1, 1), m, :],
                                            nmax[:, bass.ds(c, 1), m, :], ALU.subtract).then_inc(nm_ready, 1)
                    wait(dve, tanh_done, t - 1)
                    nc.vector.tensor_tensor(diff[:, m % 2, :], lsb[:, m % 2, 1, :], lsb[:, m % 2, 0, :], ALU.subtract
                                            ).then_inc(diff_done, 1)
                    if not first:
                        add_output(c - 1, m)
                    dve.wait_ge(tanh_done, t + 1)
                    wait(dve, slots_step, t - 1)
                    for b, sign in enumerate((-0.5, 0.5)):
                        nc.vector.tensor_scalar(disp[:, m % 2, b, :], tanh[:, m % 2, :], sign, 0.5, ALU.mult, ALU.add
                                                ).then_inc(disp_done, 1)
                    if m >= 1:
                        turn_out(c, m - 1)
                turn_out(c, MT - 1)
                dve.wait_ge(slots_step, MT * (c + 1))
                wait(dve, y_mm, JT * c)
                for cc in range(KC):
                    nc.vector.tensor_copy(slots[:, 1, cc, :], sl[:, 1, cc, :]).then_inc(sl_dve, 1)
                for j in range(JT):
                    dve.wait_ge(y_mm, JT * c + j + 1)
                    bank = oy if j % 2 == 0 else tb
                    nc.vector.tensor_tensor(y[:, j], bank[:].rearrange("p (b e) -> p b e", b=BATCH),
                                            ebias[:, bass.ds(c * JT + j, 1), :].to_broadcast([P, BATCH, DM]), ALU.add
                                            ).then_inc(y_sb, 1)

            dve.wait_ge(init_done, 2)
            dve.wait_ge(loaded_b, 16)
            chunk(0, True)
            with dve.Fori(1, NCH) as c:
                chunk(c, False)
            dve.wait_ge(alpha_done, MT * NCH)
            dve.wait_ge(exp_done, 2 * MT * NCH)
            link(nc.vector.tensor_copy(den[:], part[:, 0]))
            for c in range(1, NCH):
                link(nc.vector.tensor_tensor(den[:], den[:], alpha[:, c], ALU.mult))
                link(nc.vector.tensor_tensor(den[:], den[:], part[:, c], ALU.add))
            link(nc.vector.reciprocal(rden[:], den[:]))
            for m in range(MT):
                add_output(NCH - 1, m)
                dve.wait_ge(acc_done, MT * (NCH - 1) + m + 1)
                dve.wait_ge(res_loaded[m % 2], 16 * (m // 2 + 1))
                for b in range(BATCH):
                    last = nc.vector.scalar_tensor_tensor(xres[:, m % 2, b, :], acc[:, m, b, :], rden[:, m, b:b + 1],
                                                          xres[:, m % 2, b, :], ALU.mult, ALU.add)
                last.then_inc(res_done, 1)


def ffn_inputs(i):
    g = {k: np.asarray(v) for k, v in i.items()}
    w = g["L0_ffn_W"].reshape(NP // P, XPT, KC, P, DM).transpose(0, 3, 1, 2, 4)
    b = g["L0_ffn_b"].reshape(NP // P, XPT, 1, DM)
    return {
        "phi": rows(g["L0_ffn_phi"].reshape(DM, NP)), "ew": np.ascontiguousarray(w),
        "ebias": np.broadcast_to(b, (NP // P, XPT, SLOTS, DM)).reshape(NP // P, P, DM).transpose(1, 0, 2),
    }


CONST = {
    "ident": np.eye(P, dtype=np.float32),
    "tri": np.broadcast_to(np.tril(np.ones((EXPERTS, EXPERTS), np.float32), -1)[None], (P, EXPERTS, EXPERTS)),
    "sel": np.repeat(np.eye(EXPERTS, dtype=np.float32)[:, :, None], P, 2),
}


def rows(w, k=P):
    w = np.asarray(w)
    return np.ascontiguousarray(w.reshape(w.shape[0] // k, k, -1).transpose(1, 0, 2))


def moe_inputs(i):
    g = {k: np.asarray(v) for k, v in i.items()}
    return {
        "xT": rows(g["x"].reshape(TOKENS, DM).T), "temb_T": rows(g["cond_1024"].T),
        "router_T": rows(g["L0_cond_router_w"].T), "router_t_T": rows(g["L0_cond_router_t_w"].T),
        "router_bias": g["L0_cond_router_bias"],
        "sw1T": rows(g["L0_cond_sw1"].T), "sw3T": rows(g["L0_cond_sw3"].T), "sw2T": rows(g["L0_cond_sw2"].T),
        "rw1T": rows(g["L0_cond_rw1"].transpose(2, 0, 1).reshape(DM, -1)),
        "rw2T": np.ascontiguousarray(g["L0_cond_rw2"].transpose(2, 0, 1)),
    }


def build(nc, a, out):
    cond = nc.dram_tensor("cond", [GROUPS, P, KC, SEQ], F32).ap()
    bc_rows = nc.dram_tensor("bc_rows", [GROUPS * HALVES, 2 * NST, CT], F32).ap()
    y_all = nc.dram_tensor("y_all", [GROUPS, P, KC, SEQ], F32).ap()
    x1_t = nc.dram_tensor("x1_t", [P, KC, TOKENS], F32).ap()
    x1_rows = nc.dram_tensor("x1_rows", [P, BATCH, MT, DM], F32).ap()
    moe_phase(nc, a, cond)
    mamba_phase(nc, a, cond, bc_rows, y_all)
    mix_phase(nc, a, y_all, x1_t)
    ffn_phase(nc, a, x1_t, x1_rows, out)


def kernel(**inputs):
    from concourse import bacc
    from concourse.bass_utils import run_bass_kernel_spmd

    arrays = {**moe_inputs(inputs), **mamba_inputs(inputs), **mix_inputs(inputs), **ffn_inputs(inputs), **CONST}
    arrays = {f"in_{k}": np.ascontiguousarray(v) for k, v in arrays.items()}
    nc = bacc.Bacc("TRN2", target_bir_lowering=False, num_devices=1)
    a = {k[3:]: nc.dram_tensor(k, v.shape, F32, kind="ExternalInput").ap() for k, v in arrays.items()}
    out = nc.dram_tensor("out", [BATCH, SEQ, DM], F32, kind="ExternalOutput").ap()
    build(nc, a, out)
    r = run_bass_kernel_spmd(nc, [arrays], core_ids=[0])
    return r.results[0]["out"]
```

```python
from contextlib import ExitStack

import numpy as np

import concourse.bass as bass
from concourse import mybir

F32 = mybir.dt.float32
ALU = mybir.AluOpType
ACT = mybir.ActivationFunctionType
AX_X = mybir.AxisListType.X

P = 128
BATCH, SEQ, DM = 2, 1024, 256
TOKENS = BATCH * SEQ
CT = 512
KC = DM // P

SHARED, EXPERTS, EXPERT_H, TOP_K = 512, 8, 128, 2
SU = SHARED // P
UNITS = SU + EXPERTS


def wait(eng, semaphore, value):
    if isinstance(value, int) and value <= 0:
        return
    eng.wait_ge(semaphore, value)


def moe_phase(nc, a, cond):
    with ExitStack() as ctx:
        def sb(name, shape):
            return ctx.enter_context(nc.sbuf_tensor("moe_" + name, shape, F32))

        def ps(name, shape):
            return ctx.enter_context(nc.psum_tensor("moe_" + name, shape, F32))

        def sem(name):
            return ctx.enter_context(nc.semaphore("moe_" + name))

        NT = TOKENS // P
        CB, NC = SEQ // CT, TOKENS // CT
        TPB = SEQ // P
        HB = 4
        xT = sb("xT", [P, KC, TOKENS])
        sw1, sw3 = sb("sw1", [P, KC, SHARED]), sb("sw3", [P, KC, SHARED])
        sw2 = sb("sw2", [P, SU, DM])
        rw1, rw2 = sb("rw1", [P, KC, EXPERTS * P]), sb("rw2", [P, EXPERTS, DM])
        rout = sb("rout", [P, KC, EXPERTS])
        rout_t = sb("rout_t", [P, KC, EXPERTS])
        temb = sb("temb", [P, KC, BATCH])
        temb_wide = sb("temb_wide", [P, KC, BATCH, P])
        bias = sb("bias", [P, EXPERTS])
        ident, tri, sel = sb("ident", [P, P]), sb("tri", [P, EXPERTS, EXPERTS]), sb("sel", [EXPERTS, EXPERTS, P])
        prob, score, mask, comb = (sb(n, [P, NT, EXPERTS]) for n in ("prob", "score", "mask", "comb"))
        gt, eq = (sb(n, [P, NT, EXPERTS, EXPERTS]) for n in ("gt", "eq"))
        rank = sb("rank", [P, NT, EXPERTS])
        den, rden, big, half = (sb(n, [P, NT]) for n in ("den", "rden", "big", "half"))
        comb_t = sb("comb_t", [EXPERTS, TOKENS])
        act_h = sb("act_h", [P, 2, CT])
        hid = sb("hid", [P, HB, CT])
        out_sb, rev_sb = sb("out_sb", [P, KC, CT]), sb("rev_sb", [P, KC, CT])
        scratch = sb("scratch", [P, 8])
        first = ps("first", [P, 3, 2, CT])
        second = ps("second", [P, KC, CT])

        loaded_router, loaded_x = sem("loaded_router"), sem("loaded_x")
        loaded_w1, loaded_w2 = sem("loaded_w1"), sem("loaded_w2")
        wide_made, logits_done, probs_done = sem("wide_made"), sem("logits_done"), sem("probs_done")
        chain = sem("chain")
        comb_ready, comb_turned, comb_t_ready = sem("comb_ready"), sem("comb_turned"), sem("comb_t_ready")
        first_done, act_done = sem("first_done"), sem("act_done")
        hid_done, hid_used = sem("hid_done"), sem("hid_used")
        second_done, second_read = sem("second_done"), sem("second_read")
        turned_back = sem("turned_back")
        stored = [[sem(f"stored{d}_{cc}") for cc in range(KC)] for d in range(2)]

        logits = first[:, 0, 0, 0:NT * EXPERTS].rearrange("p (t e) -> p t e", e=EXPERTS)
        turned = [first[0:EXPERTS, 1 + q // 2, q % 2, :] for q in range(4)]

        block = ctx.enter_context(nc.Block())

        @block.sync
        def _(sp):
            for dst, src in ((rout, a["router_T"]), (rout_t, a["router_t_T"]), (temb, a["temb_T"]), (ident, a["ident"]),
                             (tri, a["tri"]), (sel, a["sel"])):
                sp.dma_start(dst[:], src).then_inc(loaded_router, 16)
            sp.dma_start(bias[:], a["router_bias"].partition_broadcast(P)).then_inc(loaded_router, 16)
            sp.dma_start(xT[:], a["xT"]).then_inc(loaded_x, 16)
            for dst, src in ((sw1, a["sw1T"]), (sw3, a["sw3T"]), (rw1, a["rw1T"])):
                sp.dma_start(dst[:], src).then_inc(loaded_w1, 16)
            for dst, src in ((sw2, a["sw2T"]), (rw2, a["rw2T"])):
                sp.dma_start(dst[:], src).then_inc(loaded_w2, 16)
            for c in range(NC):
                b, h = divmod(c, CB)
                for cc in range(KC):
                    sp.wait_ge(second_read, KC * c + cc + 1)
                    sp.dma_start(cond[2 * b, :, cc, h * CT:(h + 1) * CT], out_sb[:, cc, :]
                                 ).then_inc(stored[0][cc], 16)
                    sp.wait_ge(turned_back, KC * c + cc + 1)
                    sp.dma_start(cond[2 * b + 1, :, cc, (CB - 1 - h) * CT:(CB - h) * CT], rev_sb[:, cc, :]
                                 ).then_inc(stored[1][cc], 16)
            for slot in stored[0] + stored[1]:
                sp.wait_ge(slot, 16 * NC)

        @block.tensor
        def _(pe):
            pe.wait_ge(loaded_router, 7 * 16)
            pe.wait_ge(wide_made, 1)
            pe.wait_ge(loaded_x, 16)
            for t in range(NT):
                for k in range(KC):
                    nc.tensor.matmul(logits[:, t, :], xT[:, k, t * P:(t + 1) * P], rout[:, k, :],
                                     start=(k == 0), stop=False)
                for k in range(KC):
                    mm = nc.tensor.matmul(logits[:, t, :], temb_wide[:, k, t // TPB, :], rout_t[:, k, :],
                                          start=False, stop=(k == KC - 1))
            mm.then_inc(logits_done, 1)
            pe.wait_ge(comb_ready, 1)
            for t in range(NT):
                mm = nc.tensor.transpose(turned[t // 4][:, (t % 4) * P:(t % 4 + 1) * P], comb[:, t, :], ident[:])
            mm.then_inc(comb_turned, 1)
            pe.wait_ge(comb_t_ready, 4)
            pe.wait_ge(loaded_w1, 3 * 16)
            pe.wait_ge(loaded_w2, 2 * 16)
            def chunk(c):
                def hidden(u):
                    pe.wait_ge(hid_done, UNITS * c + u + 1)
                    value, factor = first[:, u % 3, 0, :], first[:, u % 3, 1, :]
                    xs = [xT[:, k, bass.ds(c * CT, CT)] for k in range(KC)]
                    w = sw1[:, :, u * P:(u + 1) * P] if u < SU else rw1[:, :, (u - SU) * P:(u - SU + 1) * P]
                    for k in range(KC):
                        mm = nc.tensor.matmul(value, w[:, k, :], xs[k], start=(k == 0), stop=(k == KC - 1))
                    mm.then_inc(first_done, 1)
                    if u < SU:
                        for k in range(KC):
                            mm = nc.tensor.matmul(factor, sw3[:, k, u * P:(u + 1) * P], xs[k],
                                                  start=(k == 0), stop=(k == KC - 1))
                    else:
                        mm = nc.tensor.matmul(factor, sel[:, u - SU, :], comb_t[:, bass.ds(c * CT, CT)],
                                              start=True, stop=True)
                    mm.then_inc(first_done, 1)

                def project(u):
                    pe.wait_ge(hid_done, UNITS * c + u + 1 + 3)
                    w = sw2[:, u, :] if u < SU else rw2[:, u - SU, :]
                    for cc in range(KC):
                        if u == 0:
                            wait(pe, second_read, KC * c)
                        mm = nc.tensor.matmul(second[:, cc, :], w[:, cc * P:(cc + 1) * P], hid[:, u % HB, :],
                                              start=(u == 0), stop=(u == UNITS - 1))
                        if u == UNITS - 1:
                            mm.then_inc(second_done, 1)
                        elif cc == KC - 1:
                            mm.then_inc(hid_used, 1)

                for u in range(UNITS):
                    hidden(u)
                    if u >= 2:
                        project(u - 2)
                project(UNITS - 2)
                project(UNITS - 1)

            chunk(0)
            with pe.Fori(1, NC) as c:
                chunk(c)

        @block.scalar
        def _(act):
            act.wait_ge(logits_done, 1)
            nc.scalar.activation(prob[:], logits, ACT.Sigmoid).then_inc(probs_done, 1)
            def chunk(c):
                for u in range(UNITS):
                    act.wait_ge(first_done, 2 * (UNITS * c + u) + 1)
                    act.wait_ge(hid_done, UNITS * c + u + 2)
                    nc.scalar.activation(act_h[:, u % 2, :], first[:, u % 3, 0, :],
                                         ACT.Silu if u < SU else ACT.Gelu).then_inc(act_done, 1)
                for cc in range(KC):
                    act.wait_ge(second_done, KC * c + cc + 1)
                    wait(act, stored[0][cc], 16 * c)
                    wait(act, turned_back, KC * (c - 1) + cc + 1)
                    nc.scalar.activation(out_sb[:, cc, :], second[:, cc, :], ACT.Copy,
                                         scale=1.0 / (1 + TOP_K)).then_inc(second_read, 1)

            chunk(0)
            with act.Fori(1, NC) as c:
                chunk(c)

        @block.vector
        def _(dve):
            links = [0]

            def link(ins):
                links[0] += 1
                ins.then_inc(chain, 1)
                dve.wait_ge(chain, links[0])

            dve.wait_ge(loaded_router, 7 * 16)
            nc.vector.tensor_copy(temb_wide[:], temb[:].unsqueeze(3).to_broadcast([P, KC, BATCH, P])
                                  ).then_inc(wide_made, 1)
            nc.vector.memset(scratch[:], 0.0).then_inc(hid_done, 3)
            dve.wait_ge(probs_done, 1)
            link(nc.vector.tensor_tensor(score[:], prob[:], bias[:].unsqueeze(1).to_broadcast([P, NT, EXPERTS]), ALU.add))
            other = score[:].unsqueeze(2).to_broadcast([P, NT, EXPERTS, EXPERTS])
            own = score[:].unsqueeze(3).to_broadcast([P, NT, EXPERTS, EXPERTS])
            link(nc.vector.tensor_tensor(gt[:], other, own, ALU.is_gt))
            link(nc.vector.tensor_tensor(eq[:], other, own, ALU.is_equal))
            link(nc.vector.tensor_tensor(eq[:], eq[:], tri[:].unsqueeze(1).to_broadcast([P, NT, EXPERTS, EXPERTS]), ALU.mult))
            link(nc.vector.tensor_tensor(gt[:], gt[:], eq[:], ALU.add))
            link(nc.vector.tensor_reduce(rank[:], gt[:], AX_X, ALU.add))
            link(nc.vector.tensor_scalar(mask[:], rank[:], float(TOP_K), None, ALU.is_lt))
            link(nc.vector.tensor_tensor(comb[:], prob[:], mask[:], ALU.mult))
            link(nc.vector.tensor_reduce(den[:], comb[:], AX_X, ALU.add))
            link(nc.vector.tensor_scalar(big[:], den[:], 1e-9, None, ALU.is_gt))
            link(nc.vector.tensor_scalar(half[:], big[:], -1.0 / TOP_K, 1.0 / TOP_K, ALU.mult, ALU.add))
            link(nc.vector.tensor_scalar(den[:], den[:], 1e-9, None, ALU.add))
            link(nc.vector.reciprocal(rden[:], den[:]))
            link(nc.vector.tensor_tensor(rden[:], rden[:], big[:], ALU.mult))
            link(nc.vector.tensor_tensor(comb[:], comb[:], rden[:].unsqueeze(2).to_broadcast([P, NT, EXPERTS]), ALU.mult))
            link(nc.vector.tensor_tensor(mask[:], mask[:], half[:].unsqueeze(2).to_broadcast([P, NT, EXPERTS]), ALU.mult))
            nc.vector.tensor_tensor(comb[:], comb[:], mask[:], ALU.add).then_inc(comb_ready, 1)
            dve.wait_ge(comb_turned, 1)
            for q in range(4):
                nc.vector.tensor_copy(comb_t[:, q * CT:(q + 1) * CT], turned[q]).then_inc(comb_t_ready, 1)
            def chunk(c):
                for u in range(UNITS):
                    dve.wait_ge(first_done, 2 * (UNITS * c + u) + 2)
                    dve.wait_ge(act_done, UNITS * c + u + 1)
                    if u >= HB:
                        dve.wait_ge(hid_used, (UNITS - 1) * c + u - HB + 1)
                    else:
                        wait(dve, second_done, KC * c)
                    nc.vector.tensor_tensor(hid[:, u % HB, :], act_h[:, u % 2, :], first[:, u % 3, 1, :],
                                            ALU.mult).then_inc(hid_done, 1)
                for cc in range(KC):
                    dve.wait_ge(second_read, KC * c + cc + 1)
                    wait(dve, stored[1][cc], 16 * c)
                    nc.vector.tensor_copy(rev_sb[:, cc, :], out_sb[:, cc, ::-1]).then_inc(turned_back, 1)

            chunk(0)
            with dve.Fori(1, NC) as c:
                chunk(c)


DIN, NST, DTR, TAPS = 512, 16, 16, 4
DC = DIN // P
GROUPS = 2 * BATCH
HALVES = SEQ // CT
PASSES = 2
Q = DC // PASSES
RG = 4
NR = NST // RG
UB = PASSES * NST * Q
BLOCKS = GROUPS * HALVES
HCR = 12
HSR = 4
DBR = 3
UCR = 3

IN_AT = (6, 8, 10, 12)
OUT_AT = (13, 15)
X_AT, DT_AT = 19, (22, 24)
CONV_AT = (9, 11, 13, 15)
TANH_AT = (13, 15, 17, 19)
SCALE_AT = (17, 19)
SOFT_AT = (1, 4)
ROWS_AT, NEXT_SOFT_AT = 22, (24, 27)
STEP_AT, NEXT_STEP_AT = 9, 30
TAP_AT = (20, 24, 28, 32)
SILU_AT = (27, 31, 35, 39)
GATE_AT, NEXT_GATE_AT = (5, 10), (49, 55)
ADD_AT, GATE_OUT_AT = (2, 3), (4, 5)

def bank_uses():
    def feed(k):
        return [(dc % 2, ("u", k, dc)) for dc in range(DC)] + [(0, ("x", k))] + step(k, 0)

    def step(k, p):
        return [use for q in range(Q) for use in ((0, ("dt", k, p, q)), (1, ("z", k, p, q)))]

    order = feed(0)
    for k in range(BLOCKS):
        order += step(k, 1)
        if k + 1 < BLOCKS:
            order += [(dc % 2, ("u", k + 1, dc)) for dc in range(DC)]
        if k > 0:
            order += [(cc, ("out", k - 1, cc)) for cc in range(KC)]
        if k + 1 < BLOCKS:
            order += [(0, ("x", k + 1))] + step(k + 1, 0)
    order += [(cc, ("out", BLOCKS - 1, cc)) for cc in range(KC)]
    uses, count = {}, [0, 0]
    for bank, use in order:
        count[bank] += 1
        uses[use] = count[bank]
    return uses


def mamba_phase(nc, a, cond, bc_rows, y_all):
    with ExitStack() as ctx:
        def sb(name, shape):
            return ctx.enter_context(nc.sbuf_tensor("scan_" + name, shape, F32))

        def ps(name, shape):
            return ctx.enter_context(nc.psum_tensor("scan_" + name, shape, F32))

        def sem(name):
            return ctx.enter_context(nc.semaphore("scan_" + name))

        inw = sb("inw", [P, KC, 2 * DIN])
        xw = sb("xw", [P, DC, DTR + 2 * NST])
        dtw = sb("dtw", [DTR, DIN])
        outw = sb("outw", [P, DC, DM])
        ident = sb("ident", [P, P])
        vec = sb("vec", [P, 2, DC, NST + TAPS + 3])
        neg_a, cw, cb, dtb, dp = (vec[:, :, :, lo:hi] for lo, hi in (
            (0, NST), (NST, NST + TAPS), *((NST + TAPS + j, NST + TAPS + j + 1) for j in range(3))))
        xin = sb("xin", [P, KC, CT])
        u = sb("u", [P, DC, TAPS - 1 + SEQ])
        uc = sb("uc", [P, UCR, DC, CT])
        th = sb("th", [P, 2, CT])
        thz = sb("thz", [P, Q, CT])
        dbl = sb("dbl", [DTR + 2 * NST, CT])
        delta, du, sz = (sb(n, [P, PASSES, Q, CT]) for n in ("delta", "du", "sz"))
        relu = sb("relu", [P, Q, CT])
        bc = sb("bc", [P, RG, 2, NR, CT])
        dbu = sb("dbu", [P, DBR, Q, CT])
        hc = sb("hc", [P, HCR, CT])
        carry = sb("carry", [P, DC, NST])
        yo = sb("yo", [P, KC, CT])

        ysum = ps("ysum", [P, Q, CT])
        hs = ps("hs", [P, HSR, CT])
        pb = ps("pb", [P, 2, CT])

        vecs, weights, outw_in, xin_in, ident_in = (sem(n) for n in ("vecs", "weights", "outw_in", "xin_in", "ident_in"))
        inw_in = [sem(f"inw_in{k}") for k in range(2)]
        neg_done, zeroed = sem("neg_done"), sem("zeroed")
        bank_ready = [sem(f"bank_ready{i}") for i in range(2)]
        bank_free = [sem(f"bank_free{i}") for i in range(2)]
        conv, uc_done, th_done, thz_done = sem("conv"), sem("uc_done"), sem("th_done"), sem("thz_done")
        bc_out = sem("bc_out")
        bc_in = [sem(f"bc_in{r}") for r in range(RG)]
        soft = sem("soft")
        delta_done, du_done = sem("delta_done"), sem("du_done")
        da_done, scan_done, dbu_done, hc_done = sem("da_done"), sem("scan_done"), sem("dbu_done"), sem("hc_done")
        ysum_done, y_read, yg_done = sem("ysum_done"), sem("y_read"), sem("yg_done")
        yo_stored = sem("yo_stored")
        carried = sem("carried")

        USES = bank_uses()

        block = ctx.enter_context(nc.Block())

        @block.sync
        def _(sp):
            def load_weights(g):
                for k in range(2):
                    sp.dma_start(inw[:, :, k * DIN:(k + 1) * DIN], a["inw"][g % 2][:, :, k * DIN:(k + 1) * DIN]
                                 ).then_inc(inw_in[k], 16)
                for dst, name in ((xw, "xw"), (dtw, "dtw")):
                    sp.dma_start(dst[:], a[name][g % 2]).then_inc(weights, 16)

            def load_outw(g):
                sp.dma_start(outw[:], a["outw"][g % 2]).then_inc(outw_in, 16)

            def load_x(k):
                g, h = divmod(k, HALVES)
                sp.dma_start(xin[:], cond[g][:, :, h * CT:(h + 1) * CT]).then_inc(xin_in, 16)

            def rows(k):
                sp.wait_ge(bank_free[0], USES["x", k])
                sp.dma_start(bc_rows[k], dbl[DTR:DTR + 2 * NST, :]).then_inc(bc_out, 16)
                sp.wait_ge(bc_out, 16 * (k + 1))
                for r in range(RG):
                    wait(sp, dbu_done, PASSES * NST * (k - 1) + NST + NR * (r + 1))
                    wait(sp, hc_done, UB * (k - 1) + Q * (NST + NR * (r + 1)))
                    src = bc_rows[k].rearrange("(k r n) t -> r k (n t)", k=2, r=RG)[r]
                    sp.dma_start(bc[:, r].rearrange("p k n t -> p k (n t)"), src.partition_broadcast(P)
                                 ).then_inc(bc_in[r], 16)

            def store(k):
                g, h = divmod(k, HALVES)
                for cc in range(KC):
                    sp.wait_ge(bank_free[cc], USES["out", k, cc])
                sp.dma_start(y_all[g][:, :, h * CT:(h + 1) * CT], yo[:]).then_inc(yo_stored, 16)

            load_x(0)
            load_weights(0)
            sp.dma_start(vec[:], a["vecs"]).then_inc(vecs, 16)
            sp.dma_start(ident[:], a["ident"]).then_inc(ident_in, 16)
            load_outw(0)
            rows(0)
            for k in range(BLOCKS):
                g, h = divmod(k, HALVES)
                if k + 1 < BLOCKS:
                    for q in range(Q):
                        sp.wait_ge(bank_ready[0], USES["dt", k, 1, q])
                        sp.wait_ge(bank_ready[1], USES["z", k, 1, q])
                    if h == HALVES - 1:
                        load_weights(g + 1)
                    load_x(k + 1)
                if k > 0:
                    store(k - 1)
                    if h == 0:
                        load_outw(g)
                if k + 1 < BLOCKS:
                    rows(k + 1)
            store(BLOCKS - 1)
            sp.wait_ge(yo_stored, 16 * BLOCKS)

        @block.tensor
        def _(pe):
            def claim(bank, *key):
                wait(pe, bank_free[bank], USES[key] - 1)

            def in_proj(k, dc):
                claim(dc % 2, "u", k, dc)
                if dc == 0:
                    pe.wait_ge(inw_in[0], 16 * (k // HALVES + 1))
                    pe.wait_ge(xin_in, 16 * (k + 1))
                for c in range(KC):
                    mm = nc.tensor.matmul(pb[:, dc % 2, :], inw[:, c, dc * P:(dc + 1) * P], xin[:, c, :],
                                          start=(c == 0), stop=(c == KC - 1))
                mm.then_inc(bank_ready[dc % 2], 1)

            def x_proj(k):
                pe.wait_ge(weights, 32 * (k // HALVES + 1))
                claim(0, "x", k)
                pe.wait_ge(uc_done, DC * (k + 1))
                for dc in range(DC):
                    mm = nc.tensor.matmul(pb[0:DTR + 2 * NST, 0, :], xw[:, dc, :], uc[:, k % UCR, dc, :],
                                          start=(dc == 0), stop=(dc == DC - 1))
                mm.then_inc(bank_ready[0], 1)

            def dt_z(k, p, q):
                dc = Q * p + q
                claim(0, "dt", k, p, q)
                nc.tensor.matmul(pb[:, 0, :], dtw[:, dc * P:(dc + 1) * P], dbl[0:DTR, :], start=True, stop=True
                                 ).then_inc(bank_ready[0], 1)
                claim(1, "z", k, p, q)
                if p == 0 and q == 0:
                    pe.wait_ge(inw_in[1], 16 * (k // HALVES + 1))
                for c in range(KC):
                    mm = nc.tensor.matmul(pb[:, 1, :], inw[:, c, DIN + dc * P:DIN + (dc + 1) * P], xin[:, c, :],
                                          start=(c == 0), stop=(c == KC - 1))
                mm.then_inc(bank_ready[1], 1)

            def out_proj(k, cc):
                pe.wait_ge(yg_done, DC * (k + 1))
                if k % HALVES == 0:
                    pe.wait_ge(outw_in, 16 * (k // HALVES + 1))
                claim(cc, "out", k, cc)
                for dc in range(DC):
                    mm = nc.tensor.matmul(pb[:, cc, :], outw[:, dc, cc * P:(cc + 1) * P], uc[:, k % UCR, dc, :],
                                          start=(dc == 0), stop=(dc == DC - 1))
                mm.then_inc(bank_ready[cc], 1)

            def add_states(k, p, n):
                for q in range(Q):
                    s = UB * k + (p * NST + n) * Q + q
                    pe.wait_ge(hc_done, s + 1)
                    if n == 0 and q == 0:
                        wait(pe, y_read, Q * (PASSES * k + p))
                    nc.tensor.matmul(ysum[:, q, :], ident[:], hc[:, s % HCR, :],
                                     start=(n == 0), stop=(n == NST - 1)).then_inc(ysum_done, 1)

            for dc in range(DC):
                in_proj(0, dc)
            x_proj(0)
            for q in range(Q):
                dt_z(0, 0, q)
            pe.wait_ge(ident_in, 16)
            for k in range(BLOCKS):
                for i in range(PASSES * NST):
                    if i in (0, 1):
                        dt_z(k, 1, i)
                    add_states(k, *divmod(i, NST))
                    if k + 1 < BLOCKS and i in IN_AT:
                        in_proj(k + 1, IN_AT.index(i))
                    if k > 0 and i in OUT_AT:
                        out_proj(k - 1, OUT_AT.index(i))
                    if k + 1 < BLOCKS and i == X_AT:
                        x_proj(k + 1)
                    if k + 1 < BLOCKS and i in DT_AT:
                        dt_z(k + 1, 0, DT_AT.index(i))
            for cc in range(KC):
                out_proj(BLOCKS - 1, cc)

        @block.scalar
        def _(act):
            def conv_in(k, dc):
                v = k // HALVES % 2
                bank = dc % 2
                act.wait_ge(bank_ready[bank], USES["u", k, dc])
                lo = TAPS - 1 + (k % HALVES) * CT
                nc.scalar.activation(u[:, dc, lo:lo + CT], pb[:, bank, :], ACT.Copy)
                nc.scalar.activation(uc[:, k % UCR, dc, :], pb[:, bank, :], ACT.Identity,
                                     scale=cw[:, v, dc, TAPS - 1:TAPS], bias=cb[:, v, dc]
                                     ).then_inc(bank_free[bank], 1)

            def conv_tanh(k, dc):
                act.wait_ge(conv, (TAPS - 1) * (DC * k + dc + 1))
                wait(act, uc_done, DC * k + dc - 1)
                nc.scalar.activation(th[:, dc % 2, :], uc[:, k % UCR, dc, :], ACT.Tanh).then_inc(th_done, 1)

            def copy_rows(k):
                act.wait_ge(bank_ready[0], USES["x", k])
                wait(act, bc_out, 16 * k)
                nc.scalar.activation(dbl[:], pb[0:DTR + 2 * NST, 0, :], ACT.Copy).then_inc(bank_free[0], 1)

            def soft_in(k, p, q):
                dc = Q * p + q
                w = PASSES * k + p
                act.wait_ge(bank_ready[0], USES["dt", k, p, q])
                bias = dtb[:, k // HALVES % 2, dc]
                wait(act, delta_done, Q * (w - 1) + q + 1)
                wait(act, du_done, Q * (w - PASSES) + q + 1)
                nc.scalar.activation(delta[:, p, q, :], pb[:, 0, :], ACT.Abs, bias=bias).then_inc(soft, 1)
                nc.scalar.activation(relu[:, q, :], pb[:, 0, :], ACT.Relu, bias=bias).then_inc(bank_free[0], 1)
                act.wait_ge(bank_ready[1], USES["z", k, p, q])
                wait(act, bank_free[1], USES["z", k, p, q] - 1)
                nc.scalar.activation(thz[:, q, :], pb[:, 1, :], ACT.Tanh, scale=0.5).then_inc(thz_done, 1)
                act.wait_ge(soft, 3 * Q * w + 2 * q + 1)
                nc.scalar.activation(delta[:, p, q, :], delta[:, p, q, :], ACT.Exp, scale=-1.0).then_inc(soft, 1)

            def soft_ln(k, p):
                w = PASSES * k + p
                for q in range(Q):
                    act.wait_ge(soft, 3 * Q * w + 2 * q + 2)
                    nc.scalar.activation(delta[:, p, q, :], delta[:, p, q, :], ACT.Ln, bias=1.0).then_inc(soft, 1)

            def decay(k, p, n):
                if n == 0:
                    act.wait_ge(delta_done, Q * (PASSES * k + p + 1))
                for q in range(Q):
                    s = UB * k + (p * NST + n) * Q + q
                    wait(act, hc_done, s - HSR + 1)
                    nc.scalar.activation(hs[:, s % HSR, :], delta[:, p, q, :], ACT.Exp,
                                         scale=neg_a[:, k // HALVES % 2, Q * p + q, n:n + 1]).then_inc(da_done, 1)

            def scale_out(k, cc):
                wait(act, yo_stored, 16 * k)
                act.wait_ge(bank_ready[cc], USES["out", k, cc])
                nc.scalar.activation(yo[:, cc, :], pb[:, cc, :], ACT.Copy, scale=0.5).then_inc(bank_free[cc], 1)

            act.wait_ge(vecs, 16)
            act.wait_ge(zeroed, 3)
            nc.scalar.activation(neg_a[:], neg_a[:], ACT.Exp).then_inc(neg_done, 1)
            for dc in range(DC):
                conv_in(0, dc)
                if dc >= 1:
                    conv_tanh(0, dc - 1)
            conv_tanh(0, DC - 1)
            copy_rows(0)
            for q in range(Q):
                soft_in(0, 0, q)
            soft_ln(0, 0)
            act.wait_ge(neg_done, 2)
            for k in range(BLOCKS):
                for i in range(PASSES * NST):
                    decay(k, *divmod(i, NST))
                    if i in SOFT_AT:
                        soft_in(k, 1, SOFT_AT.index(i))
                    if i == SOFT_AT[-1]:
                        soft_ln(k, 1)
                    if k + 1 < BLOCKS:
                        if i in CONV_AT:
                            conv_in(k + 1, CONV_AT.index(i))
                        if i in TANH_AT:
                            conv_tanh(k + 1, TANH_AT.index(i))
                    if k > 0 and i in SCALE_AT:
                        scale_out(k - 1, SCALE_AT.index(i))
                    if k + 1 < BLOCKS:
                        if i == ROWS_AT:
                            copy_rows(k + 1)
                        if i in NEXT_SOFT_AT:
                            soft_in(k + 1, 0, NEXT_SOFT_AT.index(i))
                        if i == NEXT_SOFT_AT[-1] + 1:
                            soft_ln(k + 1, 0)
            for cc in range(KC):
                scale_out(BLOCKS - 1, cc)

        @block.gpsimd
        def _(pool):
            def steps(k, p):
                w = PASSES * k + p
                for q in range(Q):
                    pool.wait_ge(soft, 3 * Q * w + 2 * Q + q + 1)
                    nc.gpsimd.tensor_tensor(delta[:, p, q, :], delta[:, p, q, :], relu[:, q, :], ALU.add
                                            ).then_inc(delta_done, 1)
                pool.wait_ge(uc_done, DC * (k + 1))
                for q in range(Q):
                    pool.wait_ge(delta_done, Q * w + q + 1)
                    nc.gpsimd.tensor_tensor(du[:, p, q, :], delta[:, p, q, :], uc[:, k % UCR, Q * p + q, :], ALU.mult
                                            ).then_inc(du_done, 1)

            def inputs(k, p, n):
                m = PASSES * NST * k + p * NST + n
                if n == 0:
                    pool.wait_ge(du_done, Q * (PASSES * k + p + 1))
                if n % NR == 0 and p == 0:
                    pool.wait_ge(bc_in[n // NR], 16 * (k + 1))
                wait(pool, scan_done, Q * (m - DBR + 1))
                row = bc[:, n // NR, 0, n % NR, :].unsqueeze(1).to_broadcast([P, Q, CT])
                nc.gpsimd.tensor_tensor(dbu[:, m % DBR], du[:, p], row, ALU.mult).then_inc(dbu_done, 1)

            steps(0, 0)
            for k in range(BLOCKS):
                for i in range(PASSES * NST):
                    inputs(k, *divmod(i, NST))
                    if i == STEP_AT:
                        steps(k, 1)
                    if k + 1 < BLOCKS and i == NEXT_STEP_AT:
                        steps(k + 1, 0)

        @block.vector
        def _(dve):
            def tap(k, dc, t):
                if t == 0:
                    dve.wait_ge(bank_free[dc % 2], USES["u", k, dc])
                else:
                    dve.wait_ge(conv, (TAPS - 1) * (DC * k + dc) + t)
                lo = (k % HALVES) * CT + t
                nc.vector.scalar_tensor_tensor(uc[:, k % UCR, dc, :], u[:, dc, lo:lo + CT],
                                               cw[:, k // HALVES % 2, dc, t:t + 1], uc[:, k % UCR, dc, :],
                                               ALU.mult, ALU.add).then_inc(conv, 1)

            def silu(k, dc):
                dve.wait_ge(th_done, DC * k + dc + 1)
                nc.vector.scalar_tensor_tensor(uc[:, k % UCR, dc, :], th[:, dc % 2, :], 1.0, uc[:, k % UCR, dc, :],
                                               ALU.add, ALU.mult).then_inc(uc_done, 1)

            def gate_in(k, p, q):
                dve.wait_ge(thz_done, Q * (PASSES * k + p) + q + 1)
                wait(dve, yg_done, Q * (PASSES * (k - 1) + p) + q + 1)
                nc.vector.scalar_tensor_tensor(sz[:, p, q, :], thz[:, q, :], 1.0, pb[:, 1, :], ALU.add, ALU.mult
                                               ).then_inc(bank_free[1], 1)

            def skip_add(k, p, q):
                dc = Q * p + q
                dve.wait_ge(ysum_done, UB * k + (p + 1) * NST * Q - Q + q + 1)
                nc.vector.scalar_tensor_tensor(uc[:, k % UCR, dc, :], uc[:, k % UCR, dc, :],
                                               dp[:, k // HALVES % 2, dc],
                                               ysum[:, q, :], ALU.mult, ALU.add).then_inc(y_read, 1)

            def gate_out(k, p, q):
                dc = Q * p + q
                dve.wait_ge(y_read, Q * (PASSES * k + p) + q + 1)
                nc.vector.tensor_tensor(uc[:, k % UCR, dc, :], uc[:, k % UCR, dc, :], sz[:, p, q, :], ALU.mult
                                        ).then_inc(yg_done, 1)

            def scan(k, p, n):
                h = k % HALVES
                for q in range(Q):
                    dc = Q * p + q
                    m = PASSES * NST * k + p * NST + n
                    s = m * Q + q
                    dve.wait_ge(da_done, s + 1)
                    if q == 0:
                        dve.wait_ge(dbu_done, m + 1)
                    nc.vector.tensor_tensor_scan(hs[:, s % HSR, :], hs[:, s % HSR, :], dbu[:, m % DBR, q, :],
                                                 0.0 if h == 0 else carry[:, dc, n:n + 1], ALU.mult, ALU.add
                                                 ).then_inc(scan_done, 1)

            def keep(k, p, n, q):
                s = UB * k + (p * NST + n) * Q + q
                dve.wait_ge(scan_done, s + 1)
                nc.vector.tensor_copy(carry[:, Q * p + q, n:n + 1], hs[:, s % HSR, CT - 1:CT]).then_inc(carried, 1)

            def weigh(k, p, n, q):
                s = UB * k + (p * NST + n) * Q + q
                dve.wait_ge(scan_done, s + 1)
                if n % NR == 0 and p == 0 and q == 0:
                    dve.wait_ge(bc_in[n // NR], 16 * (k + 1))
                wait(dve, ysum_done, s - HCR + 1)
                nc.vector.tensor_tensor(hc[:, s % HCR, :], hs[:, s % HSR, :], bc[:, n // NR, 1, n % NR, :], ALU.mult
                                        ).then_inc(hc_done, 1)

            def between(k, j):
                if k + 1 < BLOCKS:
                    for dc in range(DC):
                        if j - TAP_AT[dc] in range(TAPS - 1):
                            tap(k + 1, dc, j - TAP_AT[dc])
                        if j == SILU_AT[dc]:
                            silu(k + 1, dc)
                    if j in NEXT_GATE_AT:
                        gate_in(k + 1, 0, NEXT_GATE_AT.index(j))
                if j in GATE_AT:
                    gate_in(k, 1, GATE_AT.index(j))
                if k > 0 and j in ADD_AT:
                    skip_add(k - 1, 1, ADD_AT.index(j))
                if k > 0 and j in GATE_OUT_AT:
                    gate_out(k - 1, 1, GATE_OUT_AT.index(j))
                if j - 2 * NST in ADD_AT:
                    skip_add(k, 0, ADD_AT.index(j - 2 * NST))
                if j - 2 * NST in GATE_OUT_AT:
                    gate_out(k, 0, GATE_OUT_AT.index(j - 2 * NST))

            nc.vector.memset(u[:, :, 0:TAPS - 1], 0.0).then_inc(zeroed, 1)
            dve.wait_ge(vecs, 16)
            nc.vector.tensor_scalar(cw[:], cw[:], 0.5, None, ALU.mult).then_inc(zeroed, 1)
            nc.vector.tensor_scalar(cb[:], cb[:], 0.5, None, ALU.mult).then_inc(zeroed, 1)
            dve.wait_ge(neg_done, 1)
            dve.wait_ge(zeroed, 3)
            nc.vector.tensor_scalar(neg_a[:], neg_a[:], -1.0, None, ALU.mult).then_inc(neg_done, 1)
            for dc in range(DC):
                for t in range(TAPS - 1):
                    tap(0, dc, t)
                silu(0, dc)
            for q in range(Q):
                gate_in(0, 0, q)
            for k in range(BLOCKS):
                for i in range(PASSES * NST):
                    p, n = divmod(i, NST)
                    scan(k, p, n)
                    between(k, 2 * i)
                    for q in range(Q):
                        if k % HALVES == 0:
                            keep(k, p, n, q)
                        weigh(k, p, n, q)
                    between(k, 2 * i + 1)
            for q in range(Q):
                skip_add(BLOCKS - 1, 1, q)
            for q in range(Q):
                gate_out(BLOCKS - 1, 1, q)


def mamba_inputs(i):
    g = {k[8:]: np.asarray(v) for k, v in i.items() if k.startswith("L0_attn_")}

    def both(f):
        return np.stack([f(g, "_f"), f(g, "_b")])

    def cols(v):
        return np.ascontiguousarray(np.moveaxis(v.reshape(DC, P, *v.shape[1:]), 0, 1))

    r = {
        "inw": both(lambda g, d: rows(g["inproj" + d])), "xw": both(lambda g, d: rows(g["xproj" + d])),
        "dtw": both(lambda g, d: g["dt_w" + d]), "outw": both(lambda g, d: rows(g["outproj" + d])),
        "vecs": np.ascontiguousarray(np.stack([np.concatenate(
            [cols(v if v.ndim == 2 else v[:, None]) for v in (g[n + d] for n in ("Alog", "conv_w", "conv_b", "dt_b", "Dp"))],
            axis=2) for d in ("_f", "_b")], axis=1)),
    }
    return r


def mix_phase(nc, a, y_all, x1_t):
    with ExitStack() as ctx:
        def sb(name, shape):
            return ctx.enter_context(nc.sbuf_tensor("mix_" + name, shape, F32))

        def ps(name, shape):
            return ctx.enter_context(nc.psum_tensor("mix_" + name, shape, F32))

        def sem(name):
            return ctx.enter_context(nc.semaphore("mix_" + name))

        NC = TOKENS // CT
        gw, pw = sb("gw", [P, 2 * KC, DM]), sb("pw", [P, KC, DM])
        gb, prb = sb("gb", [P, KC]), sb("prb", [P, KC])
        yf, yb, xt = (sb(n, [P, KC, TOKENS]) for n in ("yf", "yb", "xt"))
        gate, dif, y = (sb(n, [P, 2, KC, CT]) for n in ("gate", "dif", "y"))
        res = sb("res", [P, 2, KC, CT])
        pg, pp = ps("pg", [P, 2, KC, CT]), ps("pp", [P, 2, KC, CT])

        loaded_w = sem("loaded_w")
        loaded_y = [sem(f"loaded_y{b}") for b in range(BATCH)]
        gate_mm, gate_done, dif_done, mul_done, y_done = (sem(n) for n in ("gate_mm", "gate_done", "dif_done", "mul_done", "y_done"))
        proj_mm, res_done = sem("proj_mm"), sem("res_done")
        stored = [sem(f"stored{s}") for s in range(2)]

        def backward(t, k, c):
            b, h = divmod(c, SEQ // CT)
            lo = b * SEQ + (SEQ // CT - 1 - h) * CT
            return t[:, k, lo:lo + CT][:, ::-1]

        block = ctx.enter_context(nc.Block())

        @block.sync
        def _(sp):
            for dst, name in ((gw, "gatew"), (pw, "projw"), (gb, "gateb"), (prb, "projb")):
                sp.dma_start(dst[:], a[name]).then_inc(loaded_w, 16)
            for b in range(BATCH):
                for d, t in enumerate((yf, yb)):
                    sp.dma_start(t[:, :, b * SEQ:(b + 1) * SEQ], y_all[2 * b + d]).then_inc(loaded_y[b], 16)
                sp.dma_start(xt[:, :, b * SEQ:(b + 1) * SEQ], a["xT"][:, :, b * SEQ:(b + 1) * SEQ]
                             ).then_inc(loaded_y[b], 16)
            for c in range(NC):
                sp.wait_ge(res_done, KC * (c + 1))
                sp.dma_start(x1_t[:, :, c * CT:(c + 1) * CT], res[:, c % 2]).then_inc(stored[c % 2], 16)
            for slot in stored:
                sp.wait_ge(slot, 16 * NC // 2)

        @block.tensor
        def _(pe):
            def gates(c):
                if c % 2 == 0:
                    pe.wait_ge(loaded_y[c // 2], 3 * 16)
                if c >= 2:
                    pe.wait_ge(gate_done, KC * (c - 1))
                for cc in range(KC):
                    for k in range(2 * KC):
                        rhs = yf[:, k, c * CT:(c + 1) * CT] if k < KC else backward(yb, k - KC, c)
                        mm = nc.tensor.matmul(pg[:, c % 2, cc, :], gw[:, k, cc * P:(cc + 1) * P], rhs,
                                              start=(k == 0), stop=(k == 2 * KC - 1))
                    mm.then_inc(gate_mm, 1)

            def project(c):
                pe.wait_ge(y_done, KC * (c + 1))
                if c >= 2:
                    pe.wait_ge(res_done, KC * (c - 1))
                for cc in range(KC):
                    for k in range(KC):
                        mm = nc.tensor.matmul(pp[:, c % 2, cc, :], pw[:, k, cc * P:(cc + 1) * P], y[:, c % 2, k, :],
                                              start=(k == 0), stop=(k == KC - 1))
                    mm.then_inc(proj_mm, 1)

            pe.wait_ge(loaded_w, 4 * 16)
            for c in range(NC):
                gates(c)
                if c >= 1:
                    project(c - 1)
            project(NC - 1)

        @block.scalar
        def _(act):
            act.wait_ge(loaded_w, 4 * 16)
            for c in range(NC):
                for cc in range(KC):
                    act.wait_ge(gate_mm, KC * c + cc + 1)
                    if c >= 2:
                        act.wait_ge(mul_done, KC * (c - 2) + cc + 1)
                    nc.scalar.activation(gate[:, c % 2, cc, :], pg[:, c % 2, cc, :], ACT.Sigmoid, bias=gb[:, cc:cc + 1]
                                         ).then_inc(gate_done, 1)

        @block.vector
        def _(dve):
            def mix(c):
                for k in range(KC):
                    dve.wait_ge(loaded_y[c // 2], 3 * 16)
                    nc.vector.tensor_tensor(dif[:, c % 2, k, :], yf[:, k, c * CT:(c + 1) * CT], backward(yb, k, c),
                                            ALU.subtract).then_inc(dif_done, 1)
                for k in range(KC):
                    dve.wait_ge(gate_done, KC * c + k + 1)
                    dve.wait_ge(dif_done, KC * c + k + 1)
                    nc.vector.tensor_tensor(dif[:, c % 2, k, :], dif[:, c % 2, k, :], gate[:, c % 2, k, :], ALU.mult
                                            ).then_inc(mul_done, 1)
                for k in range(KC):
                    dve.wait_ge(mul_done, KC * c + k + 1)
                    if c >= 2:
                        dve.wait_ge(proj_mm, KC * (c - 1))
                    nc.vector.tensor_tensor(y[:, c % 2, k, :], dif[:, c % 2, k, :], backward(yb, k, c), ALU.add
                                            ).then_inc(y_done, 1)

            def residual(c):
                for cc in range(KC):
                    dve.wait_ge(proj_mm, KC * c + cc + 1)
                    if c >= 2:
                        dve.wait_ge(stored[c % 2], 16 * (c // 2))
                    nc.vector.scalar_tensor_tensor(res[:, c % 2, cc, :], pp[:, c % 2, cc, :], prb[:, cc:cc + 1],
                                                   xt[:, cc, c * CT:(c + 1) * CT], ALU.add, ALU.add).then_inc(res_done, 1)

            for c in range(NC):
                mix(c)
                if c >= 1:
                    residual(c - 1)
            residual(NC - 1)


def mix_inputs(i):
    g = {k: np.asarray(v) for k, v in i.items()}
    return {"gatew": rows(g["L0_attn_gate_w"]), "projw": rows(g["L0_attn_proj_w"]),
            "gateb": np.ascontiguousarray(g["L0_attn_gate_b"].reshape(KC, P).T),
            "projb": np.ascontiguousarray(g["L0_attn_proj_b"].reshape(KC, P).T)}


NEXP, SLOTS = 64, 32
NP = NEXP * SLOTS
NCH = NP // CT
MT = SEQ // P
JT = CT // P
XPT = P // SLOTS
FAR = 1.0e30


def ffn_phase(nc, a, x1_t, x1_rows, out):
    with ExitStack() as ctx:
        def sb(name, shape):
            return ctx.enter_context(nc.sbuf_tensor("ffn_" + name, shape, F32))

        def ps(name, shape):
            return ctx.enter_context(nc.psum_tensor("ffn_" + name, shape, F32))

        def sem(name):
            return ctx.enter_context(nc.semaphore("ffn_" + name))

        xm_t = sb("xm_t", [P, KC, BATCH, SEQ])
        xm = sb("xm", [P, BATCH, MT, DM])
        et = sb("et", [P, BATCH, JT, SEQ])
        work = et[:].rearrange("p b j s -> p (b j s)")
        x1s = [work[:, u * SEQ:(u + 1) * SEQ] for u in range(4)]
        mag, share, cum, ones = (work[:, (4 + u) * SEQ:(5 + u) * SEQ] for u in range(4))
        below = sb("below", [P, SEQ + 1])
        rv = sb("rv", [P, KC, BATCH])
        stat = sb("stat", [P, 4, 8])
        ident = sb("ident", [P, P])
        phi = sb("phi", [P, KC, NP])
        wt = sb("wt", [P, JT, XPT, KC, DM])
        ebias = sb("ebias", [P, NP // P, DM])
        turn_sb = sb("turn_sb", [P, 2, CT])
        lsb = sb("lsb", [P, 2, BATCH, CT])
        diff, tanh = sb("diff", [P, 2, CT]), sb("tanh", [P, 2, CT])
        disp, ex = sb("disp", [P, 2, BATCH, CT]), sb("ex", [P, 2, BATCH, CT])
        slots = sb("slots", [P, BATCH, KC, CT])
        y = sb("y", [P, JT, BATCH, DM])
        acc = sb("acc", [P, MT, BATCH, DM])
        nmax = sb("nmax", [P, NCH + 1, MT, BATCH])
        lmax = sb("lmax", [P, MT, BATCH])
        drop = sb("drop", [P, NCH, MT, BATCH])
        alpha = sb("alpha", [P, NCH, MT, BATCH])
        part = sb("part", [P, NCH, MT, BATCH])
        den, rden = sb("den", [P, MT, BATCH]), sb("rden", [P, MT, BATCH])
        xres = sb("xres", [P, 2, BATCH, DM])

        lg = ps("lg", [P, BATCH, CT])
        sl = ps("sl", [P, BATCH, KC, CT])
        tb = ps("tb", [P, CT])
        oy = ps("oy", [P, CT])

        loaded_x, loaded_c, loaded_phi, loaded_b = sem("loaded_x"), sem("loaded_c"), sem("loaded_phi"), sem("loaded_b")
        mag_done, exp2_done, xm_done, chain = sem("mag_done"), sem("exp2_done"), sem("xm_done"), sem("chain")
        sum_inv = sem("sum_inv")
        turned = sem("turned")
        turn_read = [sem(f"turn_read{q}") for q in range(2)]
        xrow_stored = [sem(f"xrow_stored{q}") for q in range(2)]
        init_done, alpha_done = sem("init_done"), sem("alpha_done")
        l_done, l_copied, nm_ready, diff_done = sem("l_done"), sem("l_copied"), sem("nm_ready"), sem("diff_done")
        tanh_done, disp_done, exp_done = sem("tanh_done"), sem("disp_done"), sem("exp_done")
        slots_step, sl_act, sl_dve = sem("slots_step"), sem("sl_act"), sem("sl_dve")
        et_turned, et_act, et_dve = sem("et_turned"), sem("et_act"), sem("et_dve")
        y_mm, y_sb = sem("y_mm"), sem("y_sb")
        out_done, acc_done = sem("out_done"), sem("acc_done")
        small = sem("small")
        w_loaded = [sem(f"w_loaded{j}") for j in range(JT)]
        res_loaded = [sem(f"res_loaded{j}") for j in range(2)]
        res_done = sem("res_done")
        stored = [sem(f"stored{s}") for s in range(2)]

        PIECES = [(b, cc) for b in range(BATCH) for cc in range(KC)]

        block = ctx.enter_context(nc.Block())

        @block.sync
        def _(sp):
            for u, (b, cc) in enumerate(PIECES):
                sp.dma_start(x1s[u], x1_t[:, cc, b * SEQ:(b + 1) * SEQ]).then_inc(loaded_x, 16)
            sp.dma_start(rv[:], a["temb_T"]).then_inc(loaded_c, 16)
            sp.dma_start(ident[:], a["ident"]).then_inc(loaded_c, 16)
            sp.dma_start(phi[:], a["phi"]).then_inc(loaded_phi, 16)
            sp.dma_start(ebias[:], a["ebias"]).then_inc(loaded_b, 16)
            for j in range(JT):
                sp.dma_start(wt[:, j], a["ew"][j]).then_inc(w_loaded[j], 16)
            for g in range(MT):
                sp.wait_ge(turn_read[g % 2], g // 2 + 1)
                b, m = divmod(2 * g, MT)
                sp.dma_start(x1_rows[:, b, m:m + 2, :], turn_sb[:, g % 2, :].rearrange("p (m d) -> p m d", m=2)
                             ).then_inc(xrow_stored[g % 2], 16)
            with sp.Fori(1, NCH) as c:
                for j in range(JT):
                    sp.wait_ge(y_mm, JT * (c - 1) + j + 1)
                    sp.dma_start(wt[:, j], a["ew"][bass.ds(c * JT + j, 1)].rearrange("o p n k e -> (o p) n k e")
                                 ).then_inc(w_loaded[j], 16)
            for q in range(2):
                sp.wait_ge(xrow_stored[q], 16 * MT // 2)
            for m in range(MT):
                if m >= 2:
                    sp.wait_ge(stored[m % 2], 16 * (m // 2))
                sp.dma_start(xres[:, m % 2], x1_rows[:, :, m, :]).then_inc(res_loaded[m % 2], 16)
                if m >= 1:
                    sp.wait_ge(res_done, m)
                    sp.dma_start(out[:, (m - 1) * P:m * P, :].rearrange("b p d -> p b d"), xres[:, (m - 1) % 2]
                                 ).then_inc(stored[(m - 1) % 2], 16)
            sp.wait_ge(res_done, MT)
            sp.dma_start(out[:, (MT - 1) * P:MT * P, :].rearrange("b p d -> p b d"), xres[:, (MT - 1) % 2]
                         ).then_inc(stored[(MT - 1) % 2], 16)
            for slot in stored:
                sp.wait_ge(slot, 16 * MT // 2)

        @block.tensor
        def _(pe):
            pe.wait_ge(loaded_c, 32)
            pe.wait_ge(loaded_x, 4 * 16)
            banks = [tb, oy]
            for g in range(2 * MT):
                b, m = divmod(2 * (g % MT), MT)
                if g >= MT:
                    pe.wait_ge(xm_done, KC * b + KC)
                if g >= 2:
                    pe.wait_ge(turn_read[g % 2], g // 2)
                for q in range(4):
                    cc, mm_ = q % 2, m + q // 2
                    src = x1s[KC * b + cc] if g < MT else xm_t[:, cc, b, :]
                    mm = nc.tensor.transpose(banks[g % 2][:, q * P:(q + 1) * P], src[:, mm_ * P:(mm_ + 1) * P], ident[:])
                mm.then_inc(turned, 1)
            for q in range(2):
                pe.wait_ge(turn_read[q], MT)
            pe.wait_ge(loaded_phi, 16)

            def logits(c, m):
                wait(pe, l_copied, BATCH * (MT * c + m))
                for b in range(BATCH):
                    for k in range(KC):
                        mm = nc.tensor.matmul(lg[:, b, :], xm_t[:, k, b, m * P:(m + 1) * P],
                                              phi[:, k, bass.ds(c * CT, CT)], start=(k == 0), stop=(k == KC - 1))
                    mm.then_inc(l_done, 1)

            def combine(c, m):
                if m == 0:
                    pe.wait_ge(y_sb, JT * (c + 1))
                else:
                    wait(pe, acc_done, MT * c + m)
                for b in range(BATCH):
                    for j in range(JT):
                        mm = nc.tensor.matmul(oy[:, b * DM:(b + 1) * DM], et[:, b, j, m * P:(m + 1) * P], y[:, j, b, :],
                                              start=(j == 0), stop=(j == JT - 1))
                mm.then_inc(out_done, 1)

            def gather(c, m, b):
                pe.wait_ge(disp_done, 2 * (MT * c + m) + b + 1)
                if m == 0 and b == 0:
                    wait(pe, sl_act, KC * c)
                    wait(pe, sl_dve, KC * c)
                for cc in range(KC):
                    mm = nc.tensor.matmul(sl[:, b, cc, :], xm[:, b, m, cc * P:(cc + 1) * P], disp[:, m % 2, b, :],
                                          start=(m == 0), stop=(m == MT - 1))
                if b == BATCH - 1:
                    mm.then_inc(slots_step, 1)

            def turn(c, m, b):
                pe.wait_ge(exp_done, 2 * (MT * c + m) + b + 1)
                if b == 0:
                    wait(pe, et_dve, MT * c + m)
                    if m == 0:
                        wait(pe, y_sb, JT * c)
                else:
                    pe.wait_ge(et_act, MT * c + m + 1)
                for j in range(JT):
                    mm = nc.tensor.transpose(tb[:, j * P:(j + 1) * P], ex[:, m % 2, b, j * P:(j + 1) * P], ident[:])
                mm.then_inc(et_turned, 1)

            def tile_rest(c, m):
                gather(c, m, 0)
                turn(c, m, 0)
                gather(c, m, 1)
                turn(c, m, 1)

            def experts(c, j):
                pe.wait_ge(w_loaded[j], 16 * (c + 1))
                if j == 0:
                    pe.wait_ge(sl_act, KC * (c + 1))
                    pe.wait_ge(sl_dve, KC * (c + 1))
                    wait(pe, acc_done, MT * c)
                elif j == 1:
                    pe.wait_ge(et_dve, MT * (c + 1))
                else:
                    pe.wait_ge(y_sb, JT * c + j - 1)
                bank = oy if j % 2 == 0 else tb
                for b in range(BATCH):
                    for k in range(KC):
                        for n in range(XPT):
                            mm = nc.tensor.matmul(bank[n * SLOTS:(n + 1) * SLOTS, b * DM:(b + 1) * DM],
                                                  slots[:, b, k, j * P + n * SLOTS:j * P + (n + 1) * SLOTS],
                                                  wt[:, j, n, k, :], start=(k == 0), stop=(k == KC - 1),
                                                  tile_position=(0, n * SLOTS))
                mm.then_inc(y_mm, 1)

            def chunk(c, first):
                for m in range(MT):
                    logits(c, m)
                    if not first:
                        combine(c - 1, m)
                    if m >= 1:
                        tile_rest(c, m - 1)
                gather(c, MT - 1, 0)
                gather(c, MT - 1, 1)
                turn(c, MT - 1, 0)
                turn(c, MT - 1, 1)
                for j in range(JT):
                    experts(c, j)

            chunk(0, True)
            with pe.Fori(1, NCH) as c:
                chunk(c, False)
            for m in range(MT):
                combine(NCH - 1, m)

        @block.scalar
        def _(act):
            def turned_out(g):
                b, m = divmod(2 * (g % MT), MT)
                act.wait_ge(turned, g + 1)
                bank = (tb, oy)[g % 2]
                if g < MT:
                    if g >= 2:
                        act.wait_ge(xrow_stored[g % 2], 16 * (g // 2))
                    nc.scalar.activation(turn_sb[:, g % 2, :], bank[:], ACT.Copy).then_inc(turn_read[g % 2], 1)
                else:
                    nc.scalar.activation(xm[:, b, m:m + 2, :], bank[:].rearrange("p (m d) -> p m d", m=2), ACT.Copy
                                         ).then_inc(turn_read[g % 2], 1)

            act.wait_ge(loaded_x, 4 * 16)
            for u in range(len(PIECES)):
                if u >= 1:
                    act.wait_ge(xm_done, u)
                nc.scalar.activation(mag, x1s[u], ACT.Abs, accum_out=stat[:, u, 0:1]).then_inc(mag_done, 1)
                act.wait_ge(sum_inv, u + 1)
                nc.scalar.activation(share, mag, ACT.Exp, scale=stat[:, u, 2:3],
                                     accum_out=stat[:, u, 3:4]).then_inc(exp2_done, 1)
                turned_out(2 * u)
                turned_out(2 * u + 1)
            for g in range(MT + 1, 2 * MT, 2):
                turned_out(g)

            def turn_out(c, m):
                act.wait_ge(et_turned, 2 * (MT * c + m) + 1)
                wait(act, out_done, MT * (c - 1) + m + 1)
                nc.scalar.activation(et[:, 0, :, m * P:(m + 1) * P], tb[:].rearrange("p (j s) -> p j s", j=JT),
                                     ACT.Copy).then_inc(et_act, 1)

            def chunk(c):
                for m in range(MT):
                    t = MT * c + m
                    wait(act, diff_done, t - 1)
                    for b in range(BATCH):
                        act.wait_ge(l_done, BATCH * t + b + 1)
                        nc.scalar.activation(lsb[:, m % 2, b, :], lg[:, b, :], ACT.Copy).then_inc(l_copied, 1)
                    act.wait_ge(diff_done, t + 1)
                    wait(act, disp_done, 2 * (t - 1))
                    nc.scalar.activation(tanh[:, m % 2, :], diff[:, m % 2, :], ACT.Tanh, scale=0.5
                                         ).then_inc(tanh_done, 1)
                    act.wait_ge(nm_ready, t + 1)
                    wait(act, et_turned, 2 * (t - 1))
                    for b in range(BATCH):
                        nc.scalar.activation(ex[:, m % 2, b, :], lsb[:, m % 2, b, :], ACT.Exp,
                                             bias=nmax[:, bass.ds(c + 1, 1), m, b],
                                             accum_out=part[:, bass.ds(c, 1), m, b]).then_inc(exp_done, 1)
                    nc.scalar.activation(alpha[:, bass.ds(c, 1), m, :], drop[:, bass.ds(c, 1), m, :], ACT.Exp
                                         ).then_inc(alpha_done, 1)
                    if m >= 1:
                        turn_out(c, m - 1)
                turn_out(c, MT - 1)
                act.wait_ge(slots_step, MT * (c + 1))
                wait(act, y_mm, JT * c)
                for cc in range(KC):
                    nc.scalar.activation(slots[:, 0, cc, :], sl[:, 0, cc, :], ACT.Copy).then_inc(sl_act, 1)

            act.wait_ge(init_done, 2)
            chunk(0)
            with act.Fori(1, NCH) as c:
                chunk(c)

        @block.gpsimd
        def _(pool):
            nc.gpsimd.memset(nmax[:, 0], FAR).then_inc(init_done, 1)
            nc.gpsimd.memset(acc[:], 0.0).then_inc(init_done, 1)

        @block.vector
        def _(dve):
            links = [0]

            def link(ins):
                links[0] += 1
                ins.then_inc(chain, 1)
                dve.wait_ge(chain, links[0])

            link(nc.vector.memset(ones, 1.0))
            link(nc.vector.memset(below[:, 0:1], 1.0))
            dve.wait_ge(loaded_c, 32)
            for u, (b, cc) in enumerate(PIECES):
                s = stat[:, u, :]
                dve.wait_ge(mag_done, u + 1)
                link(nc.vector.reciprocal(s[:, 1:2], s[:, 0:1]))
                nc.vector.tensor_scalar(s[:, 2:3], s[:, 1:2], 2.0, None, ALU.mult).then_inc(sum_inv, 1)
                dve.wait_ge(exp2_done, u + 1)
                link(nc.vector.reciprocal(s[:, 4:5], s[:, 3:4]))
                link(nc.vector.tensor_scalar(share, share, s[:, 4:5], None, ALU.mult))
                link(nc.vector.tensor_tensor_scan(cum, ones, share, 0.0, ALU.mult, ALU.add))
                link(nc.vector.tensor_scalar(below[:, 1:SEQ + 1], cum, 0.001, rv[:, cc, b:b + 1], ALU.add, ALU.is_le))
                link(nc.vector.tensor_tensor(cum, below[:, 0:SEQ], below[:, 1:SEQ + 1], ALU.subtract))
                link(nc.vector.tensor_tensor_reduce(share, mag, cum, 1.0, 0.0, ALU.mult, ALU.add, s[:, 5:6]))
                link(nc.vector.tensor_scalar(s[:, 6:7], below[:, SEQ:SEQ + 1], 3.0e38, s[:, 5:6], ALU.mult, ALU.add))
                nc.vector.scalar_tensor_tensor(xm_t[:, cc, b, :], mag, s[:, 6:7], x1s[u], ALU.is_ge, ALU.mult
                                               ).then_inc(xm_done, 1)
            for g in range(MT, 2 * MT, 2):
                b, m = divmod(2 * (g % MT), MT)
                dve.wait_ge(turned, g + 1)
                nc.vector.tensor_copy(xm[:, b, m:m + 2, :], tb[:].rearrange("p (m d) -> p m d", m=2)
                                      ).then_inc(turn_read[0], 1)

            def turn_out(c, m):
                dve.wait_ge(et_turned, 2 * (MT * c + m) + 2)
                wait(dve, out_done, MT * (c - 1) + m + 1)
                nc.vector.tensor_copy(et[:, 1, :, m * P:(m + 1) * P], tb[:].rearrange("p (j s) -> p j s", j=JT)
                                      ).then_inc(et_dve, 1)

            def add_output(c, m):
                dve.wait_ge(out_done, MT * c + m + 1)
                dve.wait_ge(alpha_done, MT * c + m + 1)
                for b in range(BATCH):
                    last = nc.vector.scalar_tensor_tensor(acc[:, m, b, :], acc[:, m, b, :], alpha[:, bass.ds(c, 1), m, b],
                                                          oy[:, b * DM:(b + 1) * DM], ALU.mult, ALU.add)
                last.then_inc(acc_done, 1)

            def chunk(c, first):
                for m in range(MT):
                    t = MT * c + m
                    dve.wait_ge(l_copied, BATCH * (t + 1))
                    nc.vector.tensor_reduce(lmax[:, m, :], lsb[:, m % 2], AX_X, ALU.max, negate=True).then_inc(small, 1)
                    dve.wait_ge(small, 2 * t + 1)
                    nc.vector.tensor_tensor(nmax[:, bass.ds(c + 1, 1), m, :].rearrange("p o b -> p (o b)"),
                                            nmax[:, bass.ds(c, 1), m, :].rearrange("p o b -> p (o b)"), lmax[:, m, :],
                                            ALU.min).then_inc(small, 1)
                    dve.wait_ge(small, 2 * t + 2)
                    nc.vector.tensor_tensor(drop[:, bass.ds(c, 1), m, :], nmax[:, bass.ds(c + 1, 1), m, :],
                                            nmax[:, bass.ds(c, 1), m, :], ALU.subtract).then_inc(nm_ready, 1)
                    wait(dve, tanh_done, t - 1)
                    nc.vector.tensor_tensor(diff[:, m % 2, :], lsb[:, m % 2, 1, :], lsb[:, m % 2, 0, :], ALU.subtract
                                            ).then_inc(diff_done, 1)
                    if not first:
                        add_output(c - 1, m)
                    dve.wait_ge(tanh_done, t + 1)
                    wait(dve, slots_step, t - 1)
                    for b, sign in enumerate((-0.5, 0.5)):
                        nc.vector.tensor_scalar(disp[:, m % 2, b, :], tanh[:, m % 2, :], sign, 0.5, ALU.mult, ALU.add
                                                ).then_inc(disp_done, 1)
                    if m >= 1:
                        turn_out(c, m - 1)
                turn_out(c, MT - 1)
                dve.wait_ge(slots_step, MT * (c + 1))
                wait(dve, y_mm, JT * c)
                for cc in range(KC):
                    nc.vector.tensor_copy(slots[:, 1, cc, :], sl[:, 1, cc, :]).then_inc(sl_dve, 1)
                for j in range(JT):
                    dve.wait_ge(y_mm, JT * c + j + 1)
                    bank = oy if j % 2 == 0 else tb
                    nc.vector.tensor_tensor(y[:, j], bank[:].rearrange("p (b e) -> p b e", b=BATCH),
                                            ebias[:, bass.ds(c * JT + j, 1), :].to_broadcast([P, BATCH, DM]), ALU.add
                                            ).then_inc(y_sb, 1)

            dve.wait_ge(init_done, 2)
            dve.wait_ge(loaded_b, 16)
            chunk(0, True)
            with dve.Fori(1, NCH) as c:
                chunk(c, False)
            dve.wait_ge(alpha_done, MT * NCH)
            dve.wait_ge(exp_done, 2 * MT * NCH)
            link(nc.vector.tensor_copy(den[:], part[:, 0]))
            for c in range(1, NCH):
                link(nc.vector.tensor_tensor(den[:], den[:], alpha[:, c], ALU.mult))
                link(nc.vector.tensor_tensor(den[:], den[:], part[:, c], ALU.add))
            link(nc.vector.reciprocal(rden[:], den[:]))
            for m in range(MT):
                add_output(NCH - 1, m)
                dve.wait_ge(acc_done, MT * (NCH - 1) + m + 1)
                dve.wait_ge(res_loaded[m % 2], 16 * (m // 2 + 1))
                for b in range(BATCH):
                    last = nc.vector.scalar_tensor_tensor(xres[:, m % 2, b, :], acc[:, m, b, :], rden[:, m, b:b + 1],
                                                          xres[:, m % 2, b, :], ALU.mult, ALU.add)
                last.then_inc(res_done, 1)


def ffn_inputs(i):
    g = {k: np.asarray(v) for k, v in i.items()}
    w = g["L0_ffn_W"].reshape(NP // P, XPT, KC, P, DM).transpose(0, 3, 1, 2, 4)
    b = g["L0_ffn_b"].reshape(NP // P, XPT, 1, DM)
    return {
        "phi": rows(g["L0_ffn_phi"].reshape(DM, NP)), "ew": np.ascontiguousarray(w),
        "ebias": np.broadcast_to(b, (NP // P, XPT, SLOTS, DM)).reshape(NP // P, P, DM).transpose(1, 0, 2),
    }


CONST = {
    "ident": np.eye(P, dtype=np.float32),
    "tri": np.broadcast_to(np.tril(np.ones((EXPERTS, EXPERTS), np.float32), -1)[None], (P, EXPERTS, EXPERTS)),
    "sel": np.repeat(np.eye(EXPERTS, dtype=np.float32)[:, :, None], P, 2),
}


def rows(w, k=P):
    w = np.asarray(w)
    return np.ascontiguousarray(w.reshape(w.shape[0] // k, k, -1).transpose(1, 0, 2))


def moe_inputs(i):
    g = {k: np.asarray(v) for k, v in i.items()}
    return {
        "xT": rows(g["x"].reshape(TOKENS, DM).T), "temb_T": rows(g["cond_1024"].T),
        "router_T": rows(g["L0_cond_router_w"].T), "router_t_T": rows(g["L0_cond_router_t_w"].T),
        "router_bias": g["L0_cond_router_bias"],
        "sw1T": rows(g["L0_cond_sw1"].T), "sw3T": rows(g["L0_cond_sw3"].T), "sw2T": rows(g["L0_cond_sw2"].T),
        "rw1T": rows(g["L0_cond_rw1"].transpose(2, 0, 1).reshape(DM, -1)),
        "rw2T": np.ascontiguousarray(g["L0_cond_rw2"].transpose(2, 0, 1)),
    }


def build(nc, a, out):
    cond = nc.dram_tensor("cond", [GROUPS, P, KC, SEQ], F32).ap()
    bc_rows = nc.dram_tensor("bc_rows", [GROUPS * HALVES, 2 * NST, CT], F32).ap()
    y_all = nc.dram_tensor("y_all", [GROUPS, P, KC, SEQ], F32).ap()
    x1_t = nc.dram_tensor("x1_t", [P, KC, TOKENS], F32).ap()
    x1_rows = nc.dram_tensor("x1_rows", [P, BATCH, MT, DM], F32).ap()
    moe_phase(nc, a, cond)
    mamba_phase(nc, a, cond, bc_rows, y_all)
    mix_phase(nc, a, y_all, x1_t)
    ffn_phase(nc, a, x1_t, x1_rows, out)


def kernel(**inputs):
    from concourse import bacc
    from concourse.bass_utils import run_bass_kernel_spmd

    arrays = {**moe_inputs(inputs), **mamba_inputs(inputs), **mix_inputs(inputs), **ffn_inputs(inputs), **CONST}
    arrays = {f"in_{k}": np.ascontiguousarray(v) for k, v in arrays.items()}
    nc = bacc.Bacc("TRN2", target_bir_lowering=False, num_devices=1)
    a = {k[3:]: nc.dram_tensor(k, v.shape, F32, kind="ExternalInput").ap() for k, v in arrays.items()}
    out = nc.dram_tensor("out", [BATCH, SEQ, DM], F32, kind="ExternalOutput").ap()
    build(nc, a, out)
    r = run_bass_kernel_spmd(nc, [arrays], core_ids=[0])
    return r.results[0]["out"]
```

```python
from contextlib import ExitStack

import numpy as np

import concourse.bass as bass
from concourse import mybir

F32 = mybir.dt.float32
F32R = mybir.dt.float32r
ALU = mybir.AluOpType
ACT = mybir.ActivationFunctionType
AX_X = mybir.AxisListType.X

P = 128
BATCH, SEQ, DM = 2, 1024, 256
TOKENS = BATCH * SEQ
CT = 512
KC = DM // P

SHARED, EXPERTS, EXPERT_H, TOP_K = 512, 8, 128, 2
SU = SHARED // P
UNITS = SU + EXPERTS


def split_products(nc, out, lhs, rhs, first, last):
    for i, (x, y) in enumerate(((0, 0), (0, 1), (1, 0))):
        mm = nc.tensor.matmul(out, lhs[x], rhs[y], start=first and i == 0, stop=last and i == 2)
    return mm


def wait(eng, semaphore, value):
    if isinstance(value, int) and value <= 0:
        return
    eng.wait_ge(semaphore, value)


def moe_phase(nc, a, cond, ahead):
    with ExitStack() as ctx:
        def sb(name, shape, dtype=F32):
            return ctx.enter_context(nc.sbuf_tensor("moe_" + name, shape, dtype))

        def ps(name, shape):
            return ctx.enter_context(nc.psum_tensor("moe_" + name, shape, F32))

        def sem(name):
            return ctx.enter_context(nc.semaphore("moe_" + name))

        NT = TOKENS // P
        CB, NC = SEQ // CT, TOKENS // CT
        TPB = SEQ // P
        HB = 4
        xT = sb("xT", [P, KC, TOKENS])
        sw1, sw3 = sb("sw1", [P, KC, SHARED]), sb("sw3", [P, KC, SHARED])
        sw2 = sb("sw2", [P, SU, DM])
        rw1, rw2 = sb("rw1", [P, KC, EXPERTS * P]), sb("rw2", [P, EXPERTS, DM])
        x_s = [sb(f"x_s{i}", [P, KC, TOKENS], F32R) for i in range(2)]
        w1_s = [sb(f"w1_s{i}", [P, KC, UNITS * P], F32R) for i in range(2)]
        w3_s = [sb(f"w3_s{i}", [P, KC, SHARED], F32R) for i in range(2)]
        w2_s = [sb(f"w2_s{i}", [P, UNITS, DM], F32R) for i in range(2)]
        hid_s = [sb(f"hid_s{i}", [P, HB, CT], F32R) for i in range(2)]
        comb_s = [sb(f"comb_s{i}", [P, CT // P, EXPERTS], F32R) for i in range(2)]
        ident_s = sb("ident_s", [P, P], F32R)
        SPLITS = [(xT[:, :, 0:CT], x_s, (slice(None), slice(0, CT))),
                  (sw1[:], w1_s, (slice(None), slice(0, SHARED))), (sw3[:], w3_s, (slice(None), slice(None))),
                  (sw2[:], w2_s, (slice(0, SU), slice(None)))]
        SPLITS += [(rw1[:, k, :], w1_s, (k, slice(SHARED, UNITS * P))) for k in range(KC)]
        SPLITS += [(rw2[:, e:e + SU, :], w2_s, (slice(SU + e, 2 * SU + e), slice(None))) for e in range(0, EXPERTS, SU)]
        SPLITS += [(xT[:, :, c * CT:(c + 1) * CT], x_s, (slice(None), slice(c * CT, (c + 1) * CT))) for c in range(1, NC)]
        X0, SW1, SW3, SW2, RW1, RW2, X1 = 1, 2, 3, 4, 6, 8, 9

        def part(s, i):
            _, parts, (rows, cols) = SPLITS[s]
            return parts[i][:, rows, cols]
        rout = sb("rout", [P, KC, EXPERTS])
        rout_t = sb("rout_t", [P, KC, EXPERTS])
        temb = sb("temb", [P, KC, BATCH])
        temb_wide = sb("temb_wide", [P, KC, BATCH, P])
        bias = sb("bias", [P, EXPERTS])
        ident, tri = sb("ident", [P, P]), sb("tri", [P, EXPERTS, EXPERTS])
        t_logit = sb("t_logit", [P, BATCH, EXPERTS])
        prob, score, mask, comb = (sb(n, [P, NT, EXPERTS]) for n in ("prob", "score", "mask", "comb"))
        gt, eq = (sb(n, [P, NT, EXPERTS, EXPERTS]) for n in ("gt", "eq"))
        rank = sb("rank", [P, NT, EXPERTS])
        den, rden, big, half = (sb(n, [P, NT]) for n in ("den", "rden", "big", "half"))
        act_h = sb("act_h", [P, 2, CT])
        hid = sb("hid", [P, 2, CT])
        out_sb, rev_sb = sb("out_sb", [P, KC, CT]), sb("rev_sb", [P, KC, CT])
        scratch = sb("scratch", [P, 8])
        first = ps("first", [P, 3, 2, CT])
        second = ps("second", [P, KC, CT])

        loaded_router = sem("loaded_router")
        loaded_x = [sem(f"loaded_x{c}") for c in range(NC)]
        loaded_w = [sem(f"loaded_w{n}") for n in ("sw1", "sw3", "sw2", "rw1", "rw2")]
        high_done, split_done = sem("high_done"), sem("split_done")
        ident_done, hid_high, hid_split = sem("ident_done"), sem("hid_high"), sem("hid_split")
        loaded_tri = sem("loaded_tri")
        wide_made, logits_done, probs_done = sem("wide_made"), sem("logits_done"), sem("probs_done")
        chain = sem("chain")
        t_done, summed, comb_ready = sem("t_done"), sem("summed"), sem("comb_ready")
        first_done, act_done = sem("first_done"), sem("act_done")
        hid_done, hid_used = sem("hid_done"), sem("hid_used")
        second_done, second_read = sem("second_done"), sem("second_read")
        turned_back = sem("turned_back")
        stored = [[sem(f"stored{d}_{cc}") for cc in range(KC)] for d in range(2)]

        logits = first[:, 2, 1, 0:NT * EXPERTS].rearrange("p (t e) -> p t e", e=EXPERTS)
        t_part = first[:, 1, 1, 0:BATCH * EXPERTS].rearrange("p (b e) -> p b e", e=EXPERTS)

        block = ctx.enter_context(nc.Block())

        @block.sync
        def _(sp):
            for dst, src in ((temb, a["temb_T"]), (rout_t, a["router_t_T"]), (rout, a["router_T"])):
                sp.dma_start(dst[:], src).then_inc(loaded_router, 16)
            for c in range(NC):
                sp.dma_start(xT[:, :, c * CT:(c + 1) * CT], a["xT"][:, :, c * CT:(c + 1) * CT]).then_inc(loaded_x[c], 16)
            sp.dma_start(bias[:], a["router_bias"].partition_broadcast(P)).then_inc(loaded_tri, 16)
            for dst, src in ((tri, a["tri"]), (ident, a["ident"])):
                sp.dma_start(dst[:], src).then_inc(loaded_tri, 16)
            for i, (dst, src) in enumerate(((sw1, a["sw1T"]), (sw3, a["sw3T"]), (sw2, a["sw2T"]), (rw1, a["rw1T"]),
                                            (rw2, a["rw2T"]))):
                sp.dma_start(dst[:], src).then_inc(loaded_w[i], 16)
            ahead.load_vectors(sp, a)
            ahead.load_weights(sp, a, 0)
            for c in range(NC):
                b, h = divmod(c, CB)
                if c == 2:
                    for cc in range(KC):
                        sp.wait_ge(stored[0][cc], 16)
                    ahead.load_tokens(sp, cond, 0)
                for cc in range(KC):
                    sp.wait_ge(second_read, KC * c + cc + 1)
                    sp.dma_start(cond[2 * b, :, cc, h * CT:(h + 1) * CT], out_sb[:, cc, :]
                                 ).then_inc(stored[0][cc], 16)
                    sp.wait_ge(turned_back, KC * c + cc + 1)
                    sp.dma_start(cond[2 * b + 1, :, cc, (CB - 1 - h) * CT:(CB - h) * CT], rev_sb[:, cc, :]
                                 ).then_inc(stored[1][cc], 16)
            for slot in stored[0] + stored[1]:
                sp.wait_ge(slot, 16 * NC)

        @block.tensor
        def _(pe):
            pe.wait_ge(loaded_router, 3 * 16)
            pe.wait_ge(wide_made, 1)
            for b in range(BATCH):
                for k in range(KC):
                    mm = nc.tensor.matmul(t_part[:, b, :], temb_wide[:, k, b, :], rout_t[:, k, :],
                                          start=(k == 0), stop=(k == KC - 1))
            mm.then_inc(t_done, 1)
            for t in range(NT):
                if t % (CT // P) == 0:
                    pe.wait_ge(loaded_x[t * P // CT], 16)
                for k in range(KC):
                    mm = nc.tensor.matmul(logits[:, t, :], xT[:, k, t * P:(t + 1) * P], rout[:, k, :],
                                          start=(k == 0), stop=(k == KC - 1))
            mm.then_inc(logits_done, 1)
            pe.wait_ge(ident_done, 1)

            def chunk(c, first_chunk=False):
                xs = [[x_s[i][:, k, bass.ds(c * CT, CT)] for i in range(2)] for k in range(KC)]

                def hidden(u):
                    if first_chunk:
                        pe.wait_ge(split_done, SW3 if u < SU else RW1)
                        if u == 1:
                            pe.wait_ge(summed, 1)
                    elif u == 0:
                        pe.wait_ge(split_done, X1 + c - 1)
                    if u == SU:
                        pe.wait_ge(comb_ready, 2 * (c + 1))
                    pe.wait_ge(hid_done, UNITS * c + u + 1)
                    value, factor = first[:, u % 3, 0, :], first[:, u % 3, 1, :]
                    for k in range(KC):
                        mm = split_products(nc, value, [w[:, k, u * P:(u + 1) * P] for w in w1_s], xs[k], k == 0, k == KC - 1)
                    mm.then_inc(first_done, 1)
                    if u < SU:
                        for k in range(KC):
                            mm = split_products(nc, factor, [w[:, k, u * P:(u + 1) * P] for w in w3_s], xs[k],
                                                k == 0, k == KC - 1)
                    else:
                        for t in range(CT // P):
                            for i in range(2):
                                gates = comb_s[i][:, t, u - SU:u - SU + 1].to_broadcast([P, P])
                                mm = nc.tensor.matmul(factor[:, t * P:(t + 1) * P], gates, ident_s[:],
                                                      start=(i == 0), stop=(i == 1))
                    mm.then_inc(first_done, 1)

                def project(u):
                    if first_chunk:
                        pe.wait_ge(split_done, SW2 if u < SU else RW2)
                    pe.wait_ge(hid_split, UNITS * c + u + 1)
                    for cc in range(KC):
                        if u == 0:
                            wait(pe, second_read, KC * c)
                        mm = split_products(nc, second[:, cc, :], [w[:, u, cc * P:(cc + 1) * P] for w in w2_s],
                                            [h[:, u % HB, :] for h in hid_s], u == 0, u == UNITS - 1)
                        if u == UNITS - 1:
                            mm.then_inc(second_done, 1)
                        elif cc == KC - 1:
                            mm.then_inc(hid_used, 1)

                for u in range(UNITS):
                    hidden(u)
                    if u >= 2:
                        project(u - 2)
                project(UNITS - 2)
                project(UNITS - 1)

            chunk(0, first_chunk=True)
            with pe.Fori(1, NC) as c:
                chunk(c)

        @block.scalar
        def _(act):
            def high(s):
                if s == 0:
                    act.wait_ge(loaded_x[0], 16)
                elif s < X1 - 1:
                    act.wait_ge(loaded_w[(0, 1, 2, 3, 3, 4, 4)[s - 1]], 16)
                else:
                    act.wait_ge(loaded_x[s - X1 + 2], 16)
                nc.scalar.activation(part(s, 0), SPLITS[s][0], ACT.Copy).then_inc(high_done, 1)

            for s in range(SW3):
                high(s)
            act.wait_ge(loaded_tri, 3 * 16)
            nc.scalar.activation(ident_s[:], ident[:], ACT.Copy).then_inc(ident_done, 1)
            act.wait_ge(summed, 1)
            nc.scalar.activation(prob[:], score[:], ACT.Sigmoid).then_inc(probs_done, 1)
            def high_hidden(c, u):
                act.wait_ge(hid_done, UNITS * c + u + 1 + 3)
                if u >= HB:
                    act.wait_ge(hid_used, (UNITS - 1) * c + u - HB + 1)
                else:
                    wait(act, second_done, KC * c)
                nc.scalar.activation(hid_s[0][:, u % HB, :], hid[:, u % 2, :], ACT.Copy).then_inc(hid_high, 1)

            def chunk(c, first_chunk=False):
                for u in range(UNITS):
                    act.wait_ge(first_done, 2 * (UNITS * c + u) + 1)
                    act.wait_ge(hid_done, UNITS * c + u + 2)
                    nc.scalar.activation(act_h[:, u % 2, :], first[:, u % 3, 0, :],
                                         ACT.Silu if u < SU else ACT.Gelu).then_inc(act_done, 1)
                    if first_chunk and SW3 + u < len(SPLITS):
                        high(SW3 + u)
                    if u >= 1:
                        high_hidden(c, u - 1)
                high_hidden(c, UNITS - 1)
                for cc in range(KC):
                    act.wait_ge(second_done, KC * c + cc + 1)
                    wait(act, stored[0][cc], 16 * c)
                    wait(act, turned_back, KC * (c - 1) + cc + 1)
                    nc.scalar.activation(out_sb[:, cc, :], second[:, cc, :], ACT.Copy,
                                         scale=1.0 / (1 + TOP_K)).then_inc(second_read, 1)

            chunk(0, first_chunk=True)
            with act.Fori(1, NC) as c:
                chunk(c)

        @block.gpsimd
        def _(pool):
            for s in range(len(SPLITS)):
                pool.wait_ge(high_done, s + 1)
                nc.gpsimd.tensor_tensor(part(s, 1), SPLITS[s][0], part(s, 0).bitcast(F32), ALU.subtract
                                        ).then_inc(split_done, 1)

        @block.vector
        def _(dve):
            links = [0]

            def link(ins):
                links[0] += 1
                ins.then_inc(chain, 1)
                dve.wait_ge(chain, links[0])

            dve.wait_ge(loaded_router, 3 * 16)
            nc.vector.tensor_copy(temb_wide[:], temb[:].unsqueeze(3).to_broadcast([P, KC, BATCH, P])
                                  ).then_inc(wide_made, 1)
            nc.vector.memset(scratch[:], 0.0).then_inc(hid_done, 3)
            dve.wait_ge(t_done, 1)
            link(nc.vector.tensor_copy(t_logit[:], t_part))
            dve.wait_ge(logits_done, 1)
            for b in range(BATCH):
                step = nc.vector.tensor_tensor(score[:, b * TPB:(b + 1) * TPB, :], logits[:, b * TPB:(b + 1) * TPB, :],
                                               t_logit[:, b, :].unsqueeze(1).to_broadcast([P, TPB, EXPERTS]), ALU.add)
            step.then_inc(summed, 1)
            dve.wait_ge(loaded_tri, 3 * 16)
            dve.wait_ge(probs_done, 1)
            link(nc.vector.tensor_tensor(score[:], prob[:], bias[:].unsqueeze(1).to_broadcast([P, NT, EXPERTS]), ALU.add))
            other = score[:].unsqueeze(2).to_broadcast([P, NT, EXPERTS, EXPERTS])
            own = score[:].unsqueeze(3).to_broadcast([P, NT, EXPERTS, EXPERTS])
            link(nc.vector.tensor_tensor(gt[:], other, own, ALU.is_gt))
            link(nc.vector.tensor_tensor(eq[:], other, own, ALU.is_equal))
            link(nc.vector.tensor_tensor(eq[:], eq[:], tri[:].unsqueeze(1).to_broadcast([P, NT, EXPERTS, EXPERTS]), ALU.mult))
            link(nc.vector.tensor_tensor(gt[:], gt[:], eq[:], ALU.add))
            link(nc.vector.tensor_reduce(rank[:], gt[:], AX_X, ALU.add))
            link(nc.vector.tensor_scalar(mask[:], rank[:], float(TOP_K), None, ALU.is_lt))
            link(nc.vector.tensor_tensor(comb[:], prob[:], mask[:], ALU.mult))
            link(nc.vector.tensor_reduce(den[:], comb[:], AX_X, ALU.add))
            link(nc.vector.tensor_scalar(big[:], den[:], 1e-9, None, ALU.is_gt))
            link(nc.vector.tensor_scalar(half[:], big[:], -1.0 / TOP_K, 1.0 / TOP_K, ALU.mult, ALU.add))
            link(nc.vector.tensor_scalar(den[:], den[:], 1e-9, None, ALU.add))
            link(nc.vector.reciprocal(rden[:], den[:]))
            link(nc.vector.tensor_tensor(rden[:], rden[:], big[:], ALU.mult))
            link(nc.vector.tensor_tensor(comb[:], comb[:], rden[:].unsqueeze(2).to_broadcast([P, NT, EXPERTS]), ALU.mult))
            link(nc.vector.tensor_tensor(mask[:], mask[:], half[:].unsqueeze(2).to_broadcast([P, NT, EXPERTS]), ALU.mult))
            link(nc.vector.tensor_tensor(comb[:], comb[:], mask[:], ALU.add))
            def chunk(c):
                wait(dve, first_done, 2 * UNITS * c)
                whole = comb[:, bass.ds(c * (CT // P), CT // P), :]
                nc.vector.tensor_copy(comb_s[0][:], whole).then_inc(comb_ready, 1)
                dve.wait_ge(comb_ready, 2 * c + 1)
                nc.vector.tensor_tensor(comb_s[1][:], whole, comb_s[0][:].bitcast(F32), ALU.subtract
                                        ).then_inc(comb_ready, 1)

                def low_hidden(u):
                    dve.wait_ge(hid_high, UNITS * c + u + 1)
                    nc.vector.tensor_tensor(hid_s[1][:, u % HB, :], hid[:, u % 2, :], hid_s[0][:, u % HB, :].bitcast(F32),
                                            ALU.subtract).then_inc(hid_split, 1)

                for u in range(UNITS):
                    dve.wait_ge(first_done, 2 * (UNITS * c + u) + 2)
                    dve.wait_ge(act_done, UNITS * c + u + 1)
                    wait(dve, hid_split, UNITS * c + u - 1)
                    nc.vector.tensor_tensor(hid[:, u % 2, :], act_h[:, u % 2, :], first[:, u % 3, 1, :],
                                            ALU.mult).then_inc(hid_done, 1)
                    if u >= 1:
                        low_hidden(u - 1)
                low_hidden(UNITS - 1)
                for cc in range(KC):
                    dve.wait_ge(second_read, KC * c + cc + 1)
                    wait(dve, stored[1][cc], 16 * c)
                    nc.vector.tensor_copy(rev_sb[:, cc, :], out_sb[:, cc, ::-1]).then_inc(turned_back, 1)

            chunk(0)
            with dve.Fori(1, NC) as c:
                chunk(c)


DIN, NST, DTR, TAPS = 512, 16, 16, 4
DC = DIN // P
GROUPS = 2 * BATCH
HALVES = SEQ // CT
PASSES = 2
Q = DC // PASSES
RG = 4
NR = NST // RG
UB = PASSES * NST * Q
BLOCKS = GROUPS * HALVES
HCR = 9
HSR = 4
DBR = 3
UCR = 3

IN_AT = (4, 7, 8, 11)
OUT_AT = (13, 15)
X_AT, DT_AT = 19, (21, 23)
CONV_AT = (9, 11, 13, 15)
TANH_AT = (13, 16, 17, 19)
SCALE_AT = (18, 20)
SOFT_AT = (3, 5)
ROWS_AT, NEXT_SOFT_AT = 22, (25, 27)
ADD_TAP_AT = (11, 12, 14, 16)
STEP_AT, NEXT_STEP_AT = 11, 30
TAP_AT = (18, 23, 27, 30)
SILU_AT = (27, 31, 35, 37)
GATE_AT, NEXT_GATE_AT = (6, 10), (51, 55)
FIRST_GATE_AT = (0, 3)
GATE_OUT_AT = (1, 2)

def bank_uses():
    def feed(k):
        return [(dc % 2, ("u", k, dc)) for dc in range(DC)] + [(0, ("x", k))] + step(k, 0)

    def step(k, p):
        return [use for q in range(Q) for use in ((0, ("dt", k, p, q)), (1, ("z", k, p, q)))]

    order = feed(0)
    for k in range(BLOCKS):
        order += step(k, 1)
        if k + 1 < BLOCKS:
            order += [(dc % 2, ("u", k + 1, dc)) for dc in range(DC)]
        if k > 0:
            order += [(cc, ("out", k - 1, cc)) for cc in range(KC)]
        if k + 1 < BLOCKS:
            order += [(0, ("x", k + 1))] + step(k + 1, 0)
    order += [(cc, ("out", BLOCKS - 1, cc)) for cc in range(KC)]
    uses, count = {}, [0, 0]
    for bank, use in order:
        count[bank] += 1
        uses[use] = count[bank]
    return uses


class GateLoads:
    def __init__(self, nc, ctx):
        self.weights = ctx.enter_context(nc.sbuf_tensor("gate_weights", [P, 2 * KC, DM], F32))
        self.bias = ctx.enter_context(nc.sbuf_tensor("gate_bias", [P, KC], F32))
        self.loaded = ctx.enter_context(nc.semaphore("gate_loaded"))

    def load(self, sp, a):
        for dst, name in ((self.weights, "gatew"), (self.bias, "gateb")):
            sp.dma_start(dst[:], a[name]).then_inc(self.loaded, 16)


class FirstLoads:
    def __init__(self, nc, ctx):
        def sb(name, shape):
            return ctx.enter_context(nc.sbuf_tensor("scan_" + name, shape, F32))

        self.inw = sb("inw", [P, KC, 2 * DIN])
        self.xw = sb("xw", [P, DC, DTR + 2 * NST])
        self.dtw = sb("dtw", [DTR, DIN])
        self.vec = sb("vec", [P, 2, DC, NST + TAPS + 3])
        self.xin = sb("xin", [P, KC, CT])
        self.vecs, self.weights, self.xin_in = (ctx.enter_context(nc.semaphore("scan_" + n)) for n in ("vecs", "weights", "xin_in"))
        self.inw_in = [ctx.enter_context(nc.semaphore(f"scan_inw_in{k}")) for k in range(2)]

    def load_weights(self, sp, a, g):
        for k in range(2):
            sp.dma_start(self.inw[:, :, k * DIN:(k + 1) * DIN], a["inw"][g % 2][:, :, k * DIN:(k + 1) * DIN]
                         ).then_inc(self.inw_in[k], 16)
        for dst, name in ((self.xw, "xw"), (self.dtw, "dtw")):
            sp.dma_start(dst[:], a[name][g % 2]).then_inc(self.weights, 16)

    def load_vectors(self, sp, a):
        sp.dma_start(self.vec[:], a["vecs"]).then_inc(self.vecs, 16)

    def load_tokens(self, sp, cond, k):
        g, h = divmod(k, HALVES)
        sp.dma_start(self.xin[:], cond[g][:, :, h * CT:(h + 1) * CT]).then_inc(self.xin_in, 16)


def mamba_phase(nc, a, cond, bc_rows, y_all, ahead, gates):
    with ExitStack() as ctx:
        def sb(name, shape):
            return ctx.enter_context(nc.sbuf_tensor("scan_" + name, shape, F32))

        def ps(name, shape):
            return ctx.enter_context(nc.psum_tensor("scan_" + name, shape, F32))

        def sem(name):
            return ctx.enter_context(nc.semaphore("scan_" + name))

        inw, xw, dtw, vec, xin = ahead.inw, ahead.xw, ahead.dtw, ahead.vec, ahead.xin
        outw = sb("outw", [P, DC, DM])
        ident = sb("ident", [P, P])
        diag = sb("diag", [P, 2, DC, P])
        neg_a, cw, cb, dtb, dp = (vec[:, :, :, lo:hi] for lo, hi in (
            (0, NST), (NST, NST + TAPS), *((NST + TAPS + j, NST + TAPS + j + 1) for j in range(3))))
        u = sb("u", [P, DC, TAPS - 1 + SEQ])
        uc = sb("uc", [P, UCR, DC, CT])
        first_tap = sb("first_tap", [P, CT])
        th = sb("th", [P, 2, CT])
        thz = sb("thz", [P, Q, CT])
        dbl = sb("dbl", [DTR + 2 * NST, CT])
        delta, du, sz = (sb(n, [P, PASSES, Q, CT]) for n in ("delta", "du", "sz"))
        relu = sb("relu", [P, Q, CT])
        bc = sb("bc", [P, RG, 2, NR, CT])
        dbu = sb("dbu", [P, DBR, Q, CT])
        hc = sb("hc", [P, HCR, CT])
        carry = sb("carry", [P, DC, NST])
        yo = sb("yo", [P, KC, CT])

        ysum = ps("ysum", [P, Q, CT])
        hs = ps("hs", [P, HSR, CT])
        pb = ps("pb", [P, 2, CT])

        vecs, weights, xin_in, inw_in = ahead.vecs, ahead.weights, ahead.xin_in, ahead.inw_in
        outw_in, ident_in = sem("outw_in"), sem("ident_in")
        neg_done, zeroed, diag_done = sem("neg_done"), sem("zeroed"), sem("diag_done")
        bank_ready = [sem(f"bank_ready{i}") for i in range(2)]
        bank_free = [sem(f"bank_free{i}") for i in range(2)]
        u_done, tap_done, tap_added = sem("u_done"), sem("tap_done"), sem("tap_added")
        conv, uc_done, th_done, thz_done = sem("conv"), sem("uc_done"), sem("th_done"), sem("thz_done")
        bc_out = sem("bc_out")
        bc_in = [sem(f"bc_in{r}") for r in range(RG)]
        soft = sem("soft")
        delta_done, du_done = sem("delta_done"), sem("du_done")
        da_done, scan_done, dbu_done, hc_done = sem("da_done"), sem("scan_done"), sem("dbu_done"), sem("hc_done")
        ysum_done, yg_done = sem("ysum_done"), sem("yg_done")
        yo_stored = sem("yo_stored")
        carried = sem("carried")

        USES = bank_uses()

        block = ctx.enter_context(nc.Block())

        def add_tap(engine, eng, k, dc):
            eng.wait_ge(tap_done, DC * k + dc + 1)
            engine.tensor_tensor(uc[:, k % UCR, dc, :], uc[:, k % UCR, dc, :], first_tap[:], ALU.add
                                 ).then_inc(tap_added, 1)

        def steps(engine, eng, k, p):
            w = PASSES * k + p
            for q in range(Q):
                eng.wait_ge(soft, 3 * Q * w + 2 * Q + q + 1)
                engine.tensor_tensor(delta[:, p, q, :], delta[:, p, q, :], relu[:, q, :], ALU.add
                                        ).then_inc(delta_done, 1)
            eng.wait_ge(uc_done, DC * (k + 1))
            for q in range(Q):
                eng.wait_ge(delta_done, Q * w + q + 1)
                engine.tensor_tensor(du[:, p, q, :], delta[:, p, q, :], uc[:, k % UCR, Q * p + q, :], ALU.mult
                                        ).then_inc(du_done, 1)

        @block.sync
        def _(sp):
            def load_outw(g):
                sp.dma_start(outw[:], a["outw"][g % 2]).then_inc(outw_in, 16)

            def rows(k):
                sp.wait_ge(bank_free[0], USES["x", k])
                sp.dma_start(bc_rows[k], dbl[DTR:DTR + 2 * NST, :]).then_inc(bc_out, 16)
                sp.wait_ge(bc_out, 16 * (k + 1))
                for r in range(RG):
                    wait(sp, dbu_done, PASSES * NST * (k - 1) + NST + NR * (r + 1))
                    wait(sp, hc_done, UB * (k - 1) + Q * (NST + NR * (r + 1)))
                    src = bc_rows[k].rearrange("(k r n) t -> r k (n t)", k=2, r=RG)[r]
                    sp.dma_start(bc[:, r].rearrange("p k n t -> p k (n t)"), src.partition_broadcast(P)
                                 ).then_inc(bc_in[r], 16)

            def store(k):
                g, h = divmod(k, HALVES)
                for cc in range(KC):
                    sp.wait_ge(bank_free[cc], USES["out", k, cc])
                sp.dma_start(y_all[g][:, :, h * CT:(h + 1) * CT], yo[:]).then_inc(yo_stored, 16)

            sp.dma_start(ident[:], a["ident"]).then_inc(ident_in, 16)
            load_outw(0)
            rows(0)
            gates.load(sp, a)
            for k in range(BLOCKS):
                g, h = divmod(k, HALVES)
                if k + 1 < BLOCKS:
                    for q in range(Q):
                        sp.wait_ge(bank_ready[0], USES["dt", k, 1, q])
                        sp.wait_ge(bank_ready[1], USES["z", k, 1, q])
                    if h == HALVES - 1:
                        ahead.load_weights(sp, a, g + 1)
                    ahead.load_tokens(sp, cond, k + 1)
                if k > 0:
                    store(k - 1)
                    if h == 0:
                        load_outw(g)
                if k + 1 < BLOCKS:
                    rows(k + 1)
            store(BLOCKS - 1)
            sp.wait_ge(yo_stored, 16 * BLOCKS)

        @block.tensor
        def _(pe):
            def claim(bank, *key):
                wait(pe, bank_free[bank], USES[key] - 1)

            def in_proj(k, dc):
                claim(dc % 2, "u", k, dc)
                if dc == 0:
                    pe.wait_ge(inw_in[0], 16 * (k // HALVES + 1))
                    pe.wait_ge(xin_in, 16 * (k + 1))
                for c in range(KC):
                    mm = nc.tensor.matmul(pb[:, dc % 2, :], inw[:, c, dc * P:(dc + 1) * P], xin[:, c, :],
                                          start=(c == 0), stop=(c == KC - 1))
                mm.then_inc(bank_ready[dc % 2], 1)

            def x_proj(k):
                pe.wait_ge(weights, 32 * (k // HALVES + 1))
                claim(0, "x", k)
                for dc in range(DC):
                    pe.wait_ge(uc_done, DC * k + dc + 1)
                    mm = nc.tensor.matmul(pb[0:DTR + 2 * NST, 0, :], xw[:, dc, :], uc[:, k % UCR, dc, :],
                                          start=(dc == 0), stop=(dc == DC - 1))
                mm.then_inc(bank_ready[0], 1)

            def step_size(k, p, q):
                dc = Q * p + q
                claim(0, "dt", k, p, q)
                nc.tensor.matmul(pb[:, 0, :], dtw[:, dc * P:(dc + 1) * P], dbl[0:DTR, :], start=True, stop=True
                                 ).then_inc(bank_ready[0], 1)

            def z_gate(k, p, q):
                dc = Q * p + q
                claim(1, "z", k, p, q)
                if p == 0 and q == 0:
                    pe.wait_ge(inw_in[1], 16 * (k // HALVES + 1))
                for c in range(KC):
                    mm = nc.tensor.matmul(pb[:, 1, :], inw[:, c, DIN + dc * P:DIN + (dc + 1) * P], xin[:, c, :],
                                          start=(c == 0), stop=(c == KC - 1))
                mm.then_inc(bank_ready[1], 1)

            def dt_z(k, p, q):
                step_size(k, p, q)
                z_gate(k, p, q)

            def out_proj(k, cc, tiles=range(DC)):
                pe.wait_ge(yg_done, DC * k + tiles[-1] + 1)
                if k % HALVES == 0:
                    pe.wait_ge(outw_in, 16 * (k // HALVES + 1))
                claim(cc, "out", k, cc)
                for dc in tiles:
                    mm = nc.tensor.matmul(pb[:, cc, :], outw[:, dc, cc * P:(cc + 1) * P], uc[:, k % UCR, dc, :],
                                          start=(dc == 0), stop=(dc == DC - 1))
                if tiles[-1] == DC - 1:
                    mm.then_inc(bank_ready[cc], 1)

            def add_states(k, p, n):
                for q in range(Q):
                    s = UB * k + (p * NST + n) * Q + q
                    pe.wait_ge(hc_done, s + 1)
                    if n == 0 and q == 0:
                        wait(pe, yg_done, Q * (PASSES * k + p))
                    if n == NST - 1:
                        nc.tensor.matmul(ysum[:, q, :], diag[:, k // HALVES % 2, Q * p + q, :], uc[:, k % UCR, Q * p + q, :],
                                         start=False, stop=False)
                    nc.tensor.matmul(ysum[:, q, :], ident[:], hc[:, s % HCR, :],
                                     start=(n == 0), stop=(n == NST - 1)).then_inc(ysum_done, 1)

            for dc in range(DC):
                in_proj(0, dc)
            x_proj(0)
            for q in range(Q):
                step_size(0, 0, q)
            for q in range(Q):
                z_gate(0, 0, q)
            pe.wait_ge(ident_in, 16)
            pe.wait_ge(diag_done, 2 * DC)
            for k in range(BLOCKS):
                for i in range(PASSES * NST):
                    if i in (0, 1):
                        dt_z(k, 1, i)
                    add_states(k, *divmod(i, NST))
                    if k + 1 < BLOCKS and i in IN_AT:
                        in_proj(k + 1, IN_AT.index(i))
                    if k > 0 and i in OUT_AT:
                        out_proj(k - 1, OUT_AT.index(i))
                    if k + 1 < BLOCKS and i == X_AT:
                        x_proj(k + 1)
                    if k + 1 < BLOCKS and i in DT_AT:
                        dt_z(k + 1, 0, DT_AT.index(i))
                    if k + 1 == BLOCKS and i in DT_AT:
                        out_proj(k, DT_AT.index(i), range(Q))
            for cc in range(KC):
                out_proj(BLOCKS - 1, cc, range(Q, DC))

        @block.scalar
        def _(act):
            def conv_in(k, dc):
                v = k // HALVES % 2
                bank = dc % 2
                act.wait_ge(bank_ready[bank], USES["u", k, dc])
                lo = TAPS - 1 + (k % HALVES) * CT
                nc.scalar.activation(u[:, dc, lo:lo + CT], pb[:, bank, :], ACT.Copy).then_inc(u_done, 1)
                nc.scalar.activation(uc[:, k % UCR, dc, :], pb[:, bank, :], ACT.Identity,
                                     scale=cw[:, v, dc, TAPS - 1:TAPS], bias=cb[:, v, dc]
                                     ).then_inc(bank_free[bank], 1)
                act.wait_ge(u_done, DC * k + dc + 1)
                wait(act, tap_added, DC * k + dc)
                nc.scalar.activation(first_tap[:], u[:, dc, lo - TAPS + 1:lo - TAPS + 1 + CT], ACT.Copy,
                                     scale=cw[:, v, dc, 0:1]).then_inc(tap_done, 1)

            def conv_tanh(k, dc):
                act.wait_ge(conv, (TAPS - 2) * (DC * k + dc + 1))
                wait(act, uc_done, DC * k + dc - 1)
                nc.scalar.activation(th[:, dc % 2, :], uc[:, k % UCR, dc, :], ACT.Tanh).then_inc(th_done, 1)

            def copy_rows(k):
                act.wait_ge(bank_ready[0], USES["x", k])
                wait(act, bc_out, 16 * k)
                nc.scalar.activation(dbl[:], pb[0:DTR + 2 * NST, 0, :], ACT.Copy).then_inc(bank_free[0], 1)

            def soft_in(k, p, q):
                dc = Q * p + q
                w = PASSES * k + p
                act.wait_ge(bank_ready[0], USES["dt", k, p, q])
                bias = dtb[:, k // HALVES % 2, dc]
                wait(act, delta_done, Q * (w - 1) + q + 1)
                wait(act, du_done, Q * (w - PASSES) + q + 1)
                nc.scalar.activation(delta[:, p, q, :], pb[:, 0, :], ACT.Abs, bias=bias).then_inc(soft, 1)
                nc.scalar.activation(relu[:, q, :], pb[:, 0, :], ACT.Relu, bias=bias).then_inc(bank_free[0], 1)

            def gate_tanh(k, p, q):
                act.wait_ge(bank_ready[1], USES["z", k, p, q])
                wait(act, bank_free[1], USES["z", k, p, q] - 1)
                nc.scalar.activation(thz[:, q, :], pb[:, 1, :], ACT.Tanh, scale=0.5).then_inc(thz_done, 1)

            def soft_exp(k, p, q):
                w = PASSES * k + p
                act.wait_ge(soft, 3 * Q * w + 2 * q + 1)
                nc.scalar.activation(delta[:, p, q, :], delta[:, p, q, :], ACT.Exp, scale=-1.0).then_inc(soft, 1)

            def soft_step(k, p, q):
                soft_in(k, p, q)
                gate_tanh(k, p, q)
                soft_exp(k, p, q)

            def soft_ln(k, p):
                w = PASSES * k + p
                for q in range(Q):
                    act.wait_ge(soft, 3 * Q * w + 2 * q + 2)
                    nc.scalar.activation(delta[:, p, q, :], delta[:, p, q, :], ACT.Ln, bias=1.0).then_inc(soft, 1)

            def keep(m):
                k, i = divmod(m, PASSES * NST)
                if m >= 0 and k % HALVES == 0:
                    p, n = divmod(i, NST)
                    act.wait_ge(hc_done, Q * (m + 1))
                    lo = Q * m % HSR
                    nc.scalar.activation(carry[:, Q * p:Q * (p + 1), n:n + 1], hs[:, lo:lo + Q, CT - 1:CT], ACT.Copy
                                         ).then_inc(carried, 1)
                    act.wait_ge(carried, PASSES * NST * (k // HALVES) + i + 1)

            def decay(k, p, n):
                m = PASSES * NST * k + p * NST + n
                keep(m - HSR // Q)
                if n == 0:
                    act.wait_ge(delta_done, Q * (PASSES * k + p + 1))
                for q in range(Q):
                    s = UB * k + (p * NST + n) * Q + q
                    wait(act, hc_done, s - HSR + 1)
                    nc.scalar.activation(hs[:, s % HSR, :], delta[:, p, q, :], ACT.Exp,
                                         scale=neg_a[:, k // HALVES % 2, Q * p + q, n:n + 1]).then_inc(da_done, 1)

            def scale_out(k, cc):
                wait(act, yo_stored, 16 * k)
                act.wait_ge(bank_ready[cc], USES["out", k, cc])
                nc.scalar.activation(yo[:, cc, :], pb[:, cc, :], ACT.Copy, scale=0.5).then_inc(bank_free[cc], 1)

            act.wait_ge(vecs, 16)
            act.wait_ge(zeroed, 3)
            nc.scalar.activation(neg_a[:], neg_a[:], ACT.Exp).then_inc(neg_done, 1)
            for dc in range(DC):
                conv_in(0, dc)
                if dc >= 1:
                    conv_tanh(0, dc - 1)
            conv_tanh(0, DC - 1)
            copy_rows(0)
            for q in range(Q):
                soft_in(0, 0, q)
                soft_exp(0, 0, q)
            soft_ln(0, 0)
            act.wait_ge(neg_done, 2)
            for k in range(BLOCKS):
                for i in range(PASSES * NST):
                    decay(k, *divmod(i, NST))
                    if k == 0 and i < Q:
                        gate_tanh(0, 0, i)
                    if i in SOFT_AT:
                        soft_step(k, 1, SOFT_AT.index(i))
                    if i == SOFT_AT[-1]:
                        soft_ln(k, 1)
                    if k + 1 < BLOCKS:
                        if i in CONV_AT:
                            conv_in(k + 1, CONV_AT.index(i))
                        if i in TANH_AT:
                            conv_tanh(k + 1, TANH_AT.index(i))
                    if k > 0 and i in SCALE_AT:
                        scale_out(k - 1, SCALE_AT.index(i))
                    if k + 1 < BLOCKS:
                        if i == ROWS_AT:
                            copy_rows(k + 1)
                        if i in NEXT_SOFT_AT:
                            soft_step(k + 1, 0, NEXT_SOFT_AT.index(i))
                        if i == NEXT_SOFT_AT[-1] + 1:
                            soft_ln(k + 1, 0)
            for cc in range(KC):
                scale_out(BLOCKS - 1, cc)

        @block.gpsimd
        def _(pool):
            def inputs(k, p, n):
                m = PASSES * NST * k + p * NST + n
                if n == 0:
                    pool.wait_ge(du_done, Q * (PASSES * k + p + 1))
                if n % NR == 0 and p == 0:
                    pool.wait_ge(bc_in[n // NR], 16 * (k + 1))
                wait(pool, scan_done, Q * (m - DBR + 1))
                row = bc[:, n // NR, 0, n % NR, :].unsqueeze(1).to_broadcast([P, Q, CT])
                nc.gpsimd.tensor_tensor(dbu[:, m % DBR], du[:, p], row, ALU.mult).then_inc(dbu_done, 1)

            for k in range(BLOCKS):
                for i in range(PASSES * NST):
                    inputs(k, *divmod(i, NST))
                    if k + 1 < BLOCKS and i in ADD_TAP_AT:
                        add_tap(nc.gpsimd, pool, k + 1, ADD_TAP_AT.index(i))
                    if i == STEP_AT:
                        steps(nc.gpsimd, pool, k, 1)
                    if k + 1 < BLOCKS and i == NEXT_STEP_AT:
                        steps(nc.gpsimd, pool, k + 1, 0)

        @block.vector
        def _(dve):
            def tap(k, dc, t):
                if t == 1:
                    dve.wait_ge(tap_added, DC * k + dc + 1)
                else:
                    dve.wait_ge(conv, (TAPS - 2) * (DC * k + dc) + t - 1)
                lo = (k % HALVES) * CT + t
                nc.vector.scalar_tensor_tensor(uc[:, k % UCR, dc, :], u[:, dc, lo:lo + CT],
                                               cw[:, k // HALVES % 2, dc, t:t + 1], uc[:, k % UCR, dc, :],
                                               ALU.mult, ALU.add).then_inc(conv, 1)

            def silu(k, dc):
                dve.wait_ge(th_done, DC * k + dc + 1)
                nc.vector.scalar_tensor_tensor(uc[:, k % UCR, dc, :], th[:, dc % 2, :], 1.0, uc[:, k % UCR, dc, :],
                                               ALU.add, ALU.mult).then_inc(uc_done, 1)

            def gate_in(k, p, q):
                dve.wait_ge(thz_done, Q * (PASSES * k + p) + q + 1)
                wait(dve, yg_done, Q * (PASSES * (k - 1) + p) + q + 1)
                nc.vector.scalar_tensor_tensor(sz[:, p, q, :], thz[:, q, :], 1.0, pb[:, 1, :], ALU.add, ALU.mult
                                               ).then_inc(bank_free[1], 1)

            def gate_out(k, p, q):
                dc = Q * p + q
                dve.wait_ge(ysum_done, UB * k + (p + 1) * NST * Q - Q + q + 1)
                nc.vector.tensor_tensor(uc[:, k % UCR, dc, :], ysum[:, q, :], sz[:, p, q, :], ALU.mult
                                        ).then_inc(yg_done, 1)

            def scan(k, p, n):
                h = k % HALVES
                for q in range(Q):
                    dc = Q * p + q
                    m = PASSES * NST * k + p * NST + n
                    s = m * Q + q
                    dve.wait_ge(da_done, s + 1)
                    if q == 0:
                        dve.wait_ge(dbu_done, m + 1)
                        if h == 1:
                            dve.wait_ge(carried, PASSES * NST * (k // HALVES) + p * NST + n + 1)
                    nc.vector.tensor_tensor_scan(hs[:, s % HSR, :], hs[:, s % HSR, :], dbu[:, m % DBR, q, :],
                                                 0.0 if h == 0 else carry[:, dc, n:n + 1], ALU.mult, ALU.add
                                                 ).then_inc(scan_done, 1)

            def weigh(k, p, n, q):
                s = UB * k + (p * NST + n) * Q + q
                dve.wait_ge(scan_done, s + 1)
                if n % NR == 0 and p == 0 and q == 0:
                    dve.wait_ge(bc_in[n // NR], 16 * (k + 1))
                wait(dve, ysum_done, s - HCR + 1)
                nc.vector.tensor_tensor(hc[:, s % HCR, :], hs[:, s % HSR, :], bc[:, n // NR, 1, n % NR, :], ALU.mult
                                        ).then_inc(hc_done, 1)

            def between(k, j):
                if k + 1 < BLOCKS:
                    for dc in range(DC):
                        if j - TAP_AT[dc] in range(1, TAPS - 1):
                            tap(k + 1, dc, j - TAP_AT[dc])
                        if j == SILU_AT[dc]:
                            silu(k + 1, dc)
                    if j in NEXT_GATE_AT:
                        gate_in(k + 1, 0, NEXT_GATE_AT.index(j))
                if k == 0 and j in FIRST_GATE_AT:
                    gate_in(0, 0, FIRST_GATE_AT.index(j))
                if j in GATE_AT:
                    gate_in(k, 1, GATE_AT.index(j))
                if k > 0 and j in GATE_OUT_AT:
                    gate_out(k - 1, 1, GATE_OUT_AT.index(j))
                if j - 2 * NST in GATE_OUT_AT:
                    gate_out(k, 0, GATE_OUT_AT.index(j - 2 * NST))

            nc.vector.memset(u[:, :, 0:TAPS - 1], 0.0).then_inc(zeroed, 1)
            dve.wait_ge(vecs, 16)
            nc.vector.tensor_scalar(cw[:], cw[:], 0.5, None, ALU.mult).then_inc(zeroed, 1)
            nc.vector.tensor_scalar(cb[:], cb[:], 0.5, None, ALU.mult).then_inc(zeroed, 1)
            dve.wait_ge(neg_done, 1)
            dve.wait_ge(zeroed, 3)
            nc.vector.tensor_scalar(neg_a[:], neg_a[:], -1.0, None, ALU.mult).then_inc(neg_done, 1)
            for dc in range(DC):
                add_tap(nc.vector, dve, 0, dc)
                for t in range(1, TAPS - 1):
                    tap(0, dc, t)
                if dc > 0:
                    silu(0, dc - 1)
            silu(0, DC - 1)
            dve.wait_ge(ident_in, 16)
            for d in range(2):
                for dc in range(DC):
                    nc.vector.tensor_scalar(diag[:, d, dc, :], ident[:], dp[:, d, dc], None, ALU.mult).then_inc(diag_done, 1)
            steps(nc.vector, dve, 0, 0)
            for k in range(BLOCKS):
                for i in range(PASSES * NST):
                    p, n = divmod(i, NST)
                    scan(k, p, n)
                    between(k, 2 * i)
                    for q in range(Q):
                        weigh(k, p, n, q)
                    between(k, 2 * i + 1)
            for q in range(Q):
                gate_out(BLOCKS - 1, 1, q)


def mamba_inputs(i):
    g = {k[8:]: np.asarray(v) for k, v in i.items() if k.startswith("L0_attn_")}

    def both(f):
        return np.stack([f(g, "_f"), f(g, "_b")])

    def cols(v):
        return np.ascontiguousarray(np.moveaxis(v.reshape(DC, P, *v.shape[1:]), 0, 1))

    r = {
        "inw": both(lambda g, d: rows(g["inproj" + d])), "xw": both(lambda g, d: rows(g["xproj" + d])),
        "dtw": both(lambda g, d: g["dt_w" + d]), "outw": both(lambda g, d: rows(g["outproj" + d])),
        "vecs": np.ascontiguousarray(np.stack([np.concatenate(
            [cols(v if v.ndim == 2 else v[:, None]) for v in (g[n + d] for n in ("Alog", "conv_w", "conv_b", "dt_b", "Dp"))],
            axis=2) for d in ("_f", "_b")], axis=1)),
    }
    return r


NEXP, SLOTS = 64, 32
NP = NEXP * SLOTS
NCH = NP // CT
MT = SEQ // P
JT = CT // P
XPT = P // SLOTS
FAR = 1.0e30


def mix_phase(nc, a, y_all, x1_rows, x1_stored, kept, gates):
    xt_s, xm_s = kept["xt_s"], kept["xm_s"]
    with ExitStack() as ctx:
        def sb(name, shape):
            return ctx.enter_context(nc.sbuf_tensor("mix_" + name, shape, F32))

        def ps(name, shape):
            return ctx.enter_context(nc.psum_tensor("mix_" + name, shape, F32))

        def sem(name):
            return ctx.enter_context(nc.semaphore("mix_" + name))

        NC, CB = TOKENS // CT, SEQ // CT
        gw, gb, loaded_w = gates.weights, gates.bias, gates.loaded
        pw, prb = sb("pw", [P, KC, DM]), sb("prb", [P, KC])
        rv = sb("rv", [P, KC, BATCH])
        yf, yb, x1 = (sb(n, [P, KC, TOKENS]) for n in ("yf", "yb", "x1"))
        xm_t = yf[:].rearrange("p k (b t) -> p k b t", b=BATCH)
        dif = sb("dif", [P, NC, KC, CT])
        gate, y = (sb(n, [P, 2, KC, CT]) for n in ("gate", "y"))
        mag, share = sb("mag", [P, 2, SEQ]), sb("share", [P, 2, SEQ])
        cum, ones = sb("cum", [P, 2, SEQ]), sb("ones", [P, SEQ])
        below = sb("below", [P, 2, SEQ + 1])
        stat = sb("stat", [P, BATCH * KC, 8])
        turn_sb = sb("turn_sb", [P, 2, CT])
        whole = sb("whole", [P, 2, CT])
        pg = ps("pg", [P, 2, KC, CT])
        pp = ps("pp", [P, KC, CT])
        tr = ps("tr", [P, 2, CT])

        loaded_c = sem("loaded_c")
        loaded_y = [sem(f"loaded_y{c}") for c in range(NC)]
        loaded_x = [sem(f"loaded_x{b}") for b in range(BATCH)]
        gate_mm, gate_done, dif_done, mul_done, y_done = (sem(n) for n in ("gate_mm", "gate_done", "dif_done", "mul_done", "y_done"))
        proj_mm, res_done = sem("proj_mm"), sem("res_done")
        mag_done, sum_inv, exp2_done, xm_done, chain = (sem(n) for n in ("mag_done", "sum_inv", "exp2_done", "xm_done", "chain"))
        turned, turn_high, low_done = (sem(n) for n in ("turned", "turn_high", "low_done"))
        half_done = sem("half_done")
        xt_high, xt_low, phi_high = sem("xt_high"), sem("xt_low"), sem("phi_high")
        turn_read = [sem(f"turn_read{q}") for q in range(2)]

        def backward(t, k, c):
            b, h = divmod(c, CB)
            lo = b * SEQ + (CB - 1 - h) * CT
            return t[:, k, lo:lo + CT][:, ::-1]

        def piece_low(engine, eng, u):
            b, cc = divmod(u, KC)
            eng.wait_ge(xt_high, u + 1)
            engine.tensor_tensor(xt_s[1][:, cc, b, :], xm_t[:, cc, b, :], xt_s[0][:, cc, b, :].bitcast(F32), ALU.subtract
                                 ).then_inc(xt_low, 1)

        def mix(engine, eng, c):
            for k in range(KC):
                eng.wait_ge(gate_done, KC * c + k + 1)
                eng.wait_ge(dif_done, KC * c + k + 1)
                engine.tensor_tensor(dif[:, c, k, :], dif[:, c, k, :], gate[:, c % 2, k, :], ALU.mult
                                        ).then_inc(mul_done, 1)
            for k in range(KC):
                eng.wait_ge(mul_done, KC * c + k + 1)
                if c >= 2:
                    eng.wait_ge(proj_mm, KC * (c - 1))
                engine.tensor_tensor(y[:, c % 2, k, :], dif[:, c, k, :], backward(yb, k, c), ALU.add
                                        ).then_inc(y_done, 1)

        TG = MT // 2

        block = ctx.enter_context(nc.Block())

        @block.sync
        def _(sp):
            for c in range(NC):
                b, h = divmod(c, CB)
                sp.dma_start(yf[:, :, c * CT:(c + 1) * CT], y_all[2 * b][:, :, h * CT:(h + 1) * CT]
                             ).then_inc(loaded_y[c], 16)
                hb = CB - 1 - h
                sp.dma_start(yb[:, :, b * SEQ + hb * CT:b * SEQ + (hb + 1) * CT],
                             y_all[2 * b + 1][:, :, hb * CT:(hb + 1) * CT]).then_inc(loaded_y[c], 16)
                if c == 0:
                    for dst, name in ((pw, "projw"), (prb, "projb"), (rv, "temb_T"), (kept["ident"], "ident")):
                        sp.dma_start(dst[:], a[name]).then_inc(loaded_c, 16)
                if h == 0:
                    sp.dma_start(x1[:, :, b * SEQ:(b + 1) * SEQ], a["xT"][:, :, b * SEQ:(b + 1) * SEQ]
                                 ).then_inc(loaded_x[b], 16)
            sp.dma_start(kept["phi"][:], a["phi"][:, :, 0:CT]).then_inc(kept["loaded_phi"], 16)
            for b in range(BATCH):
                for j in range(TG):
                    sp.wait_ge(turn_read[j % 2], b * TG + j // 2 + 1)
                    sp.dma_start(x1_rows[:, b, 2 * j:2 * j + 2, :], turn_sb[:, j % 2, :].rearrange("p (m d) -> p m d", m=2)
                                 ).then_inc(x1_stored[j % 2], 16)
            for q in range(2):
                sp.wait_ge(x1_stored[q], 16 * BATCH * TG // 2)

        @block.tensor
        def _(pe):
            def gate_sums(c):
                pe.wait_ge(loaded_y[c], 2 * 16)
                if c >= 2:
                    pe.wait_ge(gate_done, KC * (c - 1))
                for cc in range(KC):
                    for k in range(2 * KC):
                        rhs = yf[:, k, c * CT:(c + 1) * CT] if k < KC else backward(yb, k - KC, c)
                        mm = nc.tensor.matmul(pg[:, c % 2, cc, :], gw[:, k, cc * P:(cc + 1) * P], rhs,
                                              start=(k == 0), stop=(k == 2 * KC - 1))
                    mm.then_inc(gate_mm, 1)

            def project(c):
                pe.wait_ge(y_done, KC * (c + 1))
                for cc in range(KC):
                    if c >= 1:
                        pe.wait_ge(res_done, KC * (c - 1) + cc + 1)
                    for k in range(KC):
                        mm = nc.tensor.matmul(pp[:, cc, :], pw[:, k, cc * P:(cc + 1) * P], y[:, c % 2, k, :],
                                              start=(k == 0), stop=(k == KC - 1))
                    mm.then_inc(proj_mm, 1)

            def turn(g):
                b, kind, j = g // (2 * TG), g // TG % 2, g % TG
                if kind == 0:
                    pe.wait_ge(res_done, KC * CB * (b + 1))
                else:
                    pe.wait_ge(xm_done, KC * (b + 1))
                if g >= 2:
                    pe.wait_ge(turn_read[g % 2], g // 2)
                for q in range(4):
                    cc, m = q % 2, 2 * j + q // 2
                    src = x1[:, cc, b * SEQ:(b + 1) * SEQ] if kind == 0 else xm_t[:, cc, b, :]
                    mm = nc.tensor.transpose(tr[:, g % 2, q * P:(q + 1) * P], src[:, m * P:(m + 1) * P], kept["ident"][:])
                mm.then_inc(turned, 1)

            pe.wait_ge(loaded_w, 2 * 16)
            gate_sums(0)
            gate_sums(1)
            pe.wait_ge(loaded_c, 4 * 16)
            project(0)
            project(1)
            gate_sums(2)
            gate_sums(3)
            for g in range(TG):
                turn(g)
            project(2)
            project(3)
            for g in range(TG, 4 * TG):
                turn(g)

        @block.scalar
        def _(act):
            def sigmoids(c):
                for cc in range(KC):
                    act.wait_ge(gate_mm, KC * c + cc + 1)
                    if c >= 2:
                        act.wait_ge(mul_done, KC * (c - 2) + cc + 1)
                    nc.scalar.activation(gate[:, c % 2, cc, :], pg[:, c % 2, cc, :], ACT.Sigmoid, bias=gb[:, cc:cc + 1]
                                         ).then_inc(gate_done, 1)

            def magnitudes(b, cc):
                u = KC * b + cc
                act.wait_ge(res_done, KC * CB * (b + 1) - (KC - 1 - cc))
                wait(act, xm_done, u - 1)
                nc.scalar.activation(mag[:, cc, :], x1[:, cc, b * SEQ:(b + 1) * SEQ], ACT.Abs,
                                     accum_out=stat[:, u, 0:1]).then_inc(mag_done, 1)

            def shares(b, cc):
                u = KC * b + cc
                act.wait_ge(sum_inv, u + 1)
                nc.scalar.activation(share[:, cc, :], mag[:, cc, :], ACT.Exp, scale=stat[:, u, 2:3],
                                     accum_out=stat[:, u, 3:4]).then_inc(exp2_done, 1)

            def turned_out(g):
                b, kind, j = g // (2 * TG), g // TG % 2, g % TG
                act.wait_ge(turned, g + 1)
                if kind == 0:
                    if b or j >= 2:
                        act.wait_ge(x1_stored[j % 2], 16 * (b * TG // 2 + j // 2))
                    nc.scalar.activation(turn_sb[:, j % 2, :], tr[:, g % 2, :], ACT.Copy).then_inc(turn_read[g % 2], 1)
                else:
                    high = nc.scalar.activation(xm_s[0][:, b, 2 * j:2 * j + 2, :],
                                                tr[:, g % 2, :].rearrange("p (m d) -> p m d", m=2), ACT.Copy)
                    if b == 0:
                        wait(act, low_done, j - 1)
                        nc.scalar.activation(whole[:, j % 2, :], tr[:, g % 2, :], ACT.Copy).then_inc(turn_read[g % 2], 1)
                    else:
                        high.then_inc(turn_high, 1)

            def piece_high(u):
                b, cc = divmod(u, KC)
                act.wait_ge(xm_done, u + 1)
                nc.scalar.activation(xt_s[0][:, cc, b, :], xm_t[:, cc, b, :], ACT.Copy).then_inc(xt_high, 1)

            act.wait_ge(loaded_w, 2 * 16)
            sigmoids(0)
            sigmoids(1)
            for cc in range(KC):
                magnitudes(0, cc)
            for cc in range(KC):
                shares(0, cc)
            sigmoids(2)
            sigmoids(3)
            act.wait_ge(kept["loaded_phi"], 16)
            nc.scalar.activation(kept["phi_s"][0][:], kept["phi"][:], ACT.Copy).then_inc(phi_high, 1)
            for g in range(TG):
                turned_out(g)
            for cc in range(KC):
                magnitudes(1, cc)
            for cc in range(KC):
                shares(1, cc)
            for u in range(KC):
                piece_high(u)
            for g in range(TG, 3 * TG):
                turned_out(g)
            piece_high(KC)
            for j in range(TG):
                if j == 2:
                    piece_high(KC + 1)
                turned_out(3 * TG + j)

        @block.gpsimd
        def _(pool):
            nc.gpsimd.memset(ones[:], 1.0).then_inc(chain, 1)
            nc.gpsimd.memset(below[:, :, 0:1], 1.0).then_inc(chain, 1)
            for c in range(NC):
                for k in range(KC):
                    pool.wait_ge(loaded_y[c], 2 * 16)
                    nc.gpsimd.tensor_tensor(dif[:, c, k, :], yf[:, k, c * CT:(c + 1) * CT], backward(yb, k, c),
                                            ALU.subtract).then_inc(dif_done, 1)
            pool.wait_ge(y_done, KC * CB)
            mix(nc.gpsimd, pool, 2)
            mix(nc.gpsimd, pool, 3)
            pool.wait_ge(phi_high, 1)
            nc.gpsimd.tensor_tensor(kept["phi_s"][1][:], kept["phi"][:], kept["phi_s"][0][:].bitcast(F32), ALU.subtract
                                    ).then_inc(kept["phi_split"], 1)
            for j in range(TG):
                g = TG + j
                pool.wait_ge(turn_read[g % 2], g // 2 + 1)
                tile = (slice(None), 0, slice(2 * j, 2 * j + 2), slice(None))
                nc.gpsimd.tensor_tensor(xm_s[1][tile], whole[:, j % 2, :].rearrange("p (m d) -> p m d", m=2),
                                        xm_s[0][tile].bitcast(F32), ALU.subtract).then_inc(low_done, 1)
            for u in range(KC + 1):
                piece_low(nc.gpsimd, pool, u)

        @block.vector
        def _(dve):
            links = [2]

            def link(ins):
                links[0] += 1
                ins.then_inc(chain, 1)
                dve.wait_ge(chain, links[0])

            def residual(c):
                dve.wait_ge(loaded_x[c // CB], 16)
                for cc in range(KC):
                    dve.wait_ge(proj_mm, KC * c + cc + 1)
                    nc.vector.scalar_tensor_tensor(x1[:, cc, c * CT:(c + 1) * CT], pp[:, cc, :], prb[:, cc:cc + 1],
                                                   x1[:, cc, c * CT:(c + 1) * CT], ALU.add, ALU.add).then_inc(res_done, 1)

            def two_over_sum(b, cc):
                u = KC * b + cc
                dve.wait_ge(mag_done, u + 1)
                link(nc.vector.reciprocal(stat[:, u, 1:2], stat[:, u, 0:1]))
                nc.vector.tensor_scalar(stat[:, u, 2:3], stat[:, u, 1:2], 2.0, None, ALU.mult).then_inc(sum_inv, 1)

            def threshold(b, ccs):
                def each(step):
                    for cc in ccs:
                        step(cc, stat[:, KC * b + cc, :]).then_inc(chain, 1)
                        links[0] += 1
                    dve.wait_ge(chain, links[0])

                for cc in ccs:
                    dve.wait_ge(exp2_done, KC * b + cc + 1)
                each(lambda cc, s: nc.vector.reciprocal(s[:, 4:5], s[:, 3:4]))
                each(lambda cc, s: nc.vector.tensor_scalar(share[:, cc, :], share[:, cc, :], s[:, 4:5], None, ALU.mult))
                each(lambda cc, s: nc.vector.tensor_tensor_scan(cum[:, cc, :], ones[:], share[:, cc, :], 0.0,
                                                                ALU.mult, ALU.add))
                each(lambda cc, s: nc.vector.tensor_scalar(below[:, cc, 1:SEQ + 1], cum[:, cc, :], 0.001, rv[:, cc, b:b + 1],
                                                           ALU.add, ALU.is_le))
                each(lambda cc, s: nc.vector.tensor_tensor(cum[:, cc, :], below[:, cc, 0:SEQ], below[:, cc, 1:SEQ + 1],
                                                           ALU.subtract))
                each(lambda cc, s: nc.vector.tensor_tensor_reduce(share[:, cc, :], mag[:, cc, :], cum[:, cc, :], 1.0, 0.0,
                                                                  ALU.mult, ALU.add, s[:, 5:6]))
                each(lambda cc, s: nc.vector.tensor_scalar(s[:, 6:7], below[:, cc, SEQ:SEQ + 1], 3.0e38, s[:, 5:6],
                                                           ALU.mult, ALU.add))
                for cc in ccs:
                    s = stat[:, KC * b + cc, :]
                    nc.vector.scalar_tensor_tensor(xm_t[:, cc, b, :], mag[:, cc, :], s[:, 6:7],
                                                   x1[:, cc, b * SEQ:(b + 1) * SEQ], ALU.is_ge, ALU.mult,
                                                   accum_out=s[:, 7:8]).then_inc(xm_done, 1)

            def half_sum(b):
                for cc in range(KC):
                    dve.wait_ge(xm_done, KC * b + cc + 1)
                    nc.vector.tensor_scalar(kept["half_sum"][:, cc, b:b + 1], stat[:, KC * b + cc, 7:8], 0.5, None, ALU.mult
                                            ).then_inc(half_done, 1)

            dve.wait_ge(loaded_c, 4 * 16)
            dve.wait_ge(chain, 2)
            mix(nc.vector, dve, 0)
            mix(nc.vector, dve, 1)
            residual(0)
            residual(1)
            for cc in range(KC):
                two_over_sum(0, cc)
            threshold(0, range(KC))
            residual(2)
            residual(3)
            for cc in range(KC):
                two_over_sum(1, cc)
            half_sum(0)
            threshold(1, range(KC))
            half_sum(1)
            for j in range(TG):
                g = 3 * TG + j
                if j == 2:
                    piece_low(nc.vector, dve, KC + 1)
                dve.wait_ge(turn_high, j + 1)
                tile = (slice(None), 1, slice(2 * j, 2 * j + 2), slice(None))
                nc.vector.tensor_tensor(xm_s[1][tile], tr[:, g % 2, :].rearrange("p (m d) -> p m d", m=2),
                                        xm_s[0][tile].bitcast(F32), ALU.subtract).then_inc(turn_read[g % 2], 1)


def mix_inputs(i):
    g = {k: np.asarray(v) for k, v in i.items()}
    return {"gatew": rows(g["L0_attn_gate_w"]), "projw": rows(g["L0_attn_proj_w"]),
            "gateb": np.ascontiguousarray(g["L0_attn_gate_b"].reshape(KC, P).T),
            "projb": np.ascontiguousarray(g["L0_attn_proj_b"].reshape(KC, P).T)}


def ffn_phase(nc, a, x1_rows, kept, out):
    xt_s, xm_s, half_sum, phi, phi_s, ident = (kept[n] for n in ("xt_s", "xm_s", "half_sum", "phi", "phi_s", "ident"))
    loaded_phi, phi_split = kept["loaded_phi"], kept["phi_split"]
    with ExitStack() as ctx:
        def sb(name, shape, dtype=F32):
            return ctx.enter_context(nc.sbuf_tensor("ffn_" + name, shape, dtype))

        def ps(name, shape):
            return ctx.enter_context(nc.psum_tensor("ffn_" + name, shape, F32))

        def sem(name):
            return ctx.enter_context(nc.semaphore("ffn_" + name))

        et = sb("et", [P, BATCH, JT, SEQ])
        wt = sb("wt", [P, JT, XPT, KC, DM])
        ebias = sb("ebias", [P, JT, DM])
        lsb = sb("lsb", [P, 2, BATCH, CT])
        tanh = sb("tanh", [P, CT])
        tanh_s = [sb(f"tanh_s{i}", [P, 2, CT], F32R) for i in range(2)]
        ex = sb("ex", [P, 2, BATCH, CT])
        slots = sb("slots", [P, BATCH, KC, CT])
        y = sb("y", [P, JT, BATCH, DM])
        acc = sb("acc", [P, MT, BATCH, DM])
        nmax = sb("nmax", [P, NCH + 1, MT, BATCH])
        lmax = sb("lmax", [P, MT, BATCH])
        drop = sb("drop", [P, NCH, MT, BATCH])
        alpha = sb("alpha", [P, NCH, MT, BATCH])
        part = sb("part", [P, NCH, MT, BATCH])
        den, rden = sb("den", [P, MT, BATCH]), sb("rden", [P, MT, BATCH])
        xres = ex[:, :, :, 0:DM]

        lg = ps("lg", [P, BATCH, CT])
        sl = ps("sl", [P, BATCH, KC, CT])
        tb = ps("tb", [P, CT])
        oy = ps("oy", [P, CT])

        loaded_b, chain = sem("loaded_b"), sem("chain")
        init_done, alpha_done = sem("init_done"), sem("alpha_done")
        l_done, l_copied, nm_ready, diff_done = sem("l_done"), sem("l_copied"), sem("nm_ready"), sem("diff_done")
        tanh_done, split_done, exp_done = sem("tanh_done"), sem("split_done"), sem("exp_done")
        slots_step, sl_act, sl_dve = sem("slots_step"), sem("sl_act"), sem("sl_dve")
        et_turned, et_act, et_dve = sem("et_turned"), sem("et_act"), sem("et_dve")
        y_mm, y_sb = sem("y_mm"), sem("y_sb")
        out_done, acc_done = sem("out_done"), sem("acc_done")
        small, phi_high = sem("small"), sem("phi_high")
        w_loaded = [sem(f"w_loaded{j}") for j in range(JT)]
        res_loaded = [sem(f"res_loaded{j}") for j in range(2)]
        res_done = sem("res_done")
        stored = [sem(f"stored{s}") for s in range(2)]

        block = ctx.enter_context(nc.Block())

        @block.sync
        def _(sp):
            sp.dma_start(ebias[:], a["ebias"][:, 0:JT, :]).then_inc(loaded_b, 16)
            sp.dma_start(phi[:], a["phi"][:, :, CT:2 * CT]).then_inc(loaded_phi, 16)
            for j in range(JT):
                sp.dma_start(wt[:, j], a["ew"][j]).then_inc(w_loaded[j], 16)

            def chunk(c, final=False):
                for j in range(JT):
                    sp.wait_ge(y_mm, JT * (c - 1) + j + 1)
                    sp.dma_start(wt[:, j], a["ew"][bass.ds(c * JT + j, 1)].rearrange("o p n k e -> (o p) n k e")
                                 ).then_inc(w_loaded[j], 16)
                sp.wait_ge(y_sb, JT * c)
                sp.dma_start(ebias[:], a["ebias"][:, bass.ds(c * JT, JT), :]).then_inc(loaded_b, 16)
                if not final:
                    sp.wait_ge(phi_split, c + 1)
                    sp.dma_start(phi[:], a["phi"][:, :, bass.ds((c + 1) * CT, CT)]).then_inc(loaded_phi, 16)

            with sp.Fori(1, NCH - 1) as c:
                chunk(c)
            chunk(NCH - 1, final=True)
            sp.wait_ge(et_turned, 2 * MT * NCH)
            for m in range(MT):
                if m >= 2:
                    sp.wait_ge(stored[m % 2], 16 * (m // 2))
                sp.dma_start(xres[:, m % 2], x1_rows[:, :, m, :]).then_inc(res_loaded[m % 2], 16)
                if m >= 1:
                    sp.wait_ge(res_done, m)
                    sp.dma_start(out[:, (m - 1) * P:m * P, :].rearrange("b p d -> p b d"), xres[:, (m - 1) % 2]
                                 ).then_inc(stored[(m - 1) % 2], 16)
            sp.wait_ge(res_done, MT)
            sp.dma_start(out[:, (MT - 1) * P:MT * P, :].rearrange("b p d -> p b d"), xres[:, (MT - 1) % 2]
                         ).then_inc(stored[(MT - 1) % 2], 16)
            for slot in stored:
                sp.wait_ge(slot, 16 * MT // 2)

        @block.tensor
        def _(pe):
            def logits(c, m):
                if m == 0:
                    pe.wait_ge(phi_split, c + 1)
                wait(pe, l_copied, BATCH * (MT * c + m))
                for b in range(BATCH):
                    for k in range(KC):
                        mm = split_products(nc, lg[:, b, :], [x[:, k, b, m * P:(m + 1) * P] for x in xt_s],
                                            [w[:, k, :] for w in phi_s], k == 0, k == KC - 1)
                    mm.then_inc(l_done, 1)

            def combine(c, m, last=False):
                if m == 0:
                    pe.wait_ge(y_sb, JT * (c + 1))
                elif last:
                    pe.wait_ge(acc_done, MT * c + m - 1)
                else:
                    wait(pe, acc_done, MT * c + m)
                bank = (oy, tb)[m % 2] if last else oy
                for b in range(BATCH):
                    for j in range(JT):
                        mm = nc.tensor.matmul(bank[:, b * DM:(b + 1) * DM], et[:, b, j, m * P:(m + 1) * P], y[:, j, b, :],
                                              start=(j == 0), stop=(j == JT - 1))
                mm.then_inc(out_done, 1)

            def gather(c, m, b):
                pe.wait_ge(split_done, 2 * (MT * c + m) + 2)
                if m == 0 and b == 0:
                    wait(pe, sl_act, KC * c)
                    wait(pe, sl_dve, KC * c)
                for cc in range(KC):
                    mm = split_products(nc, sl[:, b, cc, :], [x[:, b, m, cc * P:(cc + 1) * P] for x in xm_s],
                                        [w[:, m % 2, :] for w in tanh_s], m == 0, m == MT - 1)
                mm.then_inc(slots_step, 1)

            def turn(c, m, b, first):
                pe.wait_ge(exp_done, 2 * (MT * c + m) + b + 1)
                bank = oy if first and b == 1 else tb
                if first:
                    wait(pe, (et_act, et_dve)[b], MT * c + m)
                elif b == 0:
                    wait(pe, et_dve, MT * c + m)
                    if m == 0:
                        wait(pe, y_sb, JT * c)
                else:
                    pe.wait_ge(et_act, MT * c + m + 1)
                for j in range(JT):
                    mm = nc.tensor.transpose(bank[:, j * P:(j + 1) * P], ex[:, m % 2, b, j * P:(j + 1) * P], ident[:])
                mm.then_inc(et_turned, 1)

            def tile_rest(c, m, first):
                for b in range(BATCH):
                    gather(c, m, b)
                    turn(c, m, b, first)

            def experts(c, j, first):
                pe.wait_ge(w_loaded[j], 16 * (c + 1))
                if j == 0:
                    pe.wait_ge(sl_act, KC * (c + 1))
                    pe.wait_ge(sl_dve, KC * (c + 1))
                    wait(pe, acc_done, MT * c)
                    if first:
                        pe.wait_ge(et_dve, MT)
                elif j == 1:
                    pe.wait_ge(et_act if first else et_dve, MT * (c + 1))
                else:
                    pe.wait_ge(y_sb, JT * c + j - 1)
                bank = oy if j % 2 == 0 else tb
                for b in range(BATCH):
                    for k in range(KC):
                        for n in range(XPT):
                            mm = nc.tensor.matmul(bank[n * SLOTS:(n + 1) * SLOTS, b * DM:(b + 1) * DM],
                                                  slots[:, b, k, j * P + n * SLOTS:j * P + (n + 1) * SLOTS],
                                                  wt[:, j, n, k, :], start=(k == 0), stop=(k == KC - 1),
                                                  tile_position=(0, n * SLOTS))
                mm.then_inc(y_mm, 1)

            def chunk(c, first):
                for m in range(MT):
                    logits(c, m)
                    if not first:
                        combine(c - 1, m)
                    if m >= 1:
                        tile_rest(c, m - 1, first)
                tile_rest(c, MT - 1, first)
                for j in range(JT):
                    experts(c, j, first)

            chunk(0, True)
            with pe.Fori(1, NCH) as c:
                chunk(c, False)
            for m in range(MT):
                combine(NCH - 1, m, last=True)

        @block.scalar
        def _(act):
            def turn_out(c, m):
                act.wait_ge(et_turned, 2 * (MT * c + m) + 1)
                wait(act, out_done, MT * (c - 1) + m + 1)
                nc.scalar.activation(et[:, 0, :, m * P:(m + 1) * P], tb[:].rearrange("p (j s) -> p j s", j=JT),
                                     ACT.Copy).then_inc(et_act, 1)

            def chunk(c, final=False):
                for m in range(MT):
                    t = MT * c + m
                    wait(act, diff_done, t - 1)
                    for b in range(BATCH):
                        act.wait_ge(l_done, BATCH * t + b + 1)
                        nc.scalar.activation(lsb[:, m % 2, b, :], lg[:, b, :], ACT.Copy).then_inc(l_copied, 1)
                    act.wait_ge(diff_done, t + 1)
                    nc.scalar.activation(tanh[:], tanh[:], ACT.Tanh, scale=0.5
                                         ).then_inc(tanh_done, 1)
                    if m >= 1:
                        turn_out(c, m - 1)
                    act.wait_ge(nm_ready, t + 1)
                    wait(act, et_turned, 2 * (t - 1))
                    for b in range(BATCH):
                        nc.scalar.activation(ex[:, m % 2, b, :], lsb[:, m % 2, b, :], ACT.Exp,
                                             bias=nmax[:, bass.ds(c + 1, 1), m, b],
                                             accum_out=part[:, bass.ds(c, 1), m, b]).then_inc(exp_done, 1)
                    nc.scalar.activation(alpha[:, bass.ds(c, 1), m, :], drop[:, bass.ds(c, 1), m, :], ACT.Exp
                                         ).then_inc(alpha_done, 1)
                turn_out(c, MT - 1)
                act.wait_ge(slots_step, 2 * MT * (c + 1) - 1)
                wait(act, y_mm, JT * c)
                for cc in range(KC):
                    nc.scalar.activation(slots[:, 0, cc, :], sl[:, 0, cc, :], ACT.Identity, scale=-0.5,
                                         bias=half_sum[:, cc, 0:1]).then_inc(sl_act, 1)
                if not final:
                    act.wait_ge(loaded_phi, 16 * (c + 2))
                    act.wait_ge(l_done, BATCH * MT * (c + 1))
                    nc.scalar.activation(phi_s[0][:], phi[:], ACT.Copy).then_inc(phi_high, 1)

            act.wait_ge(init_done, 1)
            chunk(0)
            with act.Fori(1, NCH - 1) as c:
                chunk(c)
            chunk(NCH - 1, final=True)

        @block.gpsimd
        def _(pool):
            nc.gpsimd.memset(nmax[:, 0], FAR).then_inc(init_done, 1)
            nc.gpsimd.memset(acc[:], 0.0).then_inc(init_done, 1)

        @block.vector
        def _(dve):
            links = [0]

            def link(ins):
                links[0] += 1
                ins.then_inc(chain, 1)
                dve.wait_ge(chain, links[0])

            def turn_out(c, m, first):
                dve.wait_ge(et_turned, 2 * (MT * c + m) + 2)
                wait(dve, out_done, MT * (c - 1) + m + 1)
                bank = oy if first else tb
                nc.vector.tensor_copy(et[:, 1, :, m * P:(m + 1) * P], bank[:].rearrange("p (j s) -> p j s", j=JT)
                                      ).then_inc(et_dve, 1)

            def add_output(c, m, last=False):
                dve.wait_ge(out_done, MT * c + m + 1)
                dve.wait_ge(alpha_done, MT * c + m + 1)
                bank = (oy, tb)[m % 2] if last else oy
                for b in range(BATCH):
                    step = nc.vector.scalar_tensor_tensor(acc[:, m, b, :], acc[:, m, b, :], alpha[:, bass.ds(c, 1), m, b],
                                                          bank[:, b * DM:(b + 1) * DM], ALU.mult, ALU.add)
                step.then_inc(acc_done, 1)

            def chunk(c, first=False, final=False):
                for m in range(MT):
                    t = MT * c + m
                    dve.wait_ge(l_copied, BATCH * (t + 1))
                    nc.vector.tensor_reduce(lmax[:, m, :], lsb[:, m % 2], AX_X, ALU.max, negate=True).then_inc(small, 1)
                    dve.wait_ge(small, 2 * t + 1)
                    nc.vector.tensor_tensor(nmax[:, bass.ds(c + 1, 1), m, :].rearrange("p o b -> p (o b)"),
                                            nmax[:, bass.ds(c, 1), m, :].rearrange("p o b -> p (o b)"), lmax[:, m, :],
                                            ALU.min).then_inc(small, 1)
                    dve.wait_ge(small, 2 * t + 2)
                    nc.vector.tensor_tensor(drop[:, bass.ds(c, 1), m, :], nmax[:, bass.ds(c + 1, 1), m, :],
                                            nmax[:, bass.ds(c, 1), m, :], ALU.subtract).then_inc(nm_ready, 1)
                    wait(dve, split_done, 2 * t)
                    nc.vector.tensor_tensor(tanh[:], lsb[:, m % 2, 1, :], lsb[:, m % 2, 0, :], ALU.subtract
                                            ).then_inc(diff_done, 1)
                    if not first:
                        add_output(c - 1, m)
                    dve.wait_ge(tanh_done, t + 1)
                    wait(dve, slots_step, 2 * (t - 1))
                    nc.vector.tensor_copy(tanh_s[0][:, m % 2, :], tanh[:]).then_inc(split_done, 1)
                    dve.wait_ge(split_done, 2 * t + 1)
                    nc.vector.tensor_tensor(tanh_s[1][:, m % 2, :], tanh[:], tanh_s[0][:, m % 2, :].bitcast(F32),
                                            ALU.subtract).then_inc(split_done, 1)
                    if m >= 1:
                        turn_out(c, m - 1, first)
                dve.wait_ge(slots_step, 2 * MT * (c + 1))
                wait(dve, y_mm, JT * c)
                for cc in range(KC):
                    nc.vector.tensor_scalar(slots[:, 1, cc, :], sl[:, 1, cc, :], 0.5, half_sum[:, cc, 1:2], ALU.mult, ALU.add
                                            ).then_inc(sl_dve, 1)
                turn_out(c, MT - 1, first)
                if not final:
                    dve.wait_ge(phi_high, c + 1)
                    nc.vector.tensor_tensor(phi_s[1][:], phi[:], phi_s[0][:].bitcast(F32), ALU.subtract
                                            ).then_inc(phi_split, 1)
                if first:
                    dve.wait_ge(init_done, 2)
                dve.wait_ge(loaded_b, 16 * (c + 1))
                for j in range(JT):
                    dve.wait_ge(y_mm, JT * c + j + 1)
                    bank = oy if j % 2 == 0 else tb
                    nc.vector.tensor_tensor(y[:, j], bank[:].rearrange("p (b e) -> p b e", b=BATCH),
                                            ebias[:, j:j + 1, :].to_broadcast([P, BATCH, DM]), ALU.add
                                            ).then_inc(y_sb, 1)

            dve.wait_ge(init_done, 1)
            chunk(0, first=True)
            with dve.Fori(1, NCH - 1) as c:
                chunk(c)
            chunk(NCH - 1, final=True)
            dve.wait_ge(alpha_done, MT * NCH)
            dve.wait_ge(exp_done, 2 * MT * NCH)
            link(nc.vector.tensor_copy(den[:], part[:, 0]))
            for c in range(1, NCH):
                link(nc.vector.tensor_tensor(den[:], den[:], alpha[:, c], ALU.mult))
                link(nc.vector.tensor_tensor(den[:], den[:], part[:, c], ALU.add))
            link(nc.vector.reciprocal(rden[:], den[:]))
            for m in range(MT):
                add_output(NCH - 1, m, last=True)
                dve.wait_ge(acc_done, MT * (NCH - 1) + m + 1)
                dve.wait_ge(res_loaded[m % 2], 16 * (m // 2 + 1))
                for b in range(BATCH):
                    last = nc.vector.scalar_tensor_tensor(xres[:, m % 2, b, :], acc[:, m, b, :], rden[:, m, b:b + 1],
                                                          xres[:, m % 2, b, :], ALU.mult, ALU.add)
                last.then_inc(res_done, 1)


def ffn_inputs(i):
    g = {k: np.asarray(v) for k, v in i.items()}
    w = g["L0_ffn_W"].reshape(NP // P, XPT, KC, P, DM).transpose(0, 3, 1, 2, 4)
    b = g["L0_ffn_b"].reshape(NP // P, XPT, 1, DM)
    return {
        "phi": rows(g["L0_ffn_phi"].reshape(DM, NP)), "ew": np.ascontiguousarray(w),
        "ebias": np.broadcast_to(b, (NP // P, XPT, SLOTS, DM)).reshape(NP // P, P, DM).transpose(1, 0, 2),
    }


CONST = {
    "ident": np.eye(P, dtype=np.float32),
    "tri": np.broadcast_to(np.tril(np.ones((EXPERTS, EXPERTS), np.float32), -1)[None], (P, EXPERTS, EXPERTS)),
}


def rows(w, k=P):
    w = np.asarray(w)
    return np.ascontiguousarray(w.reshape(w.shape[0] // k, k, -1).transpose(1, 0, 2))


def moe_inputs(i):
    g = {k: np.asarray(v) for k, v in i.items()}
    return {
        "xT": rows(g["x"].reshape(TOKENS, DM).T), "temb_T": rows(g["cond_1024"].T),
        "router_T": rows(g["L0_cond_router_w"].T), "router_t_T": rows(g["L0_cond_router_t_w"].T),
        "router_bias": g["L0_cond_router_bias"],
        "sw1T": rows(g["L0_cond_sw1"].T), "sw3T": rows(g["L0_cond_sw3"].T), "sw2T": rows(g["L0_cond_sw2"].T),
        "rw1T": rows(g["L0_cond_rw1"].transpose(2, 0, 1).reshape(DM, -1)),
        "rw2T": np.ascontiguousarray(g["L0_cond_rw2"].transpose(2, 0, 1)),
    }


def mix_and_ffn(nc, a, y_all, x1_rows, out, gates):
    with ExitStack() as ctx:
        kept = {name: ctx.enter_context(nc.sbuf_tensor(name, shape, F32)) for name, shape in (
            ("ident", [P, P]),
            ("phi", [P, KC, CT]),
            ("half_sum", [P, KC, BATCH]),
        )}
        for name, shape in (("xt_s", [P, KC, BATCH, SEQ]), ("xm_s", [P, BATCH, MT, DM]), ("phi_s", [P, KC, CT])):
            kept[name] = [ctx.enter_context(nc.sbuf_tensor(f"{name}{i}", shape, F32R)) for i in range(2)]
        for name in ("loaded_phi", "phi_split"):
            kept[name] = ctx.enter_context(nc.semaphore(name))
        x1_stored = [ctx.enter_context(nc.semaphore(f"x1_stored{q}")) for q in range(2)]
        mix_phase(nc, a, y_all, x1_rows, x1_stored, kept, gates)
        ffn_phase(nc, a, x1_rows, kept, out)


def build(nc, a, out):
    cond = nc.dram_tensor("cond", [GROUPS, P, KC, SEQ], F32).ap()
    bc_rows = nc.dram_tensor("bc_rows", [GROUPS * HALVES, 2 * NST, CT], F32).ap()
    y_all = nc.dram_tensor("y_all", [GROUPS, P, KC, SEQ], F32).ap()
    x1_rows = nc.dram_tensor("x1_rows", [P, BATCH, MT, DM], F32).ap()
    with ExitStack() as outer:
        gates = GateLoads(nc, outer)
        with ExitStack() as ctx:
            ahead = FirstLoads(nc, ctx)
            moe_phase(nc, a, cond, ahead)
            mamba_phase(nc, a, cond, bc_rows, y_all, ahead, gates)
        mix_and_ffn(nc, a, y_all, x1_rows, out, gates)


def kernel(**inputs):
    from concourse import bacc
    from concourse.bass_utils import run_bass_kernel_spmd

    arrays = {**moe_inputs(inputs), **mamba_inputs(inputs), **mix_inputs(inputs), **ffn_inputs(inputs), **CONST}
    arrays = {f"in_{k}": np.ascontiguousarray(v) for k, v in arrays.items()}
    nc = bacc.Bacc("TRN2", target_bir_lowering=False, num_devices=1)
    a = {k[3:]: nc.dram_tensor(k, v.shape, F32, kind="ExternalInput").ap() for k, v in arrays.items()}
    out = nc.dram_tensor("out", [BATCH, SEQ, DM], F32, kind="ExternalOutput").ap()
    build(nc, a, out)
    r = run_bass_kernel_spmd(nc, [arrays], core_ids=[0])
    return r.results[0]["out"]
```
